# Optimizing a Trainium2 kernel written in Bass

```python
import numpy as np
import jax
import jax.numpy as jnp

def _softmax(x, axis=-1):
    return jax.nn.softmax(x, axis=axis)

def _gelu(x):
    return jax.nn.gelu(x, approximate=True)

def _silu(x):
    return jax.nn.silu(x)

def _sigmoid(x):
    return jax.nn.sigmoid(x)

def _layernorm(x, axis=-1, eps=1e-05):
    m = jnp.mean(x, axis=axis, keepdims=True)
    v = jnp.var(x, axis=axis, keepdims=True)
    return (x - m) / jnp.sqrt(v + eps)

def _scatter_add(tgt, idx, src, axis=0):
    return tgt.at[idx].add(src)

def _segment_sum(src, seg, n):
    return jax.ops.segment_sum(src, seg, n)
kernel_name = 'mk_seq_preln_d1_jaxref_r8_806984'

def setup_inputs(seed: int=0):
    np.random.seed(seed)
    _w = jnp.asarray

    def _L0_attn_setup():
        import jax, jax.numpy as jnp
        import numpy as np
        NUM_HEADS = 16
        LN_EPS = 1e-05
        NORM_EPS = 1e-12

        def _l2norm(t):
            return t / jnp.maximum(jnp.linalg.norm(t, axis=-1, keepdims=True), NORM_EPS)

        def _forward(x, Wq, Wk, Wv, Wf1, Wf2, Wg, Wo1, Wo2, ln_w, Wout):
            B, N, D = x.shape
            H = NUM_HEADS
            HD = D // H
            q = jax.nn.silu(x @ Wq)
            k = jax.nn.silu(x @ Wk)
            v = jax.nn.silu(x @ Wv)
            log_f = jax.nn.log_sigmoid(x @ Wf1 @ Wf2)
            gamma = -jax.nn.sigmoid(x @ Wg)
            q = q.reshape(B, N, H, HD)
            k = k.reshape(B, N, H, HD)
            v = v.reshape(B, N, H, HD)
            log_f = log_f.reshape(B, N, H, HD)
            k = _l2norm(k)
            a = k * gamma[..., None]

            def step(S, inp):
                qt, kt, vt, at, gft = inp
                bs1 = jnp.einsum('bhk,bhkv->bhv', kt, S)
                S1 = S + at[..., :, None] * bs1[..., None, :]
                S2 = jnp.exp(gft)[..., None] * S1
                bs2 = jnp.einsum('bhk,bhkv->bhv', kt, S2)
                S3 = S2 + at[..., :, None] * bs2[..., None, :] + kt[..., :, None] * vt[..., None, :]
                o = jnp.einsum('bhk,bhkv->bhv', qt, S3)
                return (S3, o)
            to_time = lambda t: jnp.moveaxis(t, 1, 0)
            S0 = jnp.zeros((B, H, HD, HD), dtype=x.dtype)
            _, o = jax.lax.scan(step, S0, (to_time(q), to_time(k), to_time(v), to_time(a), to_time(log_f)))
            o = jnp.moveaxis(o, 0, 1)
            z = jnp.zeros_like(o)
            out3 = jnp.stack([z, z, o], axis=2).reshape(B, 3 * N, H, HD)
            out = out3[:, -N:]
            out = out.reshape(B, N, D)
            gate = jax.nn.sigmoid(x @ Wo1 @ Wo2)
            out = out * gate
            mu = jnp.mean(out, axis=-1, keepdims=True)
            var = jnp.mean((out - mu) ** 2, axis=-1, keepdims=True)
            out = (out - mu) * jax.lax.rsqrt(var + LN_EPS) * ln_w
            return out @ Wout
        key = jax.random.key(seed)
        ks = jax.random.split(key, 12)
        B, N, D = (2, 128, 128)
        HD = D // NUM_HEADS
        s = 0.02
        inp = {'x': jax.random.normal(ks[0], (B, N, D), dtype=jnp.float32), 'Wq': jax.random.normal(ks[1], (D, D), dtype=jnp.float32) * s, 'Wk': jax.random.normal(ks[2], (D, D), dtype=jnp.float32) * s, 'Wv': jax.random.normal(ks[3], (D, D), dtype=jnp.float32) * s, 'Wf1': jax.random.normal(ks[4], (D, HD), dtype=jnp.float32) * s, 'Wf2': jax.random.normal(ks[5], (HD, D), dtype=jnp.float32) * s, 'Wg': jax.random.normal(ks[6], (D, NUM_HEADS), dtype=jnp.float32) * s, 'Wo1': jax.random.normal(ks[7], (D, HD), dtype=jnp.float32) * s, 'Wo2': jax.random.normal(ks[8], (HD, D), dtype=jnp.float32) * s, 'ln_w': jnp.ones((D,), dtype=jnp.float32), 'Wout': jax.random.normal(ks[9], (D, D), dtype=jnp.float32) * s}
        return inp
    _L0_attn_in = _L0_attn_setup()

    def _L0_ffn_setup():
        import jax, jax.numpy as jnp
        import numpy as np
        E = 16
        H = 128
        F = 256
        TOP_K = 1
        B, S = (2, 128)
        key = jax.random.key(seed)
        ks = jax.random.split(key, 7)
        s = 0.02
        return {'hidden_states': jax.random.normal(ks[0], (B, S, H), jnp.float32), 'w_router': jax.random.normal(ks[1], (E, H), jnp.float32) * s, 'gate_up_proj': jax.random.normal(ks[2], (E, H, 2 * F), jnp.float32) * s, 'down_proj': jax.random.normal(ks[3], (E, F, H), jnp.float32) * s, 'w_gate': jax.random.normal(ks[4], (F, H), jnp.float32) * s, 'w_up': jax.random.normal(ks[5], (F, H), jnp.float32) * s, 'w_down': jax.random.normal(ks[6], (H, F), jnp.float32) * s}
    _L0_ffn_in = _L0_ffn_setup()
    _d = {'L0_attn_x': _L0_attn_in['x'], 'L0_attn_Wq': _L0_attn_in['Wq'], 'L0_attn_Wk': _L0_attn_in['Wk'], 'L0_attn_Wv': _L0_attn_in['Wv'], 'L0_attn_Wf1': _L0_attn_in['Wf1'], 'L0_attn_Wf2': _L0_attn_in['Wf2'], 'L0_attn_Wg': _L0_attn_in['Wg'], 'L0_attn_Wo1': _L0_attn_in['Wo1'], 'L0_attn_Wo2': _L0_attn_in['Wo2'], 'L0_attn_ln_w': _L0_attn_in['ln_w'], 'L0_attn_Wout': _L0_attn_in['Wout'], 'L0_ffn_w_router': _L0_ffn_in['w_router'], 'L0_ffn_gate_up_proj': _L0_ffn_in['gate_up_proj'], 'L0_ffn_down_proj': _L0_ffn_in['down_proj'], 'L0_ffn_w_gate': _L0_ffn_in['w_gate'], 'L0_ffn_w_up': _L0_ffn_in['w_up'], 'L0_ffn_w_down': _L0_ffn_in['w_down']}
    _x0 = _d['L0_attn_x']
    _d['L0_attn_x'] = jax.random.normal(jax.random.fold_in(jax.random.key(seed), 1), (4, 1024, 128), dtype=_x0.dtype)
    del _x0
    return _d

def reference(L0_attn_x, L0_attn_Wq, L0_attn_Wk, L0_attn_Wv, L0_attn_Wf1, L0_attn_Wf2, L0_attn_Wg, L0_attn_Wo1, L0_attn_Wo2, L0_attn_ln_w, L0_attn_Wout, L0_ffn_w_router, L0_ffn_gate_up_proj, L0_ffn_down_proj, L0_ffn_w_gate, L0_ffn_w_up, L0_ffn_w_down):

    def _L0_attn_ref(x, Wq, Wk, Wv, Wf1, Wf2, Wg, Wo1, Wo2, ln_w, Wout):
        import jax, jax.numpy as jnp
        import numpy as np
        NUM_HEADS = 16
        LN_EPS = 1e-05
        NORM_EPS = 1e-12

        def _l2norm(t):
            return t / jnp.maximum(jnp.linalg.norm(t, axis=-1, keepdims=True), NORM_EPS)

        def _forward(x, Wq, Wk, Wv, Wf1, Wf2, Wg, Wo1, Wo2, ln_w, Wout):
            B, N, D = x.shape
            H = NUM_HEADS
            HD = D // H
            q = jax.nn.silu(x @ Wq)
            k = jax.nn.silu(x @ Wk)
            v = jax.nn.silu(x @ Wv)
            log_f = jax.nn.log_sigmoid(x @ Wf1 @ Wf2)
            gamma = -jax.nn.sigmoid(x @ Wg)
            q = q.reshape(B, N, H, HD)
            k = k.reshape(B, N, H, HD)
            v = v.reshape(B, N, H, HD)
            log_f = log_f.reshape(B, N, H, HD)
            k = _l2norm(k)
            a = k * gamma[..., None]

            def step(S, inp):
                qt, kt, vt, at, gft = inp
                bs1 = jnp.einsum('bhk,bhkv->bhv', kt, S)
                S1 = S + at[..., :, None] * bs1[..., None, :]
                S2 = jnp.exp(gft)[..., None] * S1
                bs2 = jnp.einsum('bhk,bhkv->bhv', kt, S2)
                S3 = S2 + at[..., :, None] * bs2[..., None, :] + kt[..., :, None] * vt[..., None, :]
                o = jnp.einsum('bhk,bhkv->bhv', qt, S3)
                return (S3, o)
            to_time = lambda t: jnp.moveaxis(t, 1, 0)
            S0 = jnp.zeros((B, H, HD, HD), dtype=x.dtype)
            _, o = jax.lax.scan(step, S0, (to_time(q), to_time(k), to_time(v), to_time(a), to_time(log_f)))
            o = jnp.moveaxis(o, 0, 1)
            z = jnp.zeros_like(o)
            out3 = jnp.stack([z, z, o], axis=2).reshape(B, 3 * N, H, HD)
            out = out3[:, -N:]
            out = out.reshape(B, N, D)
            gate = jax.nn.sigmoid(x @ Wo1 @ Wo2)
            out = out * gate
            mu = jnp.mean(out, axis=-1, keepdims=True)
            var = jnp.mean((out - mu) ** 2, axis=-1, keepdims=True)
            out = (out - mu) * jax.lax.rsqrt(var + LN_EPS) * ln_w
            return out @ Wout
        return _forward(x, Wq, Wk, Wv, Wf1, Wf2, Wg, Wo1, Wo2, ln_w, Wout)

    def _L0_ffn_ref(hidden_states, w_router, gate_up_proj, down_proj, w_gate, w_up, w_down):
        import jax, jax.numpy as jnp
        import numpy as np
        E = 16
        H = 128
        F = 256
        TOP_K = 1
        B, S = (2, 128)
        b, s, h = hidden_states.shape
        x = hidden_states.reshape(-1, h)
        logits = x @ w_router.T
        _, top_idx = jax.lax.top_k(logits, TOP_K)
        mask = jax.nn.one_hot(top_idx, E, dtype=logits.dtype).sum(axis=1)
        scores = jax.nn.sigmoid(logits) * mask
        masked_inputs = scores.T[:, :, None] * x[None, :, :]
        gate_up = jnp.einsum('eth,ehf->etf', masked_inputs, gate_up_proj)
        gate, up = jnp.split(gate_up, 2, axis=-1)
        expert_out = jnp.einsum('etf,efh->eth', up * jax.nn.silu(gate), down_proj)
        shared = jax.nn.silu(x @ w_gate.T) * (x @ w_up.T) @ w_down.T
        out = shared + expert_out.sum(axis=0)
        return out.reshape(b, s, h)
    x = L0_attn_x
    x = x + _L0_attn_ref(_layernorm(x, axis=-1), L0_attn_Wq, L0_attn_Wk, L0_attn_Wv, L0_attn_Wf1, L0_attn_Wf2, L0_attn_Wg, L0_attn_Wo1, L0_attn_Wo2, L0_attn_ln_w, L0_attn_Wout)
    x = x + _L0_ffn_ref(_layernorm(x, axis=-1), L0_ffn_w_router, L0_ffn_gate_up_proj, L0_ffn_down_proj, L0_ffn_w_gate, L0_ffn_w_up, L0_ffn_w_down)
    return x

_drawn_inputs = setup_inputs


def setup_inputs(seed=0):
    import zlib

    import numpy as np

    out = dict(_drawn_inputs(seed))
    spreads = {'L0_attn_ln_w': (1.0, 0.6)}
    factors = {'L0_attn_Wf1': 8.0,
     'L0_attn_Wf2': 8.0,
     'L0_attn_Wg': 8.0,
     'L0_attn_Wo1': 8.0,
     'L0_attn_Wo2': 8.0,
     'L0_ffn_w_router': 8.0,
     'L0_ffn_gate_up_proj': 8.0,
     'L0_ffn_down_proj': 8.0,
     'L0_ffn_w_gate': 6.903,
     'L0_ffn_w_up': 6.851,
     'L0_ffn_w_down': 6.829}
    for name, (base, spread) in spreads.items():
        noise = np.random.default_rng([zlib.crc32(name.encode()), seed]).standard_normal(out[name].shape)
        drawn = base * np.exp(spread * noise) if base else spread * noise
        out[name] = jnp.asarray(drawn.astype(out[name].dtype))
    for name, factor in factors.items():
        out[name] = (out[name] * factor).astype(out[name].dtype)
    return out
```

```python
import numpy as np

import concourse.bass as bass
from concourse import mybir
from contextlib import ExitStack

F32 = mybir.dt.float32
I32 = mybir.dt.int32
U32 = mybir.dt.uint32
ALU = mybir.AluOpType
ACT = mybir.ActivationFunctionType
AX = mybir.AxisListType

B, N, D = 4, 1024, 128
H = 16
HD = D // H
C = 32
P = 128
NOUT = (N + 2) // 3
L2 = -(-NOUT // C)
L1 = (N - C * L2) // C
T1 = C * L1
SKIP = (N - NOUT) - T1
NT = L1 + L2
ROWS = 3 * L2
LN_EPS = 1e-5
NORM_EPS = 1e-12
E, F = 16, 256
COLS = P * HD
HALF = COLS // 2
assert T1 + C * L2 == N and SKIP >= 0


U = 2


class Tokens:

    def __init__(self, name, rows, valid):
        self.name, self.rows = name, rows
        self.n = len(rows)
        self.need = (valid - E) // P + E
        self.tiles = -(-self.need // U) * U
        self.groups = [(4 * g, min(4 * g + 4, self.n)) for g in range(-(-self.n // 4))]


OTHERS = Tokens("others", [j for j in range(ROWS) if j % 3], 2 * B * (N // 3))
MIXED = Tokens("mixed", [j for j in range(ROWS) if j % 3 == 0], B * NOUT)


def row_valid():
    tok = 3 * L2 * (np.arange(P)[:, None] % C) - 3 * SKIP + np.arange(ROWS)[None, :]
    return (tok >= 0) & (tok < N)


def constants():
    p = np.arange(P)
    parts = {}
    parts["ident"] = np.eye(P)
    parts["block"] = (p[:, None] // HD == p[None, :] // HD)
    parts["heads"] = (p[:, None] // HD == np.arange(H)[None, :])
    parts["diag8"] = (p[:, None] % HD == np.arange(HD)[None, :])
    parts["sel"] = np.concatenate([parts["block"] & (p[None, :] % HD == v) for v in range(HD)], 1)
    parts["before"] = (p[:, None] < p[None, :])
    parts["ones"] = np.ones((P, P))
    parts["mean"] = np.full((P, P), 1.0 / D)
    valid = row_valid()
    for t in (OTHERS, MIXED):
        v = valid[:, t.rows]
        parts["valid_" + t.name] = v
        spare = np.where(v, 0, t.tiles * P + np.cumsum(~v.ravel()).reshape(v.shape) - 1)
        parts["spare_" + t.name] = spare
        assert (~v).sum() <= P
    parts["prefer"] = np.tile(E - np.arange(E)[None, :], (P, 1))
    parts["steps128"] = np.tile(P * np.arange(OTHERS.n)[None, :], (P, 1))
    parts["tileno"] = np.tile(np.arange(OTHERS.tiles)[None, :], (P, 1))
    at, n = {}, 0
    for k, a in parts.items():
        at[k] = (n, n + a.shape[1])
        n += a.shape[1]
    return np.concatenate([np.asarray(a, np.float32) for a in parts.values()], 1), at


CONST, AT = constants()



Y, K, PP, FF, VV = range(5)
GROUPS = [(4 * g, min(4 * g + 4, NT)) for g in range(-(-NT // 4))]
QGROUPS = [(4 * g, min(4 * g + 4, L2)) for g in range(-(-L2 // 4))]
NG, NQ = len(GROUPS), len(QGROUPS)


def spread(ap, *shape):
    return ap.to_broadcast([P, *shape])


def build(nc, a, out, xs, ys, scr, debug=None):
    ctx = ExitStack()
    with ctx:
        def sb(name, shape, dt=F32):
            return ctx.enter_context(nc.sbuf_tensor(name, shape, dt))

        def sem(name):
            return ctx.enter_context(nc.semaphore(name))

        V, S, G, T = nc.vector, nc.scalar, nc.gpsimd, nc.tensor

        cst = sb("cst", [P, CONST.shape[1]])
        c = {k: cst[:, lo:hi] for k, (lo, hi) in AT.items()}
        zeros = sb("zeros", [P, HALF])
        eps = sb("eps", [P, 1])
        early = sb("early", [P, L2 * COLS])
        xr = early[:, 0:NT * D].rearrange("p (s d) -> p s d", s=NT)
        xnT = early[:, NT * D:2 * NT * D]
        xa = early[:, 2 * NT * D:2 * NT * D + L2 * D].rearrange("p (s d) -> p s d", s=L2)
        xaT = early[:, 2 * NT * D + L2 * D:2 * NT * D + 2 * L2 * D]
        nm, nb = C * HD * HD, C * HD * 4
        ch_m = [early[:, r * nm:(r + 1) * nm].rearrange("p (j c i) -> p j c i", j=HD, c=C) for r in (0, 1)]
        ch_b = [early[:, 2 * nm + r * nb:2 * nm + (r + 1) * nb].rearrange("p (v c i) -> p v c i", v=4, c=C)
                for r in (0, 1)]
        at = 2 * nm + 2 * nb
        ch_s = early[:, at:at + HD * (C + 1) * 4].rearrange("p (i c v) -> p i c v", i=HD, c=C + 1)
        at += HD * (C + 1) * 4
        ch_pr = early[:, at:at + 4 * HD * HD].rearrange("p (v i j) -> p v i j", v=4, i=HD)
        at += 4 * HD * HD
        ch_sum = early[:, at:at + 4 * HD].rearrange("p (v i) -> p v i", v=4)
        qs = early[:, :].rearrange("p (s h x v) -> p s h x v", s=L2, h=2, v=4)
        xf = sb("xf", [P, ROWS, D])
        steps = sb("steps", [P, NT, 5, P])
        qT = sb("qT", [P, L2 * P])
        gateT = sb("gateT", [P, L2 * P])
        wqkv = sb("wqkv", [P, 3, D])
        wgs = sb("wgs", [P, H])
        wge = sb("wge", [P, D])
        wlow = sb("wlow", [P, 2, HD])
        wlowT = sb("wlowT", [HD, 2, P])
        wup = sb("wup", [HD, 2, D])
        wfo = sb("wfo", [P, 2, D])
        wout = sb("wout", [P, D])
        lnw = sb("lnw", [P, 1])
        state = sb("state", [P, 2, HALF])
        work = sb("work", [P, 2, 2, HALF])
        decayed = sb("decayed", [P, 2, HALF])
        uv = sb("uv", [P, 2, 2, HALF])
        ucopy, vterm = uv[:, 0], uv[:, 1]
        stats = sb("stats", [P, NT, 6])
        mv = sb("mv", [P, NT + L2, 2])
        rstd = sb("rstd", [P, NT + L2])
        rk = sb("rk", [P, NT * H])
        og = work[:].rearrange("p a b c -> p (a b c)")[:, 0:L2 * P]
        od = uv[:].rearrange("p a b c -> p (a b c)")[:, 0:L2 * P]
        osq = early[:, 0:L2 * P]
        rstd2 = sb("rstd2", [P, L2])

        ps = [ctx.enter_context(nc.psum_tensor(f"ps{i}", [P, 2, HALF], F32)) for i in range(4)]
        bank = [ps[i // 2][:, i % 2, :] for i in range(8)]

        s_cst, s_x, s_xf, s_wa = sem("s_const"), sem("s_x"), sem("s_xf"), sem("s_attn_weights")
        s_zero, s_xfz = sem("s_zeros"), sem("s_xf_zeroed")
        s_st, s_mv, s_sd, s_rs, s_xn = sem("s_stats"), sem("s_mv"), sem("s_std"), sem("s_rstd"), sem("s_xn")
        s_tp, s_xT = sem("s_transposed"), sem("s_xT")
        s_wt, s_wtc, s_wp, s_w = sem("s_wlow_transposed"), sem("s_wlowT"), sem("s_wproduct"), sem("s_wfo")
        s_wge = sem("s_wge")
        s_pj, s_ev, s_sq = sem("s_projected"), sem("s_evicted"), sem("s_ksq")
        s_ss, s_no, s_nm, s_rk, s_rb = sem("s_ss"), sem("s_norm"), sem("s_normmax"), sem("s_rk"), sem("s_rb")
        s_rke = sem("s_rk_spread")
        s_k, s_fk, s_fkk, s_gk = sem("s_k"), sem("s_fk"), sem("s_fkk"), sem("s_gk")
        s_c, s_gc, s_y, s_m, s_p = sem("s_c"), sem("s_gc"), sem("s_y"), sem("s_m"), sem("s_p")
        two = lambda n: [sem(f"{n}{h}") for h in (0, 1)]
        s_state, s_prod, s_red, s_term = two("s_state"), two("s_prod"), two("s_red"), two("s_term")
        s_add, s_dec, s_uc, s_bp, s_ba = two("s_add"), two("s_dec"), two("s_uc"), two("s_bp"), two("s_ba")
        s_open, s_bs, s_bc = sem("s_open"), sem("s_bsum"), sem("s_bcopy")
        s_min, s_bin = sem("s_matrices_in"), sem("s_sums_in")
        s_mout, s_bout, s_sout = sem("s_m_out"), sem("s_b_out"), sem("s_s_out")
        s_cm, s_cr, s_ca = sem("s_chain_mul"), sem("s_chain_red"), sem("s_chain_add")
        s_chout = sem("s_chain_out")
        s_vd, s_q = two("s_vd"), two("s_q")
        s_o, s_og, s_mu, s_od, s_osq, s_dw = (sem("s_o"), sem("s_og"), sem("s_mu"), sem("s_od"), sem("s_osq"),
                                              sem("s_dw"))
        s_var, s_sd2, s_rs2, s_at, s_x1 = sem("s_var"), sem("s_std2"), sem("s_rstd2"), sem("s_at"), sem("s_x1")
        s_dbg = sem("s_dbg")
        gu = steps[:].rearrange("p a b c -> p (a b c)")[:, 0:E * 2 * F]
        dw = steps[:].rearrange("p a b c -> p (a b c)")[:, E * 2 * F:E * 3 * F]
        wnat = sb("wnat", [P, 7, D])
        wT = sb("wT", [P, 6, P])
        wrT = sb("wrT", [P, E])
        tail = steps[:].rearrange("p a b c -> p (a b c)")[:, L1 * 5 * P:]
        at = 0
        fb = {}
        for t in (OTHERS, MIXED):
            q = {}
            fb[t.name] = q

            def take(name, n, dt=F32):
                nonlocal at
                q[name] = early[:, at:at + n] if dt == F32 else early[:, at:at + n].bitcast(dt)
                at += n

            take("nat", t.n * D)
            take("lg", t.n * E)
            take("oh", t.n * E)
            take("score", t.n)
            take("mx", t.n)
            take("mw", t.n)
            take("slot", t.n)
            take("idx", t.n, I32)
            q["stats"] = sb("stats_" + t.name, [P, t.n, 6])
            q["mv"] = sb("mv_" + t.name, [P, t.n, 2])
            q["rstd"] = sb("rstd_" + t.name, [P, t.n])
            q["te"] = sb("te_" + t.name, [1, t.tiles], I32)
        n = OTHERS.n * E
        r_tot, r_inc, r_a, r_keep = (early[:, at + i * n:at + (i + 1) * n] for i in range(4))
        at += 4 * n
        r_nt, r_ti, r_ts, r_one = (early[:, at + i * E:at + (i + 1) * E] for i in range(4))
        at += 4 * E
        r_te = early[:, at:at + OTHERS.tiles * E]
        at += OTHERS.tiles * E
        r_tf = early[:, at:at + OTHERS.tiles]
        at += OTHERS.tiles
        assert at <= L2 * COLS, at
        tat = 0

        def tail_take(n):
            nonlocal tat
            tat += n
            assert tat <= L2 * 5 * P
            return tail[:, tat - n:tat]

        fxT = tail_take(4 * P)
        fsg = tail_take(4 * P)
        fhT = tail_take(8 * P).rearrange("p (k x) -> p k x", k=2)
        e_in = tail_take(U * P).rearrange("p (u d) -> p u d", u=U)
        e_xT = tail_take(U * P).rearrange("p (u d) -> p u d", u=U)
        e_sg = tail_take(U * F).rearrange("p (u d) -> p u d", u=U)
        e_h = tail_take(U * F).rearrange("p (u d) -> p u d", u=U)
        e_hT = tail_take(U * F).rearrange("p (u d) -> p u d", u=U)
        e_y = tail_take(U * P).rearrange("p (u d) -> p u d", u=U)
        s_wf, s_wft, s_wfT = sem("s_ffn_weights"), sem("s_ffn_w_transposed"), sem("s_ffn_wT")
        s_we = sem("s_expert_weights")
        s_xz = sem("s_slots_zeroed")
        s_fst, s_fmv, s_fsd, s_frs, s_fn = (sem("s_f_stats"), sem("s_f_mv"), sem("s_f_std"), sem("s_f_rstd"),
                                            sem("s_f_normed"))
        s_ft, s_fx, s_fl, s_flc, s_fgu = (sem("s_f_transposed"), sem("s_f_xT"), sem("s_f_logits"), sem("s_f_lg"),
                                          sem("s_f_gate_up"))
        s_fsg, s_fh, s_fy, s_fa = sem("s_f_silu"), sem("s_f_h"), sem("s_f_y"), sem("s_f_added")
        s_link = sem("s_route_link")
        s_oh, s_rank, s_mx, s_score = sem("s_onehot"), sem("s_rank"), sem("s_max"), sem("s_score")
        s_idx, s_te, s_sc, s_scat = sem("s_slots"), sem("s_tile_experts"), sem("s_scaled"), {t: sem("s_scattered_" + t) for t in fb}
        s_ei, s_et, s_ex, s_eg, s_es = (sem("s_e_in"), sem("s_e_transposed"), sem("s_e_xT"), sem("s_e_gate_up"),
                                        sem("s_e_silu"))
        s_eh, s_eht, s_ehc, s_ey, s_eo, s_ew = (sem("s_e_h"), sem("s_e_h_transposed"), sem("s_e_hT"), sem("s_e_y"),
                                                sem("s_e_out"), sem("s_e_written"))
        s_gat, s_fin, s_out = {t: sem("s_gathered_" + t) for t in fb}, sem("s_final"), sem("s_out")
        SETS = (OTHERS, MIXED)
        GB = {OTHERS.name: 0, MIXED.name: len(OTHERS.groups)}
        TB = {OTHERS.name: 0, MIXED.name: OTHERS.n}
        EB = {OTHERS.name: 0, MIXED.name: OTHERS.tiles // U}
        NGRP = GB[MIXED.name] + len(MIXED.groups)
        block = ctx.enter_context(nc.Block())

        jobs = []
        for lo, hi in GROUPS:
            jobs += [(wqkv[:, 1], lo, hi, K, ACT.Silu), (wqkv[:, 2], lo, hi, VV, ACT.Silu)]
        for lo, hi in QGROUPS:
            jobs.append((wqkv[:, 0], L1 + lo, L1 + hi, None, ACT.Silu))
        for lo, hi in GROUPS:
            jobs += [(wfo[:, 0], lo, hi, FF, ACT.Sigmoid), (wge[:], lo, hi, Y, ACT.Sigmoid)]
        for lo, hi in QGROUPS:
            jobs.append((wfo[:, 1], lo, hi, None, ACT.Sigmoid))
        NJ = len(jobs)
        NTP = NG + NQ

        def slot(lo, hi, k):
            return steps[:, lo:hi, k, :]

        def cols(ap, lo, hi):
            return ap[:, lo * P:hi * P].rearrange("p (s x) -> p s x", x=P)

        def psum(b, lo, hi):
            return bank[b][:, 0:(hi - lo) * P].rearrange("p (s x) -> p s x", x=P)

        REGION = ((0, L1), (L1, L2))

        def per_col(tile, k, n, h, w):
            x = slice(h * P // 2, (h + 1) * P // 2) if w == HD else slice(0, P)
            ap = steps[:, bass.ds(tile, 1), k:k + n, x].rearrange("p t e x -> p (t e) x")
            return ap.unsqueeze(3).to_broadcast([P, n, P * 4 // w, w])

        def wide(ap, w):
            return ap.rearrange("p (e x w) -> p e x w", e=1, w=w)

        @block.sync
        def _(sp):
            for b in range(B):
                sp.dma_start(xr[b * C:(b + 1) * C, 0:L1, :],
                             a["x"][b, 0:T1, :].rearrange("(c s) d -> c s d", s=L1)).then_inc(s_x, 16)
                sp.dma_start(xr[b * C:(b + 1) * C, L1:, :],
                             a["x"][b, T1:, :].rearrange("(c s) d -> c s d", s=L2)).then_inc(s_x, 16)
            sp.wait_ge(s_xfz, 1)
            n = 3 * SKIP
            for b in range(B):
                g0 = b * C
                sp.dma_start(xf[g0:g0 + 1, n:, :], a["x"][b:b + 1, 0:ROWS - n, :]).then_inc(s_xf, 16)
                sp.dma_start(xf[g0 + 1:g0 + C - 1, :, :],
                             a["x"][b, ROWS - n:(C - 1) * ROWS - n, :].rearrange("(g r) d -> g r d", r=ROWS)
                             ).then_inc(s_xf, 16)
                last = N - ((C - 1) * ROWS - n)
                sp.dma_start(xf[g0 + C - 1:g0 + C, 0:last, :], a["x"][b:b + 1, N - last:, :]).then_inc(s_xf, 16)
            for r in (0, 1):
                for h in (0, 1):
                    sp.wait_ge(s_state[h], sum(n + 1 for _, n in REGION[:r + 1]))
                sp.dma_start(scr["m"][r], state[:].rearrange("p a b -> p (a b)")).then_inc(s_mout, 16)
                sp.wait_ge(s_mout, 16 * (r + 1))
                for vh in (0, 1):
                    for b in range(B):
                        lanes = slice(vh * 64 + b * H, vh * 64 + (b + 1) * H)
                        sp.dma_start(ch_m[r][lanes].rearrange("h j c i -> h j (c i)"),
                                     scr["m"][r][:, b * 256:(b + 1) * 256].rearrange("(h j) x -> h j x", j=HD)
                                     ).then_inc(s_min, 16)
                sp.wait_ge(s_bc, r + 1)
                sp.dma_start(scr["b"][r], ucopy.rearrange("p a b -> p (a b)")).then_inc(s_bout, 16)
                sp.wait_ge(s_bout, 16 * (r + 1))
                for vh in (0, 1):
                    for b in range(B):
                        lanes = slice(vh * 64 + b * H, vh * 64 + (b + 1) * H)
                        sp.dma_start(ch_b[r][lanes].rearrange("h v c i -> h v (c i)"),
                                     scr["b"][r][:, b * 256:(b + 1) * 256].rearrange("(h v) x -> h v x", v=HD)
                                     [:, vh * 4:vh * 4 + 4, :]).then_inc(s_bin, 16)
            sp.wait_ge(s_ca, 2 * C + 1)
            sp.dma_start(scr["s"].rearrange("(l i) x -> l i x", i=HD),
                         ch_s[:, :, 0:C, :].rearrange("l i c v -> l i (c v)")).then_inc(s_sout, 16)
            sp.wait_ge(s_sout, 16)
            for vh in (0, 1):
                for b in range(B):
                    rows = (vh * B + b) * P
                    sp.dma_start(state[:, vh, b * C * 4:(b + 1) * C * 4],
                                 scr["s"][rows:rows + P, :]).then_inc(s_chout, 16)
            for h in (0, 1):
                sp.wait_ge(s_bs, 2)
            sp.wait_ge(s_state[0], L1 + 1)
            sp.wait_ge(s_state[1], L1 + 1)
            sp.wait_ge(s_bp[0], L1 + 1)
            sp.wait_ge(s_bp[1], L1 + 1)
            sp.dma_start(gu.rearrange("p (e f) -> p e f", e=E), a["gate_up_proj"].rearrange("e p f -> p e f")
                         ).then_inc(s_we, 16)
            for k in (0, 1):
                sp.dma_start(dw.rearrange("p (e k d) -> p e k d", e=E, k=2)[:, :, k],
                             a["down_proj"][:, k * P:(k + 1) * P, :].rearrange("e p d -> p e d")).then_inc(s_we, 16)
            sp.wait_ge(s_zero, 2)
            for t in SETS:
                sp.dma_start(xs[t.name].rearrange("(m p) d -> p m d", p=P),
                             zeros[:, 0:D].unsqueeze(1).to_broadcast([P, t.tiles + 1, D])).then_inc(s_xz, 16)
                sp.dma_start(ys[t.name][t.tiles * P:, :], zeros[:, 0:D]).then_inc(s_xz, 16)
            for t in SETS:
                sp.wait_ge(s_scat[t.name], 16 * t.n)
                x_in = xs[t.name].rearrange("(m p) d -> p m d", p=P)
                y_out = ys[t.name].rearrange("(m p) d -> p m d", p=P)
                e0 = EB[t.name]

                def load(i, n):
                    sp.dma_start(e_in, x_in[:, bass.ds(i * U, U), :]).then_inc(s_ei, 16)

                load(0, e0)
                with sp.Fori(1, t.tiles // U) as i:
                    sp.wait_ge(s_et, i + e0)
                    load(i, i + e0)
                    sp.wait_ge(s_eo, i + e0)
                    sp.dma_start(y_out[:, bass.ds(i * U - U, U), :], e_y).then_inc(s_ew, 16)
                sp.wait_ge(s_eo, t.tiles // U + e0)
                sp.dma_start(y_out[:, t.tiles - U:t.tiles, :], e_y).then_inc(s_ew, 16)
            sp.wait_ge(s_fin, ROWS)
            n = 3 * SKIP
            for b in range(B):
                g0 = b * C
                sp.dma_start(out[b:b + 1, 0:ROWS - n, :], xf[g0:g0 + 1, n:, :]).then_inc(s_out, 16)
                sp.dma_start(out[b, ROWS - n:(C - 1) * ROWS - n, :].rearrange("(g r) d -> g r d", r=ROWS),
                             xf[g0 + 1:g0 + C - 1, :, :]).then_inc(s_out, 16)
                last = N - ((C - 1) * ROWS - n)
                sp.dma_start(out[b:b + 1, N - last:, :], xf[g0 + C - 1:g0 + C, 0:last, :]).then_inc(s_out, 16)
            sp.wait_ge(s_out, 16 * 3 * B)
            if debug is not None:
                sp.wait_ge(s_x1, L2)
                sp.dma_start(debug["steps"], steps[:].rearrange("p a b c -> p (a b c)")).then_inc(s_dbg, 16)
                sp.dma_start(debug["xf"], xf[:].rearrange("p a b -> p (a b)")).then_inc(s_dbg, 16)
                sp.dma_start(debug["gate"], gateT[:]).then_inc(s_dbg, 16)
                sp.dma_start(debug["state"], state[:].rearrange("p a b -> p (a b)")).then_inc(s_dbg, 16)
                sp.wait_ge(s_dbg, 64)

        @block.scalar
        def _(act):
            act.dma_start(cst[:], a["const"]).then_inc(s_cst, 16)
            for dst, src in ((wqkv[:, 0], "Wq"), (wqkv[:, 1], "Wk"), (wqkv[:, 2], "Wv"), (wgs[:], "Wg"),
                             (wlow[:, 0], "Wf1"), (wlow[:, 1], "Wo1"), (wup[:, 0], "Wf2"), (wup[:, 1], "Wo2"),
                             (wout[:], "Wout")):
                act.dma_start(dst, a[src]).then_inc(s_wa, 16)
            act.dma_start(lnw[:], a["ln_w"].rearrange("(p o) -> p o", o=1)).then_inc(s_wa, 16)
            for k, name in ((0, "w_gate"), (2, "w_up")):
                act.dma_start(wnat[:, k:k + 2], a[name].rearrange("(k p) d -> p k d", p=P)).then_inc(s_wf, 16)
            for k in (0, 1):
                act.dma_start(wnat[:, 4 + k], a["w_down"][:, k * P:(k + 1) * P]).then_inc(s_wf, 16)
            act.dma_start(wnat[0:E, 6], a["w_router"]).then_inc(s_wf, 16)
            act.wait_ge(s_mv, NT)
            act.wait_ge(s_zero, 2)
            S.activation(rstd[:, 0:NT], mv[:, 0:NT, 1], ACT.Sqrt, bias=eps[:]).then_inc(s_sd, 1)
            act.wait_ge(s_mv, NT + L2)
            S.activation(rstd[:, NT:], mv[:, NT:, 1], ACT.Sqrt, bias=eps[:]).then_inc(s_sd, 1)
            act.wait_ge(s_wt, 1)
            S.activation(wlowT[:], bank[7][0:HD, 0:2 * P].rearrange("p (a b) -> p a b", a=2), ACT.Copy).then_inc(s_wtc, 1)
            act.wait_ge(s_wp, 1)
            S.activation(wfo[:], bank[7][:, 0:2 * D].rearrange("p (a b) -> p a b", a=2), ACT.Copy).then_inc(s_w, 1)
            for n, (lo, hi) in enumerate(GROUPS + QGROUPS):
                act.wait_ge(s_tp, n + 1)
                dst = xnT if n < NG else xaT
                S.activation(cols(dst, lo, hi), psum(n % 2, lo, hi), ACT.Copy).then_inc(s_xT, 1)
            for j, (_, lo, hi, k, func) in enumerate(jobs):
                act.wait_ge(s_pj, j + 1)
                if k is None:
                    dst = cols(qT, lo - L1, hi - L1) if func == ACT.Silu else cols(gateT, lo, hi)
                else:
                    dst = slot(lo, hi, k)
                S.activation(dst, psum(2 + j % 4, lo, hi), func).then_inc(s_ev, 1)
                if k == K:
                    act.wait_ge(s_ev, j + 1)
                    S.activation(slot(lo, hi, PP), slot(lo, hi, K), ACT.Square).then_inc(s_sq, 1)
            act.wait_ge(s_ss, 1)
            S.activation(rk[:], bank[6], ACT.Sqrt).then_inc(s_no, 1)
            act.wait_ge(s_rk, 1)
            for g, (lo, hi) in enumerate(GROUPS):
                S.activation(xr[:, lo:hi].rearrange("p s (h i) -> p (s h) i", i=HD),
                             rk[:, lo * H:hi * H].unsqueeze(2).to_broadcast([P, (hi - lo) * H, HD]),
                             ACT.Copy).then_inc(s_rke, 1)
            act.sem_inc(s_uc[0], 1)
            act.sem_inc(s_uc[1], 1)
            for r, (_, n) in enumerate(REGION):
                base = r * L1
                with act.Fori(0, n) as i:
                    for h in (0, 1):
                        act.wait_ge(s_term[h], i + (base + 1))
                        act.wait_ge(s_bp[h], i + (base + 1))
                        S.activation(ucopy[:, h], bank[2 * h + 1], ACT.Copy).then_inc(s_uc[h], 1)
                for h in (0, 1):
                    act.wait_ge(s_bp[h], base + n + 1)
                act.wait_ge(s_bs, 2 * r + 2)
                S.activation(ucopy, ps[2][:], ACT.Copy).then_inc(s_bc, 1)
                if r == 0:
                    act.wait_ge(s_bin, 128)
            act.wait_ge(s_bin, 256)
            turn = act.alloc_register("turn_act")
            act.reg_mov(turn, L1 - 1)
            with act.Fori(0, L2) as i:
                for h in (0, 1):
                    act.wait_ge(s_red[h], i + NT)
                    tile = i + L1
                    if h:
                        act.reg_add(turn, turn, 1)
                        tile = act.snap(turn, min_val=L1, max_val=NT - 1)
                    for v in range(4):
                        ins = S.activation(vterm[:, h].rearrange("p (x v) -> p x v", v=4)[:, :, v],
                                           steps[:, bass.ds(tile, 1), VV, :].rearrange("p a x -> p (a x)"),
                                           ACT.Copy, scale=c["diag8"][:, 4 * h + v:4 * h + v + 1])
                    ins.then_inc(s_vd[h], 1)
            for g, (lo, hi) in enumerate(QGROUPS):
                act.wait_ge(s_od, g + 1)
                S.activation(osq[:, lo * P:hi * P], od[:, lo * P:hi * P], ACT.Square).then_inc(s_osq, 1)
            act.wait_ge(s_var, 1)
            S.activation(rstd2[:], bank[3][:, 0:L2], ACT.Sqrt, bias=eps[:]).then_inc(s_sd2, 1)

            act.wait_ge(s_wft, 1)
            S.activation(wT[:, 0:4], ps[3][:, 0].rearrange("p (k x) -> p k x", k=4), ACT.Copy).then_inc(s_wfT, 1)
            S.activation(wT[:, 4:6], ps[3][:, 1, 0:2 * P].rearrange("p (k x) -> p k x", k=2), ACT.Copy).then_inc(s_wfT, 1)
            S.activation(wrT[:], ps[3][:, 1, 2 * P:2 * P + E], ACT.Copy).then_inc(s_wfT, 1)
            for t in SETS:
                q, m = fb[t.name], t is MIXED
                act.wait_ge(s_fmv, TB[t.name] + t.n)
                S.activation(q["rstd"][:], q["mv"][:, :, 1], ACT.Sqrt, bias=eps[:]).then_inc(s_fsd, 1)
                for g, (lo, hi) in enumerate(t.groups):
                    n = GB[t.name] + g
                    act.wait_ge(s_ft, n + 1)
                    S.activation(fxT[:, 0:(hi - lo) * P], bank[6][:, 0:(hi - lo) * P], ACT.Copy).then_inc(s_fx, 1)
                    act.wait_ge(s_fl, n + 1)
                    S.activation(q["lg"][:, lo * E:hi * E], bank[7][:, 0:(hi - lo) * E], ACT.Copy).then_inc(s_flc, 1)
                    for k in (0, 1):
                        act.wait_ge(s_fgu, 2 * n + k + 1)
                        if n or k:
                            act.wait_ge(s_fh, 2 * n + k)
                        S.activation(fsg[:, 0:(hi - lo) * P], bank[6][:, 0:(hi - lo) * P], ACT.Silu).then_inc(s_fsg, 1)
                act.wait_ge(s_mx, 1 + m)
                S.activation(q["score"], q["mx"], ACT.Sigmoid).then_inc(s_score, 1)
            for t in SETS:
                e0 = EB[t.name]
                with act.Fori(0, t.tiles // U) as i:
                    for u in range(U):
                        act.wait_ge(s_et, i + (e0 + 1))
                        S.activation(e_xT[:, u], bank[2 * u + 1][:, 0:P], ACT.Copy).then_inc(s_ex, 1)
                    for u in range(U):
                        act.wait_ge(s_eg, i * U + (e0 * U + u + 1))
                        S.activation(e_sg[:, u], bank[2 * u][:, 0:F], ACT.Silu).then_inc(s_es, 1)
                    for u in range(U):
                        act.wait_ge(s_ey, i * U + (e0 * U + u + 1))
                        act.wait_ge(s_ew, i * 16 + (e0 * 16))
                        ins = S.activation(e_y[:, u], bank[2 * u + 1][:, P + F:], ACT.Copy)
                    ins.then_inc(s_eo, 1)

        def pool_tt(dst, src, tile, k, h, w):
            tile = G.snap(tile)
            return G.tensor_tensor(wide(dst, w), wide(src, w), per_col(tile, k, 1, h, w), ALU.mult)

        @block.gpsimd
        def _(pool):
            G.memset(zeros[:], 0.0).then_inc(s_zero, 1)
            G.memset(eps[:], LN_EPS).then_inc(s_zero, 1)
            G.memset(xf[:], 0.0).then_inc(s_xfz, 1)
            pool.wait_ge(s_wa, 160)
            G.tensor_copy(wge[:].rearrange("p (h i) -> p h i", i=HD),
                          wgs[:].unsqueeze(2).to_broadcast([P, H, HD])).then_inc(s_wge, 1)
            fk = lambda g, n: work[:, 0, g % 2, 0:n * P].rearrange("p (s x) -> p s x", x=P)
            fkk = lambda g, n: work[:, 1, g % 2, 0:n * P].rearrange("p (s x) -> p s x", x=P)
            gk = lambda g, n: decayed[:, g % 2, 0:n * P].rearrange("p (s x) -> p s x", x=P)
            pool.wait_ge(s_ev, NJ)

            def last_p(g):
                lo, hi = GROUPS[g]
                pool.wait_ge(s_m, g + 1)
                G.tensor_tensor(slot(lo, hi, PP), slot(lo, hi, PP), slot(lo, hi, Y), ALU.add).then_inc(s_p, 1)

            for g, (lo, hi) in enumerate(GROUPS):
                pool.wait_ge(s_k, g + 1)
                if g >= 2:
                    pool.wait_ge(s_m, g - 1)
                    pool.wait_ge(s_c, g - 1)
                G.tensor_tensor(fk(g, hi - lo), slot(lo, hi, FF), slot(lo, hi, K), ALU.mult).then_inc(s_fk, 1)
                pool.wait_ge(s_fk, g + 1)
                G.tensor_tensor(fkk(g, hi - lo), fk(g, hi - lo), slot(lo, hi, K), ALU.mult).then_inc(s_fkk, 1)
                G.tensor_tensor(gk(g, hi - lo), slot(lo, hi, Y), slot(lo, hi, K), ALU.mult).then_inc(s_gk, 1)
                if g:
                    last_p(g - 1)
            last_p(NG - 1)
            for h in (0, 1):
                pool.sem_inc(s_bp[h], 1)
            for r, (_, n) in enumerate(REGION):
                base = r * L1
                last = base + n - 1

                def decay(h, tile, ready):
                    pool.wait_ge(s_state[h], ready)
                    pool_tt(decayed[:, h], state[:, h], tile, FF, h, HD).then_inc(s_dec[h], 1)

                def v_times_u(h, tile, n):
                    pool.wait_ge(s_uc[h], n + 1)
                    pool.wait_ge(s_ba[h], n)
                    pool_tt(vterm[:, h], ucopy[:, h], tile, VV, h, HD).then_inc(s_bp[h], 1)

                for h in (0, 1):
                    decay(h, last, base + r + 1)
                with pool.Fori(1, n) as i:
                    for h in (0, 1):
                        decay(h, (i * -1) + last, i + (base + r + 1))
                        v_times_u(h, (i * -1) + (last + 1), i + base)
                for h in (0, 1):
                    v_times_u(h, base, base + n)
            first = NT + 2
            turn = pool.alloc_register("turn_pool")
            pool.reg_mov(turn, L1 - 1)
            with pool.Fori(0, L2) as i:
                tile = i + L1
                for h in (0, 1):
                    pool.wait_ge(s_state[h], i + (first + 1))
                    if h:
                        pool.reg_add(turn, turn, 1)
                        tile = pool.snap(turn, min_val=L1, max_val=NT - 1)
                    pool_tt(decayed[:, h], state[:, h], tile, FF, h, 4).then_inc(s_dec[h], 1)
                for h in (0, 1):
                    pool.wait_ge(s_state[h], i + (first + 2))
                    G.tensor_tensor(qs[:, bass.ds(i, 1), h].rearrange("p s x v -> p (s x) v"),
                                    state[:, h].rearrange("p (x v) -> p x v", v=4),
                                    qT[:, bass.ds(G.snap(i * P), P)].unsqueeze(2).to_broadcast([P, P, 4]),
                                    ALU.mult).then_inc(s_q[h], 1)
            for t in SETS:
                q = fb[t.name]
                pool.wait_ge(s_xz, 64)
                pool.wait_ge(s_idx, 1 + (t is MIXED))
                for j in range(t.n):
                    pool.wait_ge(s_sc, TB[t.name] + j + 1)
                    G.indirect_dma_start(xs[t.name], bass.IndirectOffsetOnAxis(ap=q["idx"][:, j:j + 1].bitcast(U32), axis=0),
                                         q["nat"][:, j * D:(j + 1) * D], None).then_inc(s_scat[t.name], 16)
            for t in SETS:
                q = fb[t.name]
                pool.wait_ge(s_ew, 16 * (EB[t.name] + t.tiles // U))
                for j in range(t.n):
                    G.indirect_dma_start(q["nat"][:, j * D:(j + 1) * D], None, ys[t.name],
                                         bass.IndirectOffsetOnAxis(ap=q["idx"][:, j:j + 1].bitcast(U32), axis=0)
                                         ).then_inc(s_gat[t.name], 16)

        @block.vector
        def _(dve):
            dve.wait_ge(s_x, 16 * 2 * B)
            for s in range(NT):
                V.bn_stats(stats[:, s], xr[:, s]).then_inc(s_st, 1)
            for s in range(NT):
                dve.wait_ge(s_st, s + 1)
                V.bn_aggr(mv[:, s], stats[:, s]).then_inc(s_mv, 1)
            dve.wait_ge(s_xf, 16 * 3 * B)
            dve.wait_ge(s_mv, NT)
            for s in range(L2):
                V.bn_stats(stats[:, s], xf[:, 3 * s]).then_inc(s_st, 1)
            for s in range(L2):
                dve.wait_ge(s_st, NT + s + 1)
                V.bn_aggr(mv[:, NT + s], stats[:, s]).then_inc(s_mv, 1)
            dve.wait_ge(s_sd, 1)
            V.reciprocal(rstd[:, 0:NT], rstd[:, 0:NT]).then_inc(s_rs, 1)
            dve.wait_ge(s_rs, 1)
            for s in range(NT):
                V.tensor_scalar(xr[:, s], xr[:, s], mv[:, s, 0:1], rstd[:, s:s + 1], ALU.subtract,
                                ALU.mult).then_inc(s_xn, 1)
            dve.wait_ge(s_sd, 2)
            V.reciprocal(rstd[:, NT:], rstd[:, NT:]).then_inc(s_rs, 1)
            dve.wait_ge(s_rs, 2)
            for s in range(L2):
                V.tensor_scalar(xa[:, s], xf[:, 3 * s], mv[:, NT + s, 0:1], rstd[:, NT + s:NT + s + 1],
                                ALU.subtract, ALU.mult).then_inc(s_xn, 1)
            dve.wait_ge(s_no, 1)
            V.tensor_scalar(rk[:], rk[:], NORM_EPS, None, ALU.max).then_inc(s_nm, 1)
            dve.wait_ge(s_nm, 1)
            V.reciprocal(rk[:], rk[:]).then_inc(s_rk, 1)
            dve.wait_ge(s_ev, NJ)
            for g, (lo, hi) in enumerate(GROUPS):
                dve.wait_ge(s_rb, g + 1)
                V.tensor_tensor(slot(lo, hi, K), slot(lo, hi, K), psum(g % 2, lo, hi), ALU.mult).then_inc(s_k, 1)
            for g, (lo, hi) in enumerate(GROUPS):
                dve.wait_ge(s_c, g + 1)
                V.tensor_tensor(slot(lo, hi, PP), slot(lo, hi, Y), psum(2 + g % 2, lo, hi), ALU.mult).then_inc(s_gc, 1)
                dve.wait_ge(s_gk, g + 1)
                dve.wait_ge(s_gc, g + 1)
                n = hi - lo
                V.scalar_tensor_tensor(slot(lo, hi, Y), work[:, 0, g % 2, 0:n * P].rearrange("p (s x) -> p s x", x=P),
                                       -1.0, slot(lo, hi, Y), ALU.mult, ALU.mult).then_inc(s_y, 1)
                dve.wait_ge(s_y, g + 1)
                V.tensor_tensor(slot(lo, hi, PP), slot(lo, hi, PP),
                                decayed[:, g % 2, 0:n * P].rearrange("p (s x) -> p s x", x=P),
                                ALU.mult).then_inc(s_m, 1)

            def products(h, tile, ready, w):
                dve.wait_ge(s_state[h], ready)
                st = state[:, h].unsqueeze(1).to_broadcast([P, 2, HALF]).rearrange("p e (x w) -> p e x w", w=w)
                V.tensor_tensor(work[:, h].rearrange("p e (x w) -> p e x w", w=w), st, per_col(tile, Y, 2, h, w),
                                ALU.mult).then_inc(s_prod[h], 1)

            def update(h, tile, done, w, used=None):
                dve.wait_ge(s_red[h], done)
                V.tensor_tensor(work[:, h].rearrange("p e (x w) -> p e x w", w=w),
                                ps[h][:].rearrange("p e (x w) -> p e x w", w=w), per_col(tile, K, 2, h, w),
                                ALU.mult).then_inc(s_term[h], 1)
                dve.wait_ge(s_term[h], done)
                dve.wait_ge(s_dec[h], done)
                V.tensor_tensor(decayed[:, h], decayed[:, h], work[:, h, 1], ALU.add).then_inc(s_add[h], 1)
                dve.wait_ge(s_add[h], done)
                if used is not None:
                    dve.wait_ge(s_q[h], used)
                V.tensor_tensor(state[:, h], decayed[:, h], work[:, h, 0], ALU.add).then_inc(s_state[h], 1)

            for r, (first, n) in enumerate(REGION):
                base = r * L1
                if r:
                    dve.wait_ge(s_min, 128)
                else:
                    dve.wait_ge(s_p, NG)
                for h in (0, 1):
                    V.tensor_copy(state[:, h].rearrange("p (x w) -> p x w", w=HD),
                                  c["diag8"].unsqueeze(1).to_broadcast([P, P // 2, HD])).then_inc(s_state[h], 1)
                last = base + n - 1
                r0 = base + r + 1
                products(0, last, r0, HD)
                products(1, last, r0, HD)
                update(0, last, base + 1, HD)
                with dve.Fori(1, n) as i:
                    tile = (i * -1) + last
                    products(0, tile, i + r0, HD)
                    update(1, tile + 1, i + base, HD)
                    products(1, tile, i + r0, HD)
                    update(0, tile, i + (base + 1), HD)
                update(1, base, base + n, HD)
            V.memset(ch_s[:, :, 0, :], 0.0).then_inc(s_ca, 1)
            for r, n in ((0, C), (1, C - 1)):
                dve.wait_ge(s_min, 128 * (r + 1))
                dve.wait_ge(s_bin, 128 * (r + 1))
                if r:
                    dve.wait_ge(s_ca, C + 1)
                    V.tensor_copy(ch_s[:, :, 0, :], ch_s[:, :, C, :]).then_inc(s_ca, 1)
                for i in range(n):
                    m = r * C + i + 1
                    dve.wait_ge(s_ca, m + r)
                    V.tensor_tensor(ch_pr, ch_m[r][:, :, i, :].rearrange("p j i -> p i j").unsqueeze(1)
                                    .to_broadcast([P, 4, HD, HD]), ch_s[:, :, i, :].rearrange("p j v -> p v j")
                                    .unsqueeze(2).to_broadcast([P, 4, HD, HD]), ALU.mult).then_inc(s_cm, 1)
                    dve.wait_ge(s_cm, m)
                    V.tensor_reduce(ch_sum, ch_pr, AX.X, ALU.add).then_inc(s_cr, 1)
                    dve.wait_ge(s_cr, m)
                    V.tensor_tensor(ch_s[:, :, i + 1, :].rearrange("p i v -> p v i"), ch_sum,
                                    ch_b[r][:, :, i, :], ALU.add).then_inc(s_ca, 1)
            dve.wait_ge(s_chout, 128)
            for h in (0, 1):
                dve.sem_inc(s_state[h], 1)
            r0 = NT + 3
            products(0, L1, r0, 4)
            products(1, L1, r0, 4)
            update(0, L1, NT + 1, 4)
            update(1, L1, NT + 1, 4)
            with dve.Fori(1, L2) as i:
                for h in (0, 1):
                    products(h, i + L1, i + r0, 4)
                for h in (0, 1):
                    update(h, i + L1, i + (NT + 1), 4, i)
            for g, (lo, hi) in enumerate(QGROUPS):
                dve.wait_ge(s_o, g + 1)
                if g == 0:
                    dve.wait_ge(s_state[0], NT + 3 + L2)
                    dve.wait_ge(s_state[1], NT + 3 + L2)
                V.tensor_tensor(cols(og, lo, hi), psum(4 + g, lo, hi), cols(gateT, lo, hi), ALU.mult).then_inc(s_og, 1)
            for g, (lo, hi) in enumerate(QGROUPS):
                dve.wait_ge(s_mu, g + 1)
                V.tensor_tensor(cols(od, lo, hi), cols(og, lo, hi), psum(g, lo, hi), ALU.subtract).then_inc(s_od, 1)
            for g, (lo, hi) in enumerate(QGROUPS):
                dve.wait_ge(s_osq, g + 1)
                V.tensor_scalar(cols(od, lo, hi), cols(od, lo, hi), lnw[:], None, ALU.mult).then_inc(s_dw, 1)
            dve.wait_ge(s_sd2, 1)
            V.reciprocal(rstd2[:], rstd2[:]).then_inc(s_rs2, 1)
            dve.wait_ge(s_rs2, 1)
            for g, (lo, hi) in enumerate(QGROUPS):
                dve.wait_ge(s_at, g + 1)
                for s in range(lo, hi):
                    V.scalar_tensor_tensor(xf[:, 3 * s], psum(4 + g, lo, hi)[:, s - lo], rstd2[:, s:s + 1], xf[:, 3 * s],
                                           ALU.mult, ALU.add).then_inc(s_x1, 1)
            chained = [0]

            def link(ins):
                chained[0] += 1
                ins.then_inc(s_link, 1)
                dve.wait_ge(s_link, chained[0])

            dve.wait_ge(s_o, NQ)
            link(V.memset(r_one, 1.0))
            for t in SETS:
                q, m = fb[t.name], t is MIXED
                nat = q["nat"].rearrange("p (n d) -> p n d", d=D)
                t0 = TB[t.name]
                if m:
                    dve.wait_ge(s_x1, L2)
                for j, row in enumerate(t.rows):
                    V.bn_stats(q["stats"][:, j], xf[:, row]).then_inc(s_fst, 1)
                for j in range(t.n):
                    dve.wait_ge(s_fst, t0 + j + 1)
                    V.bn_aggr(q["mv"][:, j], q["stats"][:, j]).then_inc(s_fmv, 1)
                dve.wait_ge(s_fsd, 1 + m)
                V.reciprocal(q["rstd"][:], q["rstd"][:]).then_inc(s_frs, 1)
                dve.wait_ge(s_frs, 1 + m)
                for j, row in enumerate(t.rows):
                    V.tensor_scalar(nat[:, j], xf[:, row], q["mv"][:, j, 0:1], q["rstd"][:, j:j + 1], ALU.subtract,
                                    ALU.mult).then_inc(s_fn, 1)
                for g, (lo, hi) in enumerate(t.groups):
                    n, w = GB[t.name] + g, (hi - lo) * P
                    for k in (0, 1):
                        dve.wait_ge(s_fsg, 2 * n + k + 1)
                        if n and not k:
                            dve.wait_ge(s_fy, n)
                        V.tensor_tensor(fhT[:, k, 0:w], fsg[:, 0:w], bank[7][:, 0:w], ALU.mult).then_inc(s_fh, 1)
                    dve.wait_ge(s_fy, n + 1)
                    for j in range(lo, hi):
                        row = t.rows[j]
                        ins = V.tensor_tensor(xf[:, row], xf[:, row], bank[6][:, (j - lo) * D:(j - lo + 1) * D], ALU.add)
                    ins.then_inc(s_fa, 1)
                dve.wait_ge(s_flc, GB[t.name] + len(t.groups))
                ne = lambda ap: ap.rearrange("p (n e) -> p n e", e=E)
                en = lambda ap: ap[:, 0:t.n * E].rearrange("p (e n) -> p e n", e=E)
                lg, oh = ne(q["lg"]), ne(q["oh"])
                full = [P, t.n, E]
                V.tensor_reduce(q["mx"], lg, AX.X, ALU.max).then_inc(s_mx, 1)
                dve.wait_ge(s_mx, 1 + m)
                link(V.tensor_tensor(oh, lg, q["mx"].unsqueeze(2).to_broadcast(full), ALU.is_equal))
                prefer = c["prefer"].unsqueeze(1).to_broadcast(full)
                link(V.tensor_tensor(oh, oh, prefer, ALU.mult))
                link(V.tensor_reduce(q["mw"], oh, AX.X, ALU.max))
                link(V.tensor_tensor(oh, prefer, q["mw"].unsqueeze(2).to_broadcast(full), ALU.is_equal))
                V.tensor_tensor(oh, oh, c["valid_" + t.name].unsqueeze(2).to_broadcast(full), ALU.mult).then_inc(s_oh, 1)
                link(V.memset(en(r_keep), 1.0))
                link(V.memset(en(r_keep)[:, :, 0:1], 0.0))
                dve.wait_ge(s_rank, 1 + m)
                link(V.tensor_copy(en(r_tot), bank[7][:, 0:t.n * E].rearrange("p (n e) -> p e n", e=E)))
                w = t.n * E
                link(V.tensor_tensor_scan(r_inc[:, 0:w], r_keep[:, 0:w], r_tot[:, 0:w], 0.0, ALU.mult, ALU.add))
                link(V.tensor_tensor(en(r_a), c["steps128"][:, 0:t.n].unsqueeze(1).to_broadcast([P, E, t.n]),
                                     en(r_inc)[:, :, t.n - 1:t.n].to_broadcast([P, E, t.n]), ALU.is_lt))
                link(V.tensor_reduce(r_nt, en(r_a), AX.X, ALU.add))
                link(V.tensor_tensor_scan(r_ti, r_one, r_nt, 0.0, ALU.mult, ALU.add))
                link(V.tensor_tensor(r_ts, r_ti, r_nt, ALU.subtract))
                link(V.tensor_tensor(r_inc[:, 0:w], r_inc[:, 0:w], r_tot[:, 0:w], ALU.subtract))
                link(V.scalar_tensor_tensor(en(r_inc), r_ts.unsqueeze(2).to_broadcast([P, E, t.n]), float(P), en(r_inc),
                                            ALU.mult, ALU.add))
                link(V.tensor_tensor(ne(r_a[:, 0:w]), bank[6][:, 0:w].rearrange("p (n e) -> p n e", e=E),
                                     en(r_inc).rearrange("p e n -> p n e"), ALU.add))
                link(V.tensor_tensor(ne(r_a[:, 0:w]), ne(r_a[:, 0:w]), oh, ALU.mult))
                link(V.tensor_reduce(q["slot"], ne(r_a[:, 0:w]), AX.X, ALU.add))
                V.tensor_tensor(q["idx"], q["slot"], c["spare_" + t.name], ALU.add).then_inc(s_idx, 1)
                te = r_te[0:1, 0:t.tiles * E].rearrange("p (m e) -> p m e", e=E)
                link(V.tensor_tensor(te, r_ti[0:1].unsqueeze(1).to_broadcast([1, t.tiles, E]),
                                     c["tileno"][0:1, 0:t.tiles].unsqueeze(2).to_broadcast([1, t.tiles, E]), ALU.is_le))
                link(V.tensor_reduce(r_tf[0:1, 0:t.tiles], te, AX.X, ALU.add))
                V.tensor_scalar(q["te"][:], r_tf[0:1, 0:t.tiles], float(E - 1), None, ALU.min).then_inc(s_te, 1)
                dve.wait_ge(s_score, 1 + m)
                for j in range(t.n):
                    V.tensor_scalar(nat[:, j], nat[:, j], q["score"][:, j:j + 1], None, ALU.mult).then_inc(s_sc, 1)
            for t in SETS:
                e0 = EB[t.name]
                with dve.Fori(0, t.tiles // U) as i:
                    for u in range(U):
                        dve.wait_ge(s_es, i * U + (e0 * U + u + 1))
                        V.tensor_tensor(e_h[:, u], e_sg[:, u], bank[2 * u][:, F:], ALU.mult).then_inc(s_eh, 1)
                    for u in range(U):
                        dve.wait_ge(s_eht, i * U + (e0 * U + u + 1))
                        V.tensor_copy(e_hT[:, u], bank[2 * u + 1][:, P:P + F]).then_inc(s_ehc, 1)
            for t in SETS:
                nat = fb[t.name]["nat"].rearrange("p (n d) -> p n d", d=D)
                for j, row in enumerate(t.rows):
                    dve.wait_ge(s_gat[t.name], 16 * t.n)
                    V.tensor_tensor(xf[:, row], xf[:, row], nat[:, j], ALU.add).then_inc(s_fin, 1)

        @block.tensor
        def _(pe):
            pe.wait_ge(s_cst, 16)
            pe.wait_ge(s_wa, 160)
            for k in (0, 1):
                ins = T.transpose(bank[7][0:HD, k * P:(k + 1) * P], wlow[:, k], c["ident"])
            ins.then_inc(s_wt, 1)
            pe.wait_ge(s_wtc, 1)
            for k in (0, 1):
                ins = T.matmul(bank[7][:, k * D:(k + 1) * D], wlowT[:, k], wup[:, k], start=True, stop=True)
            ins.then_inc(s_wp, 1)
            for n, (lo, hi) in enumerate(GROUPS + QGROUPS):
                pe.wait_ge(s_xn, hi + (NT if n >= NG else 0))
                if n >= 2:
                    pe.wait_ge(s_xT, n - 1)
                for s in range(lo, hi):
                    src = xr[:, s] if n < NG else xa[:, s]
                    ins = T.transpose(bank[n % 2][:, (s - lo) * P:(s - lo + 1) * P], src, c["ident"])
                ins.then_inc(s_tp, 1)
            pe.wait_ge(s_w, 1)
            pe.wait_ge(s_wge, 1)
            pe.wait_ge(s_xT, NTP)
            for j, (w, lo, hi, k, func) in enumerate(jobs):
                if j >= 4:
                    pe.wait_ge(s_ev, j - 3)
                src = xaT if k is None and func == ACT.Sigmoid else xnT
                T.matmul(bank[2 + j % 4][:, 0:(hi - lo) * P], w, src[:, lo * P:hi * P],
                         start=True, stop=True).then_inc(s_pj, 1)
            for g, (lo, hi) in enumerate(GROUPS):
                pe.wait_ge(s_sq, g + 1)
                for s in range(lo, hi):
                    ins = T.matmul(bank[6][:, s * H:(s + 1) * H], steps[:, s, PP], c["heads"], start=True, stop=True)
            ins.then_inc(s_ss, 1)
            for g, (lo, hi) in enumerate(GROUPS):
                pe.wait_ge(s_rke, g + 1)
                if g >= 2:
                    pe.wait_ge(s_k, g - 1)
                for s in range(lo, hi):
                    ins = T.matmul(bank[g % 2][:, (s - lo) * P:(s - lo + 1) * P], xr[:, s], c["ident"], start=True, stop=True)
                ins.then_inc(s_rb, 1)
            pe.wait_ge(s_ev, NJ)
            for g, (lo, hi) in enumerate(GROUPS):
                pe.wait_ge(s_fkk, g + 1)
                if g >= 2:
                    pe.wait_ge(s_gc, g - 1)
                T.matmul(bank[2 + g % 2][:, 0:(hi - lo) * P], c["block"], work[:, 1, g % 2, 0:(hi - lo) * P],
                         start=True, stop=True).then_inc(s_c, 1)
            for h in (0, 1):
                pe.sem_inc(s_ba[h], 1)
            pe.wait_ge(s_zero, 1)

            def sums(h):
                for e in (0, 1):
                    ins = T.matmul(bank[2 * h + e], c["block"], work[:, h, e], start=True, stop=True)
                return ins

            for r, (_, n) in enumerate(REGION):
                base = r * L1
                if r:
                    pe.wait_ge(s_bc, 1)
                pe.wait_ge(s_gc, NG)
                for h in (0, 1):
                    T.matmul(bank[4 + h], zeros[:, 0:P], zeros[:], start=True, stop=False)
                def add_sum(h, n):
                    pe.wait_ge(s_bp[h], n)
                    T.matmul(bank[4 + h], c["ident"], vterm[:, h], start=False, stop=False).then_inc(s_ba[h], 1)

                for h in (0, 1):
                    pe.wait_ge(s_prod[h], base + 1)
                    pe.wait_ge(s_uc[h], base + 1)
                    sums(h).then_inc(s_red[h], 1)
                with pe.Fori(1, n) as i:
                    for h in (0, 1):
                        pe.wait_ge(s_prod[h], i + (base + 1))
                        pe.wait_ge(s_uc[h], i + (base + 1))
                        sums(h).then_inc(s_red[h], 1)
                        add_sum(h, i + (base + 1))
                for h in (0, 1):
                    add_sum(h, base + n + 1)
                for h in (0, 1):
                    T.matmul(bank[4 + h], zeros[:, 0:P], zeros[:], start=False, stop=True).then_inc(s_bs, 1)
            with pe.Fori(0, L2) as i:
                for h in (0, 1):
                    pe.wait_ge(s_prod[h], i + (NT + 1))
                    T.matmul(bank[2 * h + 1], c["block"], work[:, h, 1], start=True, stop=True)
                    T.matmul(bank[2 * h], c["block"], work[:, h, 0], start=True, stop=False)
                    pe.wait_ge(s_vd[h], i + 1)
                    T.matmul(bank[2 * h], c["block"], vterm[:, h], start=False, stop=True).then_inc(s_red[h], 1)
            pe.wait_ge(s_bc, 2)
            for g, (lo, hi) in enumerate(QGROUPS):
                for h in (0, 1):
                    pe.wait_ge(s_q[h], hi)
                for v in range(HD):
                    ins = T.matmul(psum(4 + g, lo, hi), c["sel"][:, v * P:(v + 1) * P], qs[:, lo:hi, v // 4, :, v % 4],
                                   start=(v == 0), stop=(v == HD - 1))
                ins.then_inc(s_o, 1)
            for g, (lo, hi) in enumerate(QGROUPS):
                pe.wait_ge(s_og, g + 1)
                T.matmul(bank[g][:, 0:(hi - lo) * P], c["mean"], og[:, lo * P:hi * P], start=True,
                         stop=True).then_inc(s_mu, 1)
            for s in range(L2):
                pe.wait_ge(s_osq, s // 4 + 1)
                ins = T.matmul(bank[3][:, s:s + 1], osq[:, s * P:(s + 1) * P], c["mean"][:, 0:1], start=True, stop=True)
            ins.then_inc(s_var, 1)
            for g, (lo, hi) in enumerate(QGROUPS):
                pe.wait_ge(s_dw, g + 1)
                for s in range(lo, hi):
                    ins = T.matmul(bank[4 + g][:, (s - lo) * D:(s - lo + 1) * D], od[:, s * P:(s + 1) * P], wout[:],
                                   start=True, stop=True)
                ins.then_inc(s_at, 1)
            pe.wait_ge(s_wf, 80)
            pe.wait_ge(s_x1, L2)
            for k in range(4):
                T.transpose(bank[6][:, k * P:(k + 1) * P], wnat[:, k], c["ident"])
            for k in range(2):
                T.transpose(bank[7][:, k * P:(k + 1) * P], wnat[:, 4 + k], c["ident"])
            T.transpose(bank[7][:, 2 * P:2 * P + E], wnat[0:E, 6], c["ident"][0:E, 0:E]).then_inc(s_wft, 1)
            pe.wait_ge(s_wfT, 3)
            for t in SETS:
                q, m = fb[t.name], t is MIXED
                nat = q["nat"].rearrange("p (n d) -> p n d", d=D)
                for g, (lo, hi) in enumerate(t.groups):
                    n, w = GB[t.name] + g, (hi - lo) * P
                    pe.wait_ge(s_fn, TB[t.name] + hi)
                    if n:
                        pe.wait_ge(s_fa, n)
                    if m and not g:
                        pe.wait_ge(s_idx, 1)
                    for j in range(lo, hi):
                        ins = T.transpose(bank[6][:, (j - lo) * P:(j - lo + 1) * P], nat[:, j], c["ident"])
                    ins.then_inc(s_ft, 1)
                    pe.wait_ge(s_fx, n + 1)
                    for j in range(lo, hi):
                        ins = T.matmul(bank[7][:, (j - lo) * E:(j - lo + 1) * E], fxT[:, (j - lo) * P:(j - lo + 1) * P],
                                       wrT[:], start=True, stop=True)
                    ins.then_inc(s_fl, 1)
                    pe.wait_ge(s_flc, n + 1)
                    for k in (0, 1):
                        if k:
                            pe.wait_ge(s_fh, 2 * n + 1)
                        T.matmul(bank[6][:, 0:w], wT[:, k], fxT[:, 0:w], start=True, stop=True)
                        T.matmul(bank[7][:, 0:w], wT[:, 2 + k], fxT[:, 0:w], start=True, stop=True).then_inc(s_fgu, 1)
                    pe.wait_ge(s_fh, 2 * n + 2)
                    for j in range(lo, hi):
                        at = (j - lo) * P
                        for k in (0, 1):
                            ins = T.matmul(bank[6][:, at:at + D], fhT[:, k, at:at + P], wT[:, 4 + k], start=(k == 0),
                                           stop=(k == 1))
                    ins.then_inc(s_fy, 1)
                pe.wait_ge(s_fa, GB[t.name] + len(t.groups))
                pe.wait_ge(s_oh, 1 + m)
                T.matmul(bank[6][:, 0:t.n * E], c["before"], q["oh"], start=True, stop=True)
                T.matmul(bank[7][:, 0:t.n * E], c["ones"], q["oh"], start=True, stop=True).then_inc(s_rank, 1)
            pe.wait_ge(s_we, 48)
            pe.wait_ge(s_te, 2)
            for t in SETS:
                te, e0 = fb[t.name]["te"], EB[t.name]
                with pe.Fori(0, t.tiles // U) as i:
                    k0 = i * U + e0 * U
                    pe.wait_ge(s_ei, i * 16 + (e0 + 1) * 16)
                    for u in range(U):
                        pe.wait_ge(s_eo, i + e0)
                        ins = T.transpose(bank[2 * u + 1][:, 0:P], e_in[:, u], c["ident"])
                    ins.then_inc(s_et, 1)
                    ex = [pe.value_load(te[0:1, bass.ds(i * U + u, 1)], min_val=0, max_val=E - 1) for u in range(U)]
                    for u in range(U):
                        pe.wait_ge(s_ex, k0 + (u + 1))
                        T.matmul(bank[2 * u], e_xT[:, u], gu[:, bass.ds(ex[u] * (2 * F), 2 * F)], start=True,
                                 stop=True).then_inc(s_eg, 1)
                    for u in range(U):
                        pe.wait_ge(s_eh, k0 + (u + 1))
                        for k in (0, 1):
                            ins = T.transpose(bank[2 * u + 1][:, P + k * P:P + (k + 1) * P],
                                              e_h[:, u, k * P:(k + 1) * P], c["ident"])
                        ins.then_inc(s_eht, 1)
                    for u in range(U):
                        pe.wait_ge(s_ehc, k0 + (u + 1))
                        for k in (0, 1):
                            ins = T.matmul(bank[2 * u + 1][:, P + F:], e_hT[:, u, k * P:(k + 1) * P],
                                           dw[:, bass.ds(ex[u] * F + k * D, D)], start=(k == 0), stop=(k == 1))
                        ins.then_inc(s_ey, 1)


_NAMES = {
    "L0_attn_x": "x", "L0_attn_Wq": "Wq", "L0_attn_Wk": "Wk", "L0_attn_Wv": "Wv", "L0_attn_Wf1": "Wf1",
    "L0_attn_Wf2": "Wf2", "L0_attn_Wg": "Wg", "L0_attn_Wo1": "Wo1", "L0_attn_Wo2": "Wo2",
    "L0_attn_ln_w": "ln_w", "L0_attn_Wout": "Wout", "L0_ffn_w_router": "w_router",
    "L0_ffn_gate_up_proj": "gate_up_proj", "L0_ffn_down_proj": "down_proj", "L0_ffn_w_gate": "w_gate",
    "L0_ffn_w_up": "w_up", "L0_ffn_w_down": "w_down",
}


def kernel(**inputs):
    import concourse.bacc as bacc
    from concourse.bass_utils import run_bass_kernel_spmd

    nc = bacc.Bacc("TRN2", target_bir_lowering=False, num_devices=1)
    arrays, aps = {}, {}
    for name, short in _NAMES.items():
        arrays[short] = np.ascontiguousarray(inputs[name])
    arrays["const"] = CONST
    for short, v in arrays.items():
        aps[short] = nc.dram_tensor(short, v.shape, F32, kind="ExternalInput").ap()
    out = nc.dram_tensor("out", (B, N, D), F32, kind="ExternalOutput").ap()
    xs = {t.name: nc.dram_tensor("xs_" + t.name, ((t.tiles + 1) * P, D), F32).ap() for t in (OTHERS, MIXED)}
    ys = {t.name: nc.dram_tensor("ys_" + t.name, ((t.tiles + 1) * P, D), F32).ap() for t in (OTHERS, MIXED)}
    scr = {"m": [nc.dram_tensor(f"chain_m{r}", (P, COLS), F32).ap() for r in (0, 1)],
           "b": [nc.dram_tensor(f"chain_b{r}", (P, COLS), F32).ap() for r in (0, 1)],
           "s": nc.dram_tensor("chain_s", (P * HD, C * 4), F32).ap()}
    build(nc, aps, out, xs, ys, scr)
    r = run_bass_kernel_spmd(nc, [arrays], core_ids=[0])
    return r.results[0]["out"]
```

```python
import numpy as np

import concourse.bass as bass
from concourse import mybir
from contextlib import ExitStack

F32 = mybir.dt.float32
I32 = mybir.dt.int32
U32 = mybir.dt.uint32
ALU = mybir.AluOpType
ACT = mybir.ActivationFunctionType
AX = mybir.AxisListType

B, N, D = 4, 1024, 128
H = 16
HD = D // H
C = 32
P = 128
NOUT = (N + 2) // 3
L2 = -(-NOUT // C)
L1 = (N - C * L2) // C
T1 = C * L1
SKIP = (N - NOUT) - T1
NT = L1 + L2
ROWS = 3 * L2
LN_EPS = 1e-5
NORM_EPS = 1e-12
E, F = 16, 256
COLS = P * HD
HALF = COLS // 2
assert T1 + C * L2 == N and SKIP >= 0


U = 2


class Tokens:

    def __init__(self, name, rows, valid):
        self.name, self.rows = name, rows
        self.n = len(rows)
        self.need = (valid - E) // P + E
        self.tiles = -(-self.need // U) * U
        self.groups = [(4 * g, min(4 * g + 4, self.n)) for g in range(-(-self.n // 4))]


class Run:

    def __init__(self, t, first, n, g0, base):
        self.t, self.first, self.n, self.g0, self.base = t, first, n, g0, base


OTHERS = Tokens("others", [j for j in range(ROWS) if j % 3], 2 * B * (N // 3))
MIXED = Tokens("mixed", [j for j in range(ROWS) if j % 3 == 0], B * NOUT)


def row_valid():
    tok = 3 * L2 * (np.arange(P)[:, None] % C) - 3 * SKIP + np.arange(ROWS)[None, :]
    return (tok >= 0) & (tok < N)


def constants():
    p = np.arange(P)
    parts = {}
    parts["ident"] = np.eye(P)
    parts["block"] = (p[:, None] // HD == p[None, :] // HD)
    parts["heads"] = (p[:, None] // HD == np.arange(H)[None, :])
    parts["diag8"] = (p[:, None] % HD == np.arange(HD)[None, :])
    parts["sel"] = np.concatenate([parts["block"] & (p[None, :] % HD == v) for v in range(HD)], 1)
    parts["before"] = (p[:, None] < p[None, :])
    parts["ones"] = np.ones((P, P))
    parts["mean"] = np.full((P, P), 1.0 / D)
    valid = row_valid()
    for t in (OTHERS, MIXED):
        v = valid[:, t.rows]
        parts["valid_" + t.name] = v
        spare = np.where(v, 0, t.tiles * P + np.cumsum(~v.ravel()).reshape(v.shape) - 1)
        parts["spare_" + t.name] = spare
        assert (~v).sum() <= P
    parts["prefer"] = np.tile(E - np.arange(E)[None, :], (P, 1))
    parts["steps128"] = np.tile(P * np.arange(OTHERS.n)[None, :], (P, 1))
    parts["tileno"] = np.tile(np.arange(OTHERS.tiles)[None, :], (P, 1))
    at, n = {}, 0
    for k, a in parts.items():
        at[k] = (n, n + a.shape[1])
        n += a.shape[1]
    return np.concatenate([np.asarray(a, np.float32) for a in parts.values()], 1), at


CONST, AT = constants()



Y, K, PP, FF, VV = range(5)
GROUPS = [(4 * g, min(4 * g + 4, NT)) for g in range(-(-NT // 4))]
QGROUPS = [(4 * g, min(4 * g + 4, L2)) for g in range(-(-L2 // 4))]
NG, NQ = len(GROUPS), len(QGROUPS)


def spread(ap, *shape):
    return ap.to_broadcast([P, *shape])


def build(nc, a, out, xs, ys, scr, debug=None):
    ctx = ExitStack()
    with ctx:
        def sb(name, shape, dt=F32):
            return ctx.enter_context(nc.sbuf_tensor(name, shape, dt))

        def sem(name):
            return ctx.enter_context(nc.semaphore(name))

        V, S, G, T = nc.vector, nc.scalar, nc.gpsimd, nc.tensor

        cst = sb("cst", [P, CONST.shape[1]])
        c = {k: cst[:, lo:hi] for k, (lo, hi) in AT.items()}
        zeros = sb("zeros", [P, HALF])
        eps = sb("eps", [P, 1])
        early = sb("early", [P, L2 * COLS])
        xr = early[:, 0:NT * D].rearrange("p (s d) -> p s d", s=NT)
        xnT = early[:, NT * D:2 * NT * D]
        xa = early[:, 2 * NT * D:2 * NT * D + L2 * D].rearrange("p (s d) -> p s d", s=L2)
        xaT = early[:, 2 * NT * D + L2 * D:2 * NT * D + 2 * L2 * D]
        nm, nb = C * HD * HD, C * HD * 4
        ch_m = [early[:, r * nm:(r + 1) * nm].rearrange("p (j c i) -> p j c i", j=HD, c=C) for r in (0, 1)]
        ch_b = [early[:, 2 * nm + r * nb:2 * nm + (r + 1) * nb].rearrange("p (v c i) -> p v c i", v=4, c=C)
                for r in (0, 1)]
        at = 2 * nm + 2 * nb
        ch_s = early[:, at:at + HD * (C + 1) * 4].rearrange("p (i c v) -> p i c v", i=HD, c=C + 1)
        at += HD * (C + 1) * 4
        ch_pr = early[:, at:at + 4 * HD * HD].rearrange("p (v i j) -> p v i j", v=4, i=HD)
        at += 4 * HD * HD
        ch_sum = early[:, at:at + 4 * HD].rearrange("p (v i) -> p v i", v=4)
        qs = early[:, :].rearrange("p (s h x v) -> p s h x v", s=L2, h=2, v=4)
        xf = sb("xf", [P, ROWS, D])
        steps = sb("steps", [P, NT, 5, P])
        qT = sb("qT", [P, L2 * P])
        gateT = sb("gateT", [P, L2 * P])
        wqkv = sb("wqkv", [P, 3, D])
        wgs = sb("wgs", [P, H])
        wge = sb("wge", [P, D])
        wlow = sb("wlow", [P, 2, HD])
        wlowT = sb("wlowT", [HD, 2, P])
        wup = sb("wup", [HD, 2, D])
        wfo = sb("wfo", [P, 2, D])
        wout = sb("wout", [P, D])
        lnw = sb("lnw", [P, 1])
        state = sb("state", [P, 2, HALF])
        work = sb("work", [P, 2, 2, HALF])
        decayed = sb("decayed", [P, 2, HALF])
        uv = sb("uv", [P, 2, 2, HALF])
        ucopy, vterm = uv[:, 0], uv[:, 1]
        stats = sb("stats", [P, NT, 6])
        mv = sb("mv", [P, NT + L2, 2])
        rstd = sb("rstd", [P, NT + L2])
        rk = sb("rk", [P, NT * H])
        og = work[:].rearrange("p a b c -> p (a b c)")[:, 0:L2 * P]
        od = uv[:].rearrange("p a b c -> p (a b c)")[:, 0:L2 * P]
        osq = early[:, 0:L2 * P]
        rstd2 = sb("rstd2", [P, L2])

        ps = [ctx.enter_context(nc.psum_tensor(f"ps{i}", [P, 2, HALF], F32)) for i in range(4)]
        bank = [ps[i // 2][:, i % 2, :] for i in range(8)]

        s_cst, s_x, s_xf, s_wa = sem("s_const"), sem("s_x"), sem("s_xf"), sem("s_attn_weights")
        s_zero, s_xfz = sem("s_zeros"), sem("s_xf_zeroed")
        s_st, s_mv, s_sd, s_rs, s_xn = sem("s_stats"), sem("s_mv"), sem("s_std"), sem("s_rstd"), sem("s_xn")
        s_tp, s_xT = sem("s_transposed"), sem("s_xT")
        s_wt, s_wtc, s_wp, s_w = sem("s_wlow_transposed"), sem("s_wlowT"), sem("s_wproduct"), sem("s_wfo")
        s_wge = sem("s_wge")
        s_pj, s_ev, s_sq = sem("s_projected"), sem("s_evicted"), sem("s_ksq")
        s_ss, s_no, s_nm, s_rk, s_rb = sem("s_ss"), sem("s_norm"), sem("s_normmax"), sem("s_rk"), sem("s_rb")
        s_rke = sem("s_rk_spread")
        s_k, s_fk, s_fkk, s_gk = sem("s_k"), sem("s_fk"), sem("s_fkk"), sem("s_gk")
        s_c, s_gc, s_y, s_m, s_p = sem("s_c"), sem("s_gc"), sem("s_y"), sem("s_m"), sem("s_p")
        two = lambda n: [sem(f"{n}{h}") for h in (0, 1)]
        s_state, s_prod, s_red, s_term = two("s_state"), two("s_prod"), two("s_red"), two("s_term")
        s_add, s_dec, s_uc, s_bp, s_ba = two("s_add"), two("s_dec"), two("s_uc"), two("s_bp"), two("s_ba")
        s_open, s_bs, s_bc = sem("s_open"), sem("s_bsum"), sem("s_bcopy")
        s_min, s_bin = sem("s_matrices_in"), sem("s_sums_in")
        s_mout, s_bout, s_sout = sem("s_m_out"), sem("s_b_out"), sem("s_s_out")
        s_cm, s_cr, s_ca = sem("s_chain_mul"), sem("s_chain_red"), sem("s_chain_add")
        s_chout = sem("s_chain_out")
        s_vd, s_q = two("s_vd"), two("s_q")
        s_o, s_og, s_mu, s_od, s_osq, s_dw = (sem("s_o"), sem("s_og"), sem("s_mu"), sem("s_od"), sem("s_osq"),
                                              sem("s_dw"))
        s_var, s_sd2, s_rs2, s_at, s_x1 = sem("s_var"), sem("s_std2"), sem("s_rstd2"), sem("s_at"), sem("s_x1")
        s_dbg = sem("s_dbg")
        gu = steps[:].rearrange("p a b c -> p (a b c)")[:, 0:E * 2 * F]
        dw = steps[:].rearrange("p a b c -> p (a b c)")[:, E * 2 * F:E * 3 * F]
        wnat = sb("wnat", [P, 7, D])
        wT = sb("wT", [P, 6, P])
        wrT = sb("wrT", [P, E])
        state_all, decayed_all = (x[:].rearrange("p a b -> p (a b)") for x in (state, decayed))
        work_all, uv_all = (x[:].rearrange("p a b c -> p (a b c)") for x in (work, uv))
        rooms = [early[:, L2 * P:]]

        def take(n, dt=F32):
            k = next(k for k, r in enumerate(rooms) if r.shape[1] >= n)
            piece, rooms[k] = rooms[k][:, 0:n], rooms[k][:, n:]
            return piece if dt == F32 else piece.bitcast(dt)

        fb = {}
        w16, rest = work_all.shape[1] // D, OTHERS.n - work_all.shape[1] // D
        early_rows = [work_all[:, j * D:(j + 1) * D] for j in range(w16)]
        early_rows += [uv_all[:, j * D:(j + 1) * D] for j in range(rest)]
        ch_end = 2 * nm + 2 * nb + HD * (C + 1) * 4 + 4 * HD * HD + 4 * HD
        assert ch_end + OTHERS.n * D <= L2 * COLS
        late = early[:, ch_end:ch_end + OTHERS.n * D]
        for t in (MIXED, OTHERS):
            q = {}
            fb[t.name] = q
            if t is OTHERS:
                q["back"] = take(t.n * D)
                rooms = [uv_all[:, rest * D:], state_all, decayed_all]
                q["rows"] = q["scaled"] = early_rows
                q["shared"] = [late[:, j * D:(j + 1) * D] for j in range(t.n)]
                q["lg"] = rk[:, 0:t.n * E]
            else:
                rows, scaled = take(t.n * D), take(t.n * D)
                q["rows"] = q["shared"] = [rows[:, j * D:(j + 1) * D] for j in range(t.n)]
                q["scaled"] = [scaled[:, j * D:(j + 1) * D] for j in range(t.n)]
                q["back"] = rows
                q["lg"] = take(t.n * E)
            q["r_te"], q["oh"] = take(t.tiles * E), take(t.n * E)
            for name in ("r_tot", "r_inc", "r_a", "r_keep"):
                q[name] = take(t.n * E)
            for name in ("r_nt", "r_ti", "r_ts", "r_one"):
                q[name] = take(E)
            q["r_tf"] = take(t.tiles)
            for name in ("score", "mx", "mw", "slot"):
                q[name] = take(t.n)
            q["idx"] = sb("slots_" + t.name, [P, t.n], I32)
            q["stats"] = stats[:, 0:t.n]
            q["mv"] = sb("mv_" + t.name, [P, t.n, 2])
            q["rstd"] = sb("rstd_" + t.name, [P, t.n])
            q["te"] = sb("te_" + t.name, [1, t.tiles], I32)
        fxT_route = {OTHERS.name: gateT[:, 0:4 * P], MIXED.name: work_all[:, 0:4 * P]}
        fxT, fsg = work_all[:, 0:4 * P], work_all[:, 4 * P:8 * P]
        fhT = work_all[:, 8 * P:16 * P].rearrange("p (k x) -> p k x", k=2)
        left = steps[:].rearrange("p a b c -> p (a b c)")[:, E * 3 * F:L1 * 5 * P]
        assert 4 * U * P <= left.shape[1]
        e_in, e_xT = (left[:, k * 2 * U * P:(k + 1) * 2 * U * P].rearrange("p (b u d) -> p b u d", b=2, u=U)
                      for k in (0, 1))
        e_y = sb("e_y", [P, 2, U, P])
        e_sg = rk[:].rearrange("p (u d) -> p u d", u=U)
        e_h, e_hT = sb("e_h", [P, U, F]), sb("e_hT", [P, U, F])
        b_gu = [bank[4], bank[5]]
        b_x, b_y, b_h = bank[6][:, 0:U * P], bank[6][:, U * P:], bank[7]
        b_gate, b_up, b_xT, b_tok = (bank[0], bank[2]), (bank[1], bank[3]), bank[6], bank[7]
        b_rank = {OTHERS.name: (bank[6], bank[7]), MIXED.name: (bank[4], bank[5])}

        s_wf, s_wft, s_wfT = sem("s_ffn_weights"), sem("s_ffn_w_transposed"), sem("s_ffn_wT")
        s_we = sem("s_expert_weights")
        s_xz = sem("s_slots_zeroed")
        s_fst, s_fmv, s_fsd, s_frs, s_fn = (sem("s_f_stats"), sem("s_f_mv"), sem("s_f_std"), sem("s_f_rstd"),
                                            sem("s_f_normed"))
        s_lt, s_lx, s_lg, s_flc = sem("s_r_transposed"), sem("s_r_xT"), sem("s_logits"), sem("s_logits_out")
        s_late = sem("s_rows_again")
        s_ft, s_fx, s_fgu = sem("s_f_transposed"), sem("s_f_xT"), sem("s_f_gate_up")
        s_fsg, s_fh, s_fy, s_fa = sem("s_f_silu"), sem("s_f_h"), sem("s_f_y"), sem("s_f_added")
        s_link = sem("s_route_link")
        s_oh, s_rank, s_mx, s_score = sem("s_onehot"), sem("s_rank"), sem("s_max"), sem("s_score")
        s_idx, s_te, s_sc, s_scat = sem("s_slots"), sem("s_tile_experts"), sem("s_scaled"), {t: sem("s_scattered_" + t) for t in fb}
        s_ei, s_et, s_ex, s_eg, s_es = (two("s_e_in"), sem("s_e_transposed"), sem("s_e_xT"), sem("s_e_gate_up"),
                                        sem("s_e_silu"))
        s_eh, s_eht, s_ehc, s_ey, s_eo, s_ew = (sem("s_e_h"), sem("s_e_h_transposed"), sem("s_e_hT"), sem("s_e_y"),
                                                sem("s_e_out"), two("s_e_written"))
        s_gat, s_fin, s_out = {t: sem("s_gathered_" + t) for t in fb}, sem("s_final"), sem("s_out")
        SETS = (OTHERS, MIXED)
        GB = {OTHERS.name: 0, MIXED.name: len(OTHERS.groups)}
        TB = {OTHERS.name: 0, MIXED.name: OTHERS.n}
        GA = {OTHERS.name: 0, MIXED.name: len(OTHERS.groups)}
        both = OTHERS.tiles // U
        BESIDE = both - (L2 - 2)
        RUNS = [Run(OTHERS, 0, BESIDE, 0, (0, 0)),
                Run(OTHERS, BESIDE, both - BESIDE, BESIDE, ((BESIDE + 1) // 2, BESIDE // 2)),
                Run(MIXED, 0, MIXED.tiles // U, both, ((BESIDE + 1) // 2 + both - BESIDE, BESIDE // 2))]
        block = ctx.enter_context(nc.Block())

        jobs = []
        for lo, hi in GROUPS:
            jobs += [(wqkv[:, 1], lo, hi, K, ACT.Silu), (wqkv[:, 2], lo, hi, VV, ACT.Silu)]
        for lo, hi in QGROUPS:
            jobs.append((wqkv[:, 0], L1 + lo, L1 + hi, None, ACT.Silu))
        for lo, hi in GROUPS:
            jobs += [(wfo[:, 0], lo, hi, FF, ACT.Sigmoid), (wge[:], lo, hi, Y, ACT.Sigmoid)]
        for lo, hi in QGROUPS:
            jobs.append((wfo[:, 1], lo, hi, None, ACT.Sigmoid))
        NJ = len(jobs)
        BEGIN, SHARED_EVERY, PAIRS_FROM, PAIR_EVERY = 5, 5, 32, 3
        NSILU = 2 * NG + NQ
        NOG = len(OTHERS.groups)
        ROUTE_AT = NSILU + 1
        RANK_AT = ROUTE_AT + NOG + 4
        assert RANK_AT < NJ - NQ
        NTP = NG + NQ

        def slot(lo, hi, k):
            return steps[:, lo:hi, k, :]

        def cols(ap, lo, hi):
            return ap[:, lo * P:hi * P].rearrange("p (s x) -> p s x", x=P)

        def psum(b, lo, hi):
            return bank[b][:, 0:(hi - lo) * P].rearrange("p (s x) -> p s x", x=P)

        def rows_of(ap, t, lo, hi):
            if t is MIXED:
                return ap[:, 3 * lo:3 * hi - 2:3, :]
            return ap[:, 3 * lo // 2:3 * hi // 2, :].rearrange("p (r q) d -> p r q d", q=3)[:, :, 1:3, :]

        def tiles_of(ap, t):
            if t is MIXED:
                return ap.rearrange("p (r d) -> p r d", d=D)
            return ap.rearrange("p (r q d) -> p r q d", q=2, d=D)

        def over_pairs(engine, run, pair):
            n = run.n
            looped = (n - 3) // 2 * 2
            with engine.Fori(0, looped // 2) as half:
                i = half * 2
                for k in (0, 1):
                    pair(i, k, 3)
            for k in range(looped, n):
                pair(0, k, n - 1 - k)

        REGION = ((0, L1), (L1, L2))

        def per_col(tile, k, n, h, w):
            x = slice(h * P // 2, (h + 1) * P // 2) if w == HD else slice(0, P)
            ap = steps[:, bass.ds(tile, 1), k:k + n, x].rearrange("p t e x -> p (t e) x")
            return ap.unsqueeze(3).to_broadcast([P, n, P * 4 // w, w])

        def wide(ap, w):
            return ap.rearrange("p (e x w) -> p e x w", e=1, w=w)

        @block.sync
        def _(sp):
            for b in range(B):
                sp.dma_start(xr[b * C:(b + 1) * C, 0:L1, :],
                             a["x"][b, 0:T1, :].rearrange("(c s) d -> c s d", s=L1)).then_inc(s_x, 16)
                sp.dma_start(xr[b * C:(b + 1) * C, L1:, :],
                             a["x"][b, T1:, :].rearrange("(c s) d -> c s d", s=L2)).then_inc(s_x, 16)
            sp.wait_ge(s_zero, 2)
            for t in SETS:
                sp.dma_start(xs[t.name].rearrange("(m p) d -> p m d", p=P),
                             zeros[:, 0:D].unsqueeze(1).to_broadcast([P, t.tiles + 1, D])).then_inc(s_xz, 16)
                sp.dma_start(ys[t.name][t.tiles * P:, :], zeros[:, 0:D]).then_inc(s_xz, 16)
            sp.wait_ge(s_xfz, 1)
            n = 3 * SKIP
            for b in range(B):
                g0 = b * C
                sp.dma_start(xf[g0:g0 + 1, n:, :], a["x"][b:b + 1, 0:ROWS - n, :]).then_inc(s_xf, 16)
                sp.dma_start(xf[g0 + 1:g0 + C - 1, :, :],
                             a["x"][b, ROWS - n:(C - 1) * ROWS - n, :].rearrange("(g r) d -> g r d", r=ROWS)
                             ).then_inc(s_xf, 16)
                last = N - ((C - 1) * ROWS - n)
                sp.dma_start(xf[g0 + C - 1:g0 + C, 0:last, :], a["x"][b:b + 1, N - last:, :]).then_inc(s_xf, 16)
            def routed(t):
                return (xs[t.name].rearrange("(m p) d -> p m d", p=P), ys[t.name].rearrange("(m p) d -> p m d", p=P))

            def pairs_in_out(run):
                x_in, y_out = routed(run.t)

                def load(i, k):
                    if type(i) is not int or i + k >= 2:
                        sp.wait_ge(s_et, i + (k + run.g0 - 1))
                    elif run.g0:
                        sp.wait_ge(s_et, run.g0)
                    sp.dma_start(e_in[:, k % 2], x_in[:, bass.ds(i * U + (k + run.first) * U, U), :]
                                 ).then_inc(s_ei[k % 2], 16)

                def pair(i, k, ahead):
                    if ahead > 2:
                        load(i, k + 3)
                    sp.wait_ge(s_eo, i + (k + run.g0 + 2))
                    sp.dma_start(y_out[:, bass.ds(i * U + (k + run.first) * U, U), :], e_y[:, k % 2]
                                 ).then_inc(s_ew[k % 2], 16)

                for k in range(3):
                    load(0, k)
                over_pairs(sp, run, pair)

            for r in (0, 1):
                if r:
                    for h in (0, 1):
                        sp.wait_ge(s_state[h], L1 + 1)
                        sp.wait_ge(s_bp[h], L1 + 1)
                    sp.dma_start(gu.rearrange("p (e f) -> p e f", e=E), a["gate_up_proj"].rearrange("e p f -> p e f")
                                 ).then_inc(s_we, 16)
                    for k in (0, 1):
                        sp.dma_start(dw.rearrange("p (e k d) -> p e k d", e=E, k=2)[:, :, k],
                                     a["down_proj"][:, k * P:(k + 1) * P, :].rearrange("e p d -> p e d")
                                     ).then_inc(s_we, 16)
                for h in (0, 1):
                    sp.wait_ge(s_state[h], sum(n + 1 for _, n in REGION[:r + 1]))
                sp.dma_start(scr["m"][r], state[:].rearrange("p a b -> p (a b)")).then_inc(s_mout, 16)
                sp.wait_ge(s_mout, 16 * (r + 1))
                for vh in (0, 1):
                    for b in range(B):
                        lanes = slice(vh * 64 + b * H, vh * 64 + (b + 1) * H)
                        sp.dma_start(ch_m[r][lanes].rearrange("h j c i -> h j (c i)"),
                                     scr["m"][r][:, b * 256:(b + 1) * 256].rearrange("(h j) x -> h j x", j=HD)
                                     ).then_inc(s_min, 16)
                sp.wait_ge(s_bc, r + 1)
                sp.dma_start(scr["b"][r], ucopy.rearrange("p a b -> p (a b)")).then_inc(s_bout, 16)
                sp.wait_ge(s_bout, 16 * (r + 1))
                for vh in (0, 1):
                    for b in range(B):
                        lanes = slice(vh * 64 + b * H, vh * 64 + (b + 1) * H)
                        sp.dma_start(ch_b[r][lanes].rearrange("h v c i -> h v (c i)"),
                                     scr["b"][r][:, b * 256:(b + 1) * 256].rearrange("(h v) x -> h v x", v=HD)
                                     [:, vh * 4:vh * 4 + 4, :]).then_inc(s_bin, 16)
            for k in (0, 1):
                sp.sem_inc(s_ew[k], 16)
            sp.wait_ge(s_scat[OTHERS.name], 16 * OTHERS.n)
            pairs_in_out(RUNS[0])
            sp.wait_ge(s_ca, 2 * C + 1)
            sp.dma_start(scr["s"].rearrange("(l i) x -> l i x", i=HD),
                         ch_s[:, :, 0:C, :].rearrange("l i c v -> l i (c v)")).then_inc(s_sout, 16)
            sp.wait_ge(s_sout, 16)
            for vh in (0, 1):
                for b in range(B):
                    rows = (vh * B + b) * P
                    sp.dma_start(state[:, vh, b * C * 4:(b + 1) * C * 4],
                                 scr["s"][rows:rows + P, :]).then_inc(s_chout, 16)
            run = RUNS[1]
            x_in, y_out = routed(run.t)

            def load_one(i):
                sp.wait_ge(s_et, i + run.g0)
                sp.dma_start(e_in[:, 0], x_in[:, bass.ds((i + run.first) * U, U), :]).then_inc(s_ei[0], 16)

            def store_one(i):
                sp.wait_ge(s_eo, i + (run.g0 + 2))
                sp.dma_start(y_out[:, bass.ds((i + run.first) * U, U), :], e_y[:, 0]).then_inc(s_ew[0], 16)

            load_one(0)
            with sp.Fori(1, run.n) as i:
                load_one(i)
                store_one(i - 1)
            store_one(run.n - 1)
            sp.wait_ge(s_scat[MIXED.name], 16 * MIXED.n)
            pairs_in_out(RUNS[2])
            n = 3 * SKIP
            last = N - ((C - 1) * ROWS - n)
            for t in SETS:
                sp.wait_ge(s_fin, 1 + (t is MIXED))
                for b in range(B):
                    g0 = b * C
                    if t is OTHERS:
                        sp.dma_start(out[b:b + 1, 1:ROWS - n, :], xf[g0:g0 + 1, n + 1:, :]).then_inc(s_out, 16)
                        for q in (1, 2):
                            sp.dma_start(out[b, ROWS - n + q:(C - 1) * ROWS - n:3, :].rearrange("(g r) d -> g r d", r=L2),
                                         xf[g0 + 1:g0 + C - 1, q::3, :]).then_inc(s_out, 16)
                            sp.dma_start(out[b:b + 1, N - last + q:N:3, :],
                                         xf[g0 + C - 1:g0 + C, q:last:3, :]).then_inc(s_out, 16)
                    else:
                        sp.dma_start(out[b:b + 1, 0:1, :], xf[g0:g0 + 1, n:n + 1, :]).then_inc(s_out, 16)
                        sp.dma_start(out[b, ROWS - n:(C - 1) * ROWS - n:3, :].rearrange("(g r) d -> g r d", r=L2),
                                     xf[g0 + 1:g0 + C - 1, 0::3, :]).then_inc(s_out, 16)
                        sp.dma_start(out[b:b + 1, N - last:N:3, :], xf[g0 + C - 1:g0 + C, 0:last:3, :]
                                     ).then_inc(s_out, 16)
            sp.wait_ge(s_out, 16 * 8 * B)
            if debug is not None:
                sp.wait_ge(s_x1, L2)
                sp.dma_start(debug["steps"], steps[:].rearrange("p a b c -> p (a b c)")).then_inc(s_dbg, 16)
                sp.dma_start(debug["xf"], xf[:].rearrange("p a b -> p (a b)")).then_inc(s_dbg, 16)
                sp.dma_start(debug["gate"], gateT[:]).then_inc(s_dbg, 16)
                sp.dma_start(debug["state"], state[:].rearrange("p a b -> p (a b)")).then_inc(s_dbg, 16)
                sp.wait_ge(s_dbg, 64)

        @block.scalar
        def _(act):
            act.dma_start(cst[:], a["const"]).then_inc(s_cst, 16)
            for dst, src in ((wqkv[:, 0], "Wq"), (wqkv[:, 1], "Wk"), (wqkv[:, 2], "Wv"), (wgs[:], "Wg"),
                             (wlow[:, 0], "Wf1"), (wlow[:, 1], "Wo1"), (wup[:, 0], "Wf2"), (wup[:, 1], "Wo2"),
                             (wout[:], "Wout")):
                act.dma_start(dst, a[src]).then_inc(s_wa, 16)
            act.dma_start(lnw[:], a["ln_w"].rearrange("(p o) -> p o", o=1)).then_inc(s_wa, 16)
            for k, name in ((0, "w_gate"), (2, "w_up")):
                act.dma_start(wnat[:, k:k + 2], a[name].rearrange("(k p) d -> p k d", p=P)).then_inc(s_wf, 16)
            for k in (0, 1):
                act.dma_start(wnat[:, 4 + k], a["w_down"][:, k * P:(k + 1) * P]).then_inc(s_wf, 16)
            act.dma_start(wnat[0:E, 6], a["w_router"]).then_inc(s_wf, 16)
            act.wait_ge(s_mv, NT)
            act.wait_ge(s_zero, 2)
            S.activation(rstd[:, 0:NT], mv[:, 0:NT, 1], ACT.Sqrt, bias=eps[:]).then_inc(s_sd, 1)
            act.wait_ge(s_mv, NT + L2)
            S.activation(rstd[:, NT:], mv[:, NT:, 1], ACT.Sqrt, bias=eps[:]).then_inc(s_sd, 1)
            act.wait_ge(s_wt, 1)
            S.activation(wlowT[:], bank[7][0:HD, 0:2 * P].rearrange("p (a b) -> p a b", a=2), ACT.Copy).then_inc(s_wtc, 1)
            act.wait_ge(s_wp, 1)
            S.activation(wfo[:], bank[7][:, 0:2 * D].rearrange("p (a b) -> p a b", a=2), ACT.Copy).then_inc(s_w, 1)
            act.wait_ge(s_wft, 1)
            S.activation(wT[:, 0:4], bank[6].rearrange("p (k x) -> p k x", k=4), ACT.Copy).then_inc(s_wfT, 1)
            S.activation(wT[:, 4:6], bank[7][:, 0:2 * P].rearrange("p (k x) -> p k x", k=2), ACT.Copy).then_inc(s_wfT, 1)
            S.activation(wrT[:], bank[7][:, 2 * P:2 * P + E], ACT.Copy).then_inc(s_wfT, 1)
            for n, (lo, hi) in enumerate(GROUPS + QGROUPS):
                act.wait_ge(s_tp, n + 1)
                dst = xnT if n < NG else xaT
                S.activation(cols(dst, lo, hi), psum(n % 2, lo, hi), ACT.Copy).then_inc(s_xT, 1)
            def route_xT(t, g):
                lo, hi = t.groups[g]
                act.wait_ge(s_lt, GB[t.name] + g + 1)
                S.activation(fxT_route[t.name][:, 0:(hi - lo) * P], b_xT[:, 0:(hi - lo) * P], ACT.Copy
                             ).then_inc(s_lx, 1)

            def logits_out(t):
                act.wait_ge(s_lg, 1 + (t is MIXED))
                S.activation(fb[t.name]["lg"], b_tok[:, 0:t.n * E], ACT.Copy).then_inc(s_flc, 1)

            def score(t):
                act.wait_ge(s_mx, 1 + (t is MIXED))
                S.activation(fb[t.name]["score"], fb[t.name]["mx"], ACT.Sigmoid).then_inc(s_score, 1)

            def row_std(t):
                q = fb[t.name]
                act.wait_ge(s_fmv, TB[t.name] + t.n)
                S.activation(q["rstd"][:], q["mv"][:, :, 1], ACT.Sqrt, bias=eps[:]).then_inc(s_fsd, 1)

            for j, (_, lo, hi, k, func) in enumerate(jobs):
                if j == NSILU:
                    row_std(OTHERS)
                if ROUTE_AT < j <= ROUTE_AT + NOG:
                    route_xT(OTHERS, j - ROUTE_AT - 1)
                if j == ROUTE_AT + NOG + 2:
                    logits_out(OTHERS)
                if j == ROUTE_AT + NOG + 4:
                    score(OTHERS)
                if j == NJ - NQ:
                    act.wait_ge(s_idx, 1)
                act.wait_ge(s_pj, j + 1)
                if k is None:
                    dst = cols(qT, lo - L1, hi - L1) if func == ACT.Silu else cols(gateT, lo, hi)
                else:
                    dst = slot(lo, hi, k)
                S.activation(dst, psum(2 + j % 4, lo, hi), func).then_inc(s_ev, 1)
                if k == K:
                    act.wait_ge(s_ev, j + 1)
                    S.activation(slot(lo, hi, PP), slot(lo, hi, K), ACT.Square).then_inc(s_sq, 1)
            act.wait_ge(s_ss, 1)
            S.activation(rk[:], bank[6], ACT.Sqrt).then_inc(s_no, 1)
            act.wait_ge(s_rk, 1)
            for g, (lo, hi) in enumerate(GROUPS):
                S.activation(xr[:, lo:hi].rearrange("p s (h i) -> p (s h) i", i=HD),
                             rk[:, lo * H:hi * H].unsqueeze(2).to_broadcast([P, (hi - lo) * H, HD]),
                             ACT.Copy).then_inc(s_rke, 1)
            act.sem_inc(s_uc[0], 1)
            act.sem_inc(s_uc[1], 1)
            for r, (_, n) in enumerate(REGION):
                base = r * L1
                with act.Fori(0, n) as i:
                    for h in (0, 1):
                        act.wait_ge(s_term[h], i + (base + 1))
                        act.wait_ge(s_bp[h], i + (base + 1))
                        S.activation(ucopy[:, h], bank[2 * h + 1], ACT.Copy).then_inc(s_uc[h], 1)
                for h in (0, 1):
                    act.wait_ge(s_bp[h], base + n + 1)
                act.wait_ge(s_bs, 2 * r + 2)
                S.activation(ucopy, ps[2][:], ACT.Copy).then_inc(s_bc, 1)
                if r == 0:
                    act.wait_ge(s_bin, 128)
            act.wait_ge(s_bin, 256)
            def shared(t):
                for g, (lo, hi) in enumerate(t.groups):
                    n, w = GA[t.name] + g, (hi - lo) * P
                    act.wait_ge(s_ft, n + 1)
                    S.activation(fxT[:, 0:w], b_xT[:, 0:w], ACT.Copy).then_inc(s_fx, 1)
                    for k in (0, 1):
                        act.wait_ge(s_fgu, 2 * n + k + 1)
                        if n or k:
                            act.wait_ge(s_fh, 2 * n + k)
                        S.activation(fsg[:, 0:w], b_gate[k][:, 0:w], ACT.Silu).then_inc(s_fsg, 1)

            def copy_x(run, i, k, b):
                act.wait_ge(s_et, i + (k + run.g0 + 1))
                S.activation(e_xT[:, b], b_x.rearrange("p (u d) -> p u d", u=U), ACT.Copy).then_inc(s_ex, 1)

            def silu(run, i, k):
                for u in range(U):
                    act.wait_ge(s_eg, i * U + ((k + run.g0) * U + u + 1))
                    S.activation(e_sg[:, u], b_gu[u][:, 0:F], ACT.Silu).then_inc(s_es, 1)

            def copy_h(run, i, k):
                act.wait_ge(s_eht, i + (k + run.g0 + 1))
                S.activation(e_hT[:], b_h.rearrange("p (u x) -> p u x", u=U), ACT.Copy).then_inc(s_ehc, 1)

            def copy_y(run, i, k, b, written):
                act.wait_ge(s_ey, i + (k + run.g0 + 1))
                act.wait_ge(s_ew[b], written)
                S.activation(e_y[:, b], b_y.rearrange("p (u d) -> p u d", u=U), ACT.Copy).then_inc(s_eo, 1)

            def pairs(run):
                def pair(i, k, ahead):
                    if ahead > 1:
                        copy_x(run, i, k + 2, k % 2)
                    copy_h(run, i, k)
                    if ahead:
                        silu(run, i, k + 1)
                    copy_y(run, i, k, k % 2, i * 8 + 16 * (k // 2 + 1 + run.base[k % 2]))

                copy_x(run, 0, 0, 0)
                copy_x(run, 0, 1, 1)
                silu(run, 0, 0)
                over_pairs(act, run, pair)

            act.sem_inc(s_eo, 1)
            shared(OTHERS)
            pairs(RUNS[0])
            turn = act.alloc_register("turn_act")
            run = RUNS[1]

            def v_term(i, h):
                act.wait_ge(s_red[h], i + NT)
                tile = i + L1
                if h and type(i) is not int:
                    act.reg_add(turn, turn, 1)
                    tile = act.snap(turn, min_val=L1, max_val=NT - 1)
                for v in range(4):
                    ins = S.activation(vterm[:, h].rearrange("p (x v) -> p x v", v=4)[:, :, v],
                                       steps[:, bass.ds(tile, 1), VV, :].rearrange("p a x -> p (a x)"),
                                       ACT.Copy, scale=c["diag8"][:, 4 * h + v:4 * h + v + 1])
                ins.then_inc(s_vd[h], 1)

            def step(i, begins, ends):
                v_term(i, 0)
                if ends:
                    silu(run, i, -2)
                v_term(i, 1)
                if begins:
                    copy_x(run, i, -1, 0)
                if ends:
                    copy_h(run, i, -2)
                    copy_y(run, i, -2, 0, i * 16 + 16 * (run.base[0] - 1))

            step(0, False, False)
            step(1, True, False)
            act.reg_mov(turn, L1 + 1)
            with act.Fori(2, L2 - 1) as i:
                step(i, True, True)
            step(L2 - 1, False, True)
            for g, (lo, hi) in enumerate(QGROUPS):
                act.wait_ge(s_od, g + 1)
                S.activation(osq[:, lo * P:hi * P], od[:, lo * P:hi * P], ACT.Square).then_inc(s_osq, 1)
            act.wait_ge(s_var, 1)
            S.activation(rstd2[:], bank[3][:, 0:L2], ACT.Sqrt, bias=eps[:]).then_inc(s_sd2, 1)

            row_std(MIXED)
            for g in range(len(MIXED.groups)):
                route_xT(MIXED, g)
            logits_out(MIXED)
            score(MIXED)
            shared(MIXED)
            pairs(RUNS[2])

        def pool_tt(dst, src, tile, k, h, w):
            tile = G.snap(tile)
            return G.tensor_tensor(wide(dst, w), wide(src, w), per_col(tile, k, 1, h, w), ALU.mult)

        @block.gpsimd
        def _(pool):
            G.memset(zeros[:], 0.0).then_inc(s_zero, 1)
            G.memset(eps[:], LN_EPS).then_inc(s_zero, 1)
            G.memset(xf[:], 0.0).then_inc(s_xfz, 1)
            pool.wait_ge(s_wa, 160)
            G.tensor_copy(wge[:].rearrange("p (h i) -> p h i", i=HD),
                          wgs[:].unsqueeze(2).to_broadcast([P, H, HD])).then_inc(s_wge, 1)
            def scatter(t):
                q = fb[t.name]
                pool.wait_ge(s_xz, 64)
                pool.wait_ge(s_idx, 1 + (t is MIXED))
                for j in range(t.n):
                    pool.wait_ge(s_sc, TB[t.name] + j + 1)
                    G.indirect_dma_start(xs[t.name], bass.IndirectOffsetOnAxis(ap=q["idx"][:, j:j + 1].bitcast(U32), axis=0),
                                         q["scaled"][j], None).then_inc(s_scat[t.name], 16)

            def gather(t, pairs):
                q = fb[t.name]
                for k in (0, 1):
                    pool.wait_ge(s_ew[k], 16 * (pairs[k] + 1))
                for j in range(t.n):
                    G.indirect_dma_start(q["back"][:, j * D:(j + 1) * D], None, ys[t.name],
                                         bass.IndirectOffsetOnAxis(ap=q["idx"][:, j:j + 1].bitcast(U32), axis=0)
                                         ).then_inc(s_gat[t.name], 16)

            scatter(OTHERS)
            pool.wait_ge(s_scat[OTHERS.name], 16 * OTHERS.n)
            fk = lambda g, n: work[:, 0, g % 2, 0:n * P].rearrange("p (s x) -> p s x", x=P)
            fkk = lambda g, n: work[:, 1, g % 2, 0:n * P].rearrange("p (s x) -> p s x", x=P)
            gk = lambda g, n: decayed[:, g % 2, 0:n * P].rearrange("p (s x) -> p s x", x=P)
            pool.wait_ge(s_ev, NJ)

            def last_p(g):
                lo, hi = GROUPS[g]
                pool.wait_ge(s_m, g + 1)
                G.tensor_tensor(slot(lo, hi, PP), slot(lo, hi, PP), slot(lo, hi, Y), ALU.add).then_inc(s_p, 1)

            for g, (lo, hi) in enumerate(GROUPS):
                pool.wait_ge(s_k, g + 1)
                if g >= 2:
                    pool.wait_ge(s_m, g - 1)
                    pool.wait_ge(s_c, g - 1)
                G.tensor_tensor(fk(g, hi - lo), slot(lo, hi, FF), slot(lo, hi, K), ALU.mult).then_inc(s_fk, 1)
                pool.wait_ge(s_fk, g + 1)
                G.tensor_tensor(fkk(g, hi - lo), fk(g, hi - lo), slot(lo, hi, K), ALU.mult).then_inc(s_fkk, 1)
                G.tensor_tensor(gk(g, hi - lo), slot(lo, hi, Y), slot(lo, hi, K), ALU.mult).then_inc(s_gk, 1)
                if g:
                    last_p(g - 1)
            last_p(NG - 1)
            for h in (0, 1):
                pool.sem_inc(s_bp[h], 1)
            for r, (_, n) in enumerate(REGION):
                base = r * L1
                last = base + n - 1

                def decay(h, tile, ready):
                    pool.wait_ge(s_state[h], ready)
                    pool_tt(decayed[:, h], state[:, h], tile, FF, h, HD).then_inc(s_dec[h], 1)

                def v_times_u(h, tile, n):
                    pool.wait_ge(s_uc[h], n + 1)
                    pool.wait_ge(s_ba[h], n)
                    pool_tt(vterm[:, h], ucopy[:, h], tile, VV, h, HD).then_inc(s_bp[h], 1)

                for h in (0, 1):
                    decay(h, last, base + r + 1)
                with pool.Fori(1, n) as i:
                    for h in (0, 1):
                        decay(h, (i * -1) + last, i + (base + r + 1))
                        v_times_u(h, (i * -1) + (last + 1), i + base)
                for h in (0, 1):
                    v_times_u(h, base, base + n)
            first = NT + 2
            q = fb[OTHERS.name]
            for j, row in enumerate(OTHERS.rows):
                G.tensor_scalar(q["shared"][j], xf[:, row], q["mv"][:, j, 0:1], q["rstd"][:, j:j + 1], ALU.subtract,
                                ALU.mult).then_inc(s_late, 1)
            turn = pool.alloc_register("turn_pool")
            for h in (0, 1):
                pool.sem_inc(s_q[h], 1)
            pool.reg_mov(turn, L1 - 1)
            with pool.Fori(0, L2) as i:
                tile = i + L1
                for h in (0, 1):
                    pool.wait_ge(s_state[h], i + (first + 1))
                    if h:
                        pool.reg_add(turn, turn, 1)
                        tile = pool.snap(turn, min_val=L1, max_val=NT - 1)
                    pool_tt(decayed[:, h], state[:, h], tile, FF, h, 4).then_inc(s_dec[h], 1)
                for h in (0, 1):
                    pool.wait_ge(s_state[h], i + (first + 2))
                    G.tensor_tensor(qs[:, bass.ds(i, 1), h].rearrange("p s x v -> p (s x) v"),
                                    state[:, h].rearrange("p (x v) -> p x v", v=4),
                                    qT[:, bass.ds(G.snap(i * P), P)].unsqueeze(2).to_broadcast([P, P, 4]),
                                    ALU.mult).then_inc(s_q[h], 1)
            pool.wait_ge(s_o, NQ)
            gather(OTHERS, RUNS[2].base)
            scatter(MIXED)
            pool.wait_ge(s_fa, GA[MIXED.name] + len(MIXED.groups))
            m = RUNS[2].n
            gather(MIXED, (RUNS[2].base[0] + (m + 1) // 2, RUNS[2].base[1] + m // 2))

        @block.vector
        def _(dve):
            chained = [0]

            def link(ins):
                chained[0] += 1
                ins.then_inc(s_link, 1)
                dve.wait_ge(s_link, chained[0])

            def row_stats(t):
                q, t0 = fb[t.name], TB[t.name]
                if t is MIXED:
                    dve.wait_ge(s_x1, L2)
                for j, row in enumerate(t.rows):
                    V.bn_stats(q["stats"][:, j], xf[:, row]).then_inc(s_fst, 1)
                for j in range(t.n):
                    dve.wait_ge(s_fst, t0 + j + 1)
                    V.bn_aggr(q["mv"][:, j], q["stats"][:, j]).then_inc(s_fmv, 1)

            def row_norm(t):
                q, m = fb[t.name], t is MIXED
                dve.wait_ge(s_fsd, 1 + m)
                V.reciprocal(q["rstd"][:], q["rstd"][:]).then_inc(s_frs, 1)
                dve.wait_ge(s_frs, 1 + m)
                for j, row in enumerate(t.rows):
                    V.tensor_scalar(q["rows"][j], xf[:, row], q["mv"][:, j, 0:1], q["rstd"][:, j:j + 1], ALU.subtract,
                                    ALU.mult).then_inc(s_fn, 1)

            def route(t):
                q, m = fb[t.name], t is MIXED
                dve.wait_ge(s_flc, 1 + m)
                ne = lambda ap: ap.rearrange("p (n e) -> p n e", e=E)
                en = lambda ap: ap.rearrange("p (e n) -> p e n", e=E)
                lg, oh = ne(q["lg"]), ne(q["oh"])
                r_tot, r_inc, r_a, r_keep = (q[k] for k in ("r_tot", "r_inc", "r_a", "r_keep"))
                r_nt, r_ti, r_ts, r_one = (q[k] for k in ("r_nt", "r_ti", "r_ts", "r_one"))
                ranks, totals = b_rank[t.name]
                full, w = [P, t.n, E], t.n * E
                V.tensor_reduce(q["mx"], lg, AX.X, ALU.max).then_inc(s_mx, 1)
                dve.wait_ge(s_mx, 1 + m)
                link(V.tensor_tensor(oh, lg, q["mx"].unsqueeze(2).to_broadcast(full), ALU.is_equal))
                prefer = c["prefer"].unsqueeze(1).to_broadcast(full)
                link(V.tensor_tensor(oh, oh, prefer, ALU.mult))
                link(V.tensor_reduce(q["mw"], oh, AX.X, ALU.max))
                link(V.tensor_tensor(oh, prefer, q["mw"].unsqueeze(2).to_broadcast(full), ALU.is_equal))
                V.tensor_tensor(oh, oh, c["valid_" + t.name].unsqueeze(2).to_broadcast(full), ALU.mult).then_inc(s_oh, 1)
                V.memset(r_one, 1.0).then_inc(s_link, 1)
                V.memset(r_keep, 1.0).then_inc(s_link, 1)
                chained[0] += 2
                dve.wait_ge(s_link, chained[0])
                link(V.memset(en(r_keep)[:, :, 0:1], 0.0))
                dve.wait_ge(s_rank, 1 + m)
                link(V.tensor_copy(en(r_tot), totals[:, 0:w].rearrange("p (n e) -> p e n", e=E)))
                link(V.tensor_tensor_scan(r_inc, r_keep, r_tot, 0.0, ALU.mult, ALU.add))
                link(V.tensor_tensor(en(r_a), c["steps128"][:, 0:t.n].unsqueeze(1).to_broadcast([P, E, t.n]),
                                     en(r_inc)[:, :, t.n - 1:t.n].to_broadcast([P, E, t.n]), ALU.is_lt))
                link(V.tensor_reduce(r_nt, en(r_a), AX.X, ALU.add))
                link(V.tensor_tensor_scan(r_ti, r_one, r_nt, 0.0, ALU.mult, ALU.add))
                link(V.tensor_tensor(r_ts, r_ti, r_nt, ALU.subtract))
                link(V.tensor_tensor(r_inc, r_inc, r_tot, ALU.subtract))
                link(V.scalar_tensor_tensor(en(r_inc), r_ts.unsqueeze(2).to_broadcast([P, E, t.n]), float(P), en(r_inc),
                                            ALU.mult, ALU.add))
                link(V.tensor_tensor(ne(r_a), ranks[:, 0:w].rearrange("p (n e) -> p n e", e=E),
                                     en(r_inc).rearrange("p e n -> p n e"), ALU.add))
                link(V.tensor_tensor(ne(r_a), ne(r_a), oh, ALU.mult))
                link(V.tensor_reduce(q["slot"], ne(r_a), AX.X, ALU.add))
                V.tensor_tensor(q["idx"][:], q["slot"], c["spare_" + t.name], ALU.add).then_inc(s_idx, 1)
                dve.wait_ge(s_score, 1 + m)
                for j in range(t.n):
                    V.tensor_scalar(q["scaled"][j], q["rows"][j], q["score"][:, j:j + 1], None, ALU.mult
                                    ).then_inc(s_sc, 1)
                te = q["r_te"][0:1].rearrange("p (m e) -> p m e", e=E)
                link(V.tensor_tensor(te, r_ti[0:1].unsqueeze(1).to_broadcast([1, t.tiles, E]),
                                     c["tileno"][0:1, 0:t.tiles].unsqueeze(2).to_broadcast([1, t.tiles, E]), ALU.is_le))
                link(V.tensor_reduce(q["r_tf"][0:1], te, AX.X, ALU.add))
                V.tensor_scalar(q["te"][:], q["r_tf"][0:1], float(E - 1), None, ALU.min).then_inc(s_te, 1)

            def shared_h(t, g, k):
                lo, hi = t.groups[g]
                n, w = GA[t.name] + g, (hi - lo) * P
                dve.wait_ge(s_fsg, 2 * n + k + 1)
                if n and not k:
                    dve.wait_ge(s_fy, n)
                V.tensor_tensor(fhT[:, k, 0:w], fsg[:, 0:w], b_up[k][:, 0:w], ALU.mult).then_inc(s_fh, 1)

            def shared_add(t, g):
                lo, hi = t.groups[g]
                dve.wait_ge(s_fy, GA[t.name] + g + 1)
                V.tensor_tensor(rows_of(xf, t, lo, hi), rows_of(xf, t, lo, hi), tiles_of(b_tok[:, 0:(hi - lo) * D], t),
                                ALU.add).then_inc(s_fa, 1)

            def gate(run, i, k):
                for u in range(U):
                    dve.wait_ge(s_es, i * U + ((k + run.g0) * U + u + 1))
                    V.tensor_tensor(e_h[:, u], e_sg[:, u], b_gu[u][:, F:], ALU.mult).then_inc(s_eh, 1)

            dve.wait_ge(s_x, 16 * 2 * B)
            for s in range(NT):
                V.bn_stats(stats[:, s], xr[:, s]).then_inc(s_st, 1)
            for s in range(NT):
                dve.wait_ge(s_st, s + 1)
                V.bn_aggr(mv[:, s], stats[:, s]).then_inc(s_mv, 1)
            dve.wait_ge(s_xf, 16 * 3 * B)
            dve.wait_ge(s_mv, NT)
            for s in range(L2):
                V.bn_stats(stats[:, s], xf[:, 3 * s]).then_inc(s_st, 1)
            for s in range(L2):
                dve.wait_ge(s_st, NT + s + 1)
                V.bn_aggr(mv[:, NT + s], stats[:, s]).then_inc(s_mv, 1)
            dve.wait_ge(s_sd, 1)
            V.reciprocal(rstd[:, 0:NT], rstd[:, 0:NT]).then_inc(s_rs, 1)
            dve.wait_ge(s_rs, 1)
            for s in range(NT):
                V.tensor_scalar(xr[:, s], xr[:, s], mv[:, s, 0:1], rstd[:, s:s + 1], ALU.subtract,
                                ALU.mult).then_inc(s_xn, 1)
            dve.wait_ge(s_sd, 2)
            V.reciprocal(rstd[:, NT:], rstd[:, NT:]).then_inc(s_rs, 1)
            dve.wait_ge(s_rs, 2)
            for s in range(L2):
                V.tensor_scalar(xa[:, s], xf[:, 3 * s], mv[:, NT + s, 0:1], rstd[:, NT + s:NT + s + 1],
                                ALU.subtract, ALU.mult).then_inc(s_xn, 1)
            row_stats(OTHERS)
            row_norm(OTHERS)
            route(OTHERS)
            dve.wait_ge(s_no, 1)
            V.tensor_scalar(rk[:], rk[:], NORM_EPS, None, ALU.max).then_inc(s_nm, 1)
            dve.wait_ge(s_nm, 1)
            V.reciprocal(rk[:], rk[:]).then_inc(s_rk, 1)
            dve.wait_ge(s_ev, NJ)
            for g, (lo, hi) in enumerate(GROUPS):
                dve.wait_ge(s_rb, g + 1)
                V.tensor_tensor(slot(lo, hi, K), slot(lo, hi, K), psum(g % 2, lo, hi), ALU.mult).then_inc(s_k, 1)
            for g, (lo, hi) in enumerate(GROUPS):
                dve.wait_ge(s_c, g + 1)
                V.tensor_tensor(slot(lo, hi, PP), slot(lo, hi, Y), psum(2 + g % 2, lo, hi), ALU.mult).then_inc(s_gc, 1)
                dve.wait_ge(s_gk, g + 1)
                dve.wait_ge(s_gc, g + 1)
                n = hi - lo
                V.scalar_tensor_tensor(slot(lo, hi, Y), work[:, 0, g % 2, 0:n * P].rearrange("p (s x) -> p s x", x=P),
                                       -1.0, slot(lo, hi, Y), ALU.mult, ALU.mult).then_inc(s_y, 1)
                dve.wait_ge(s_y, g + 1)
                V.tensor_tensor(slot(lo, hi, PP), slot(lo, hi, PP),
                                decayed[:, g % 2, 0:n * P].rearrange("p (s x) -> p s x", x=P),
                                ALU.mult).then_inc(s_m, 1)

            def products(h, tile, ready, w):
                dve.wait_ge(s_state[h], ready)
                st = state[:, h].unsqueeze(1).to_broadcast([P, 2, HALF]).rearrange("p e (x w) -> p e x w", w=w)
                V.tensor_tensor(work[:, h].rearrange("p e (x w) -> p e x w", w=w), st, per_col(tile, Y, 2, h, w),
                                ALU.mult).then_inc(s_prod[h], 1)

            def update(h, tile, done, w, used=None):
                dve.wait_ge(s_red[h], done)
                V.tensor_tensor(work[:, h].rearrange("p e (x w) -> p e x w", w=w),
                                ps[h][:].rearrange("p e (x w) -> p e x w", w=w), per_col(tile, K, 2, h, w),
                                ALU.mult).then_inc(s_term[h], 1)
                dve.wait_ge(s_term[h], done)
                dve.wait_ge(s_dec[h], done)
                V.tensor_tensor(decayed[:, h], decayed[:, h], work[:, h, 1], ALU.add).then_inc(s_add[h], 1)
                dve.wait_ge(s_add[h], done)
                if used is not None:
                    dve.wait_ge(s_q[h], used)
                V.tensor_tensor(state[:, h], decayed[:, h], work[:, h, 0], ALU.add).then_inc(s_state[h], 1)

            for r, (first, n) in enumerate(REGION):
                base = r * L1
                if r:
                    dve.wait_ge(s_min, 128)
                else:
                    dve.wait_ge(s_p, NG)
                for h in (0, 1):
                    V.tensor_copy(state[:, h].rearrange("p (x w) -> p x w", w=HD),
                                  c["diag8"].unsqueeze(1).to_broadcast([P, P // 2, HD])).then_inc(s_state[h], 1)
                last = base + n - 1
                r0 = base + r + 1
                products(0, last, r0, HD)
                products(1, last, r0, HD)
                update(0, last, base + 1, HD)
                with dve.Fori(1, n) as i:
                    tile = (i * -1) + last
                    products(0, tile, i + r0, HD)
                    update(1, tile + 1, i + base, HD)
                    products(1, tile, i + r0, HD)
                    update(0, tile, i + (base + 1), HD)
                update(1, base, base + n, HD)
            def beside(m):
                if 0 <= m < SHARED_EVERY * NOG:
                    g, at = m // SHARED_EVERY, m % SHARED_EVERY
                    if at in (0, 1):
                        shared_h(OTHERS, g, at)
                    elif at == 3:
                        shared_add(OTHERS, g)
                elif (m - PAIRS_FROM) % PAIR_EVERY == 0 and 0 <= (m - PAIRS_FROM) // PAIR_EVERY < BESIDE:
                    gate(RUNS[0], 0, (m - PAIRS_FROM) // PAIR_EVERY)

            V.memset(ch_s[:, :, 0, :], 0.0).then_inc(s_ca, 1)
            for h in (0, 1):
                dve.wait_ge(s_uc[h], NT + 1)
            for r, n in ((0, C), (1, C - 1)):
                dve.wait_ge(s_min, 128 * (r + 1))
                dve.wait_ge(s_bin, 128 * (r + 1))
                if r:
                    dve.wait_ge(s_ca, C + 1)
                    V.tensor_copy(ch_s[:, :, 0, :], ch_s[:, :, C, :]).then_inc(s_ca, 1)
                for i in range(n):
                    m = r * C + i + 1
                    dve.wait_ge(s_ca, m + r)
                    V.tensor_tensor(ch_pr, ch_m[r][:, :, i, :].rearrange("p j i -> p i j").unsqueeze(1)
                                    .to_broadcast([P, 4, HD, HD]), ch_s[:, :, i, :].rearrange("p j v -> p v j")
                                    .unsqueeze(2).to_broadcast([P, 4, HD, HD]), ALU.mult).then_inc(s_cm, 1)
                    dve.wait_ge(s_cm, m)
                    V.tensor_reduce(ch_sum, ch_pr, AX.X, ALU.add).then_inc(s_cr, 1)
                    dve.wait_ge(s_cr, m)
                    V.tensor_tensor(ch_s[:, :, i + 1, :].rearrange("p i v -> p v i"), ch_sum,
                                    ch_b[r][:, :, i, :], ALU.add).then_inc(s_ca, 1)
                    beside(m - BEGIN)
            for k in range((2 * C - 1 - BEGIN - PAIRS_FROM) // PAIR_EVERY + 1, BESIDE):
                gate(RUNS[0], 0, k)
            dve.wait_ge(s_chout, 128)
            for h in (0, 1):
                dve.sem_inc(s_state[h], 1)
            r0 = NT + 3
            products(0, L1, r0, 4)
            products(1, L1, r0, 4)
            update(0, L1, NT + 1, 4)

            def step(i, ends):
                products(0, i + L1, i + r0, 4)
                update(1, i + (L1 - 1), i + NT, 4, i)
                if ends:
                    gate(RUNS[1], i, -2)
                products(1, i + L1, i + r0, 4)
                update(0, i + L1, i + (NT + 1), 4, i + 1)

            step(1, False)
            with dve.Fori(2, L2) as i:
                step(i, True)
            update(1, NT - 1, NT + L2, 4, L2)
            for g, (lo, hi) in enumerate(QGROUPS):
                dve.wait_ge(s_o, g + 1)
                if g == 0:
                    dve.wait_ge(s_state[0], NT + 3 + L2)
                    dve.wait_ge(s_state[1], NT + 3 + L2)
                V.tensor_tensor(cols(og, lo, hi), psum(4 + g, lo, hi), cols(gateT, lo, hi), ALU.mult).then_inc(s_og, 1)
            for g, (lo, hi) in enumerate(QGROUPS):
                dve.wait_ge(s_mu, g + 1)
                V.tensor_tensor(cols(od, lo, hi), cols(og, lo, hi), psum(g, lo, hi), ALU.subtract).then_inc(s_od, 1)
            for g, (lo, hi) in enumerate(QGROUPS):
                dve.wait_ge(s_osq, g + 1)
                V.tensor_scalar(cols(od, lo, hi), cols(od, lo, hi), lnw[:], None, ALU.mult).then_inc(s_dw, 1)
            dve.wait_ge(s_sd2, 1)
            V.reciprocal(rstd2[:], rstd2[:]).then_inc(s_rs2, 1)
            dve.wait_ge(s_rs2, 1)
            for g, (lo, hi) in enumerate(QGROUPS):
                dve.wait_ge(s_at, g + 1)
                for s in range(lo, hi):
                    V.scalar_tensor_tensor(xf[:, 3 * s], psum(4 + g, lo, hi)[:, s - lo], rstd2[:, s:s + 1], xf[:, 3 * s],
                                           ALU.mult, ALU.add).then_inc(s_x1, 1)
            row_stats(MIXED)
            row_norm(MIXED)
            route(MIXED)
            for g in range(len(MIXED.groups)):
                for k in (0, 1):
                    shared_h(MIXED, g, k)
                shared_add(MIXED, g)
            gate(RUNS[2], 0, 0)
            dve.wait_ge(s_gat[OTHERS.name], 16 * OTHERS.n)
            V.tensor_tensor(rows_of(xf, OTHERS, 0, OTHERS.n), rows_of(xf, OTHERS, 0, OTHERS.n),
                            tiles_of(fb[OTHERS.name]["back"], OTHERS), ALU.add).then_inc(s_fin, 1)

            def pair(i, k, ahead):
                if ahead:
                    gate(RUNS[2], i, k + 1)

            over_pairs(dve, RUNS[2], pair)
            dve.wait_ge(s_gat[MIXED.name], 16 * MIXED.n)
            V.tensor_tensor(rows_of(xf, MIXED, 0, MIXED.n), rows_of(xf, MIXED, 0, MIXED.n),
                            tiles_of(fb[MIXED.name]["back"], MIXED), ALU.add).then_inc(s_fin, 1)

        @block.tensor
        def _(pe):
            pe.wait_ge(s_cst, 16)
            pe.wait_ge(s_wa, 160)
            for k in (0, 1):
                ins = T.transpose(bank[7][0:HD, k * P:(k + 1) * P], wlow[:, k], c["ident"])
            ins.then_inc(s_wt, 1)
            pe.wait_ge(s_wtc, 1)
            for k in (0, 1):
                ins = T.matmul(bank[7][:, k * D:(k + 1) * D], wlowT[:, k], wup[:, k], start=True, stop=True)
            ins.then_inc(s_wp, 1)
            pe.wait_ge(s_wf, 80)
            pe.wait_ge(s_w, 1)
            for k in range(4):
                T.transpose(bank[6][:, k * P:(k + 1) * P], wnat[:, k], c["ident"])
            for k in range(2):
                T.transpose(bank[7][:, k * P:(k + 1) * P], wnat[:, 4 + k], c["ident"])
            T.transpose(bank[7][:, 2 * P:2 * P + E], wnat[0:E, 6], c["ident"][0:E, 0:E]).then_inc(s_wft, 1)
            for n, (lo, hi) in enumerate(GROUPS + QGROUPS):
                pe.wait_ge(s_xn, hi + (NT if n >= NG else 0))
                if n >= 2:
                    pe.wait_ge(s_xT, n - 1)
                for s in range(lo, hi):
                    src = xr[:, s] if n < NG else xa[:, s]
                    ins = T.transpose(bank[n % 2][:, (s - lo) * P:(s - lo + 1) * P], src, c["ident"])
                ins.then_inc(s_tp, 1)
            pe.wait_ge(s_w, 1)
            pe.wait_ge(s_wge, 1)
            pe.wait_ge(s_xT, NTP)
            pe.wait_ge(s_wfT, 3)

            def route_transposes(t, g):
                lo, hi = t.groups[g]
                pe.wait_ge(s_fn, TB[t.name] + hi)
                for j in range(lo, hi):
                    ins = T.transpose(b_xT[:, (j - lo) * P:(j - lo + 1) * P], fb[t.name]["rows"][j], c["ident"])
                ins.then_inc(s_lt, 1)

            def logits(t, g):
                lo, hi = t.groups[g]
                pe.wait_ge(s_lx, GB[t.name] + g + 1)
                for j in range(lo, hi):
                    ins = T.matmul(b_tok[:, j * E:(j + 1) * E], fxT_route[t.name][:, (j - lo) * P:(j - lo + 1) * P],
                                   wrT[:], start=True, stop=True)
                if g == len(t.groups) - 1:
                    ins.then_inc(s_lg, 1)

            def rank(t):
                pe.wait_ge(s_oh, 1 + (t is MIXED))
                pe.wait_ge(s_flc, 1 + (t is MIXED))
                ranks, totals = b_rank[t.name]
                T.matmul(ranks[:, 0:t.n * E], c["before"], fb[t.name]["oh"], start=True, stop=True)
                T.matmul(totals[:, 0:t.n * E], c["ones"], fb[t.name]["oh"], start=True, stop=True).then_inc(s_rank, 1)

            for j, (w, lo, hi, k, func) in enumerate(jobs):
                if ROUTE_AT < j <= ROUTE_AT + NOG + 1:
                    if j > ROUTE_AT + 1:
                        logits(OTHERS, j - ROUTE_AT - 2)
                    if j <= ROUTE_AT + NOG:
                        route_transposes(OTHERS, j - ROUTE_AT - 1)
                if j == RANK_AT:
                    rank(OTHERS)
                if j >= 4:
                    pe.wait_ge(s_ev, j - 3)
                src = xaT if k is None and func == ACT.Sigmoid else xnT
                T.matmul(bank[2 + j % 4][:, 0:(hi - lo) * P], w, src[:, lo * P:hi * P],
                         start=True, stop=True).then_inc(s_pj, 1)
            pe.wait_ge(s_idx, 1)
            for g, (lo, hi) in enumerate(GROUPS):
                pe.wait_ge(s_sq, g + 1)
                for s in range(lo, hi):
                    ins = T.matmul(bank[6][:, s * H:(s + 1) * H], steps[:, s, PP], c["heads"], start=True, stop=True)
            ins.then_inc(s_ss, 1)
            for g, (lo, hi) in enumerate(GROUPS):
                pe.wait_ge(s_rke, g + 1)
                if g >= 2:
                    pe.wait_ge(s_k, g - 1)
                for s in range(lo, hi):
                    ins = T.matmul(bank[g % 2][:, (s - lo) * P:(s - lo + 1) * P], xr[:, s], c["ident"], start=True, stop=True)
                ins.then_inc(s_rb, 1)
            pe.wait_ge(s_ev, NJ)
            for g, (lo, hi) in enumerate(GROUPS):
                pe.wait_ge(s_fkk, g + 1)
                if g >= 2:
                    pe.wait_ge(s_gc, g - 1)
                T.matmul(bank[2 + g % 2][:, 0:(hi - lo) * P], c["block"], work[:, 1, g % 2, 0:(hi - lo) * P],
                         start=True, stop=True).then_inc(s_c, 1)
            for h in (0, 1):
                pe.sem_inc(s_ba[h], 1)
            pe.wait_ge(s_zero, 1)

            def sums(h):
                for e in (0, 1):
                    ins = T.matmul(bank[2 * h + e], c["block"], work[:, h, e], start=True, stop=True)
                return ins

            for r, (_, n) in enumerate(REGION):
                base = r * L1
                if r:
                    pe.wait_ge(s_bc, 1)
                pe.wait_ge(s_gc, NG)
                for h in (0, 1):
                    T.matmul(bank[4 + h], zeros[:, 0:P], zeros[:], start=True, stop=False)
                def add_sum(h, n):
                    pe.wait_ge(s_bp[h], n)
                    T.matmul(bank[4 + h], c["ident"], vterm[:, h], start=False, stop=False).then_inc(s_ba[h], 1)

                for h in (0, 1):
                    pe.wait_ge(s_prod[h], base + 1)
                    pe.wait_ge(s_uc[h], base + 1)
                    sums(h).then_inc(s_red[h], 1)
                with pe.Fori(1, n) as i:
                    for h in (0, 1):
                        pe.wait_ge(s_prod[h], i + (base + 1))
                        pe.wait_ge(s_uc[h], i + (base + 1))
                        sums(h).then_inc(s_red[h], 1)
                        add_sum(h, i + (base + 1))
                for h in (0, 1):
                    add_sum(h, base + n + 1)
                for h in (0, 1):
                    T.matmul(bank[4 + h], zeros[:, 0:P], zeros[:], start=False, stop=True).then_inc(s_bs, 1)
            def shared(t, ranks=False):
                def transposes(g):
                    lo, hi = t.groups[g]
                    if t is OTHERS:
                        pe.wait_ge(s_late, hi)
                    for j in range(lo, hi):
                        ins = T.transpose(b_xT[:, (j - lo) * P:(j - lo + 1) * P], fb[t.name]["shared"][j], c["ident"])
                    ins.then_inc(s_ft, 1)

                transposes(0)
                for g, (lo, hi) in enumerate(t.groups):
                    n, w = GA[t.name] + g, (hi - lo) * P
                    pe.wait_ge(s_fx, n + 1)
                    for k in (0, 1):
                        if n:
                            pe.wait_ge(s_fh, 2 * n + k - 1)
                        T.matmul(b_gate[k][:, 0:w], wT[:, k], fxT[:, 0:w], start=True, stop=True)
                        T.matmul(b_up[k][:, 0:w], wT[:, 2 + k], fxT[:, 0:w], start=True, stop=True).then_inc(s_fgu, 1)
                    if ranks and not g:
                        rank(t)
                    if g + 1 < len(t.groups):
                        transposes(g + 1)
                    pe.wait_ge(s_fh, 2 * n + 2)
                    if n:
                        pe.wait_ge(s_fa, n)
                    for j in range(lo, hi):
                        at = (j - lo) * P
                        for k in (0, 1):
                            ins = T.matmul(b_tok[:, at:at + D], fhT[:, k, at:at + P], wT[:, 4 + k], start=(k == 0),
                                           stop=(k == 1))
                    ins.then_inc(s_fy, 1)

            def experts(run, i, k):
                te = fb[run.t.name]["te"]
                return [pe.value_load(te[0:1, bass.ds(i * U + ((k + run.first) * U + u), 1)], min_val=0, max_val=E - 1)
                        for u in range(U)]

            def x_transposes(run, i, k, b, loaded):
                pe.wait_ge(s_ei[b], loaded)
                for u in range(U):
                    ins = T.transpose(b_x[:, u * P:(u + 1) * P], e_in[:, b, u], c["ident"])
                ins.then_inc(s_et, 1)

            def gate_up(run, i, k, b):
                ex = experts(run, i, k)
                pe.wait_ge(s_ex, i + (k + run.g0 + 1))
                for u in range(U):
                    T.matmul(b_gu[u], e_xT[:, b, u], gu[:, bass.ds(ex[u] * (2 * F), 2 * F)],
                             start=True, stop=True).then_inc(s_eg, 1)

            def h_transposes(run, i, k):
                for u in range(U):
                    pe.wait_ge(s_eh, i * U + ((k + run.g0) * U + u + 1))
                    for f in (0, 1):
                        ins = T.transpose(b_h[:, (2 * u + f) * P:(2 * u + f + 1) * P],
                                          e_h[:, u, f * P:(f + 1) * P], c["ident"])
                ins.then_inc(s_eht, 1)

            def down(run, i, k, copied=None):
                ex = experts(run, i, k)
                if copied is not None:
                    pe.wait_ge(s_ex, copied)
                pe.wait_ge(s_ehc, i + (k + run.g0 + 1))
                for u in range(U):
                    for f in (0, 1):
                        ins = T.matmul(b_y[:, u * D:(u + 1) * D], e_hT[:, u, f * P:(f + 1) * P],
                                       dw[:, bass.ds(ex[u] * F + f * D, D)], start=(f == 0), stop=(f == 1))
                ins.then_inc(s_ey, 1)

            def pairs(run):
                def loaded(i, k):
                    return i * 8 + 16 * (k // 2 + 1 + run.base[k % 2])

                def pair(i, k, ahead):
                    h_transposes(run, i, k)
                    pe.wait_ge(s_eo, i + (k + run.g0 + 1))
                    if ahead > 1:
                        pe.wait_ge(s_ex, i + (k + run.g0 + 2))
                        x_transposes(run, i, k + 2, k % 2, loaded(i, k + 2))
                    if ahead:
                        gate_up(run, i, k + 1, (k + 1) % 2)
                    down(run, i, k, i + (k + run.g0 + 3) if ahead > 1 else None)

                pe.wait_ge(s_te, 1 + (run.t is MIXED))
                pe.wait_ge(s_eo, run.g0 + 1)
                x_transposes(run, 0, 0, 0, loaded(0, 0))
                pe.wait_ge(s_ex, run.g0 + 1)
                x_transposes(run, 0, 1, 1, loaded(0, 1))
                gate_up(run, 0, 0, 0)
                over_pairs(pe, run, pair)

            pe.wait_ge(s_bc, 2)
            shared(OTHERS)
            pe.wait_ge(s_fa, NOG)
            pe.wait_ge(s_we, 48)
            pairs(RUNS[0])
            run = RUNS[1]

            def forward(i, h):
                pe.wait_ge(s_prod[h], i + (NT + 1))
                T.matmul(bank[2 * h + 1], c["block"], work[:, h, 1], start=True, stop=True)
                T.matmul(bank[2 * h], c["block"], work[:, h, 0], start=True, stop=False)
                pe.wait_ge(s_vd[h], i + 1)
                T.matmul(bank[2 * h], c["block"], vterm[:, h], start=False, stop=True).then_inc(s_red[h], 1)

            def step(i, begins, ends):
                forward(i, 0)
                if begins:
                    pe.wait_ge(s_eo, i + (run.g0 - 1))
                    x_transposes(run, i, -1, 0, i * 16 + 16 * run.base[0])
                forward(i, 1)
                if ends:
                    h_transposes(run, i, -2)
                if begins:
                    gate_up(run, i, -1, 0)
                if ends:
                    down(run, i, -2)

            pe.wait_ge(s_eo, run.g0 + 1)
            step(0, False, False)
            step(1, True, False)
            with pe.Fori(2, L2 - 1) as i:
                step(i, True, True)
            step(L2 - 1, False, True)
            pe.wait_ge(s_eo, run.g0 + run.n + 1)
            pe.wait_ge(s_bc, 2)
            for g, (lo, hi) in enumerate(QGROUPS):
                for h in (0, 1):
                    pe.wait_ge(s_q[h], hi + 1)
                for v in range(HD):
                    ins = T.matmul(psum(4 + g, lo, hi), c["sel"][:, v * P:(v + 1) * P], qs[:, lo:hi, v // 4, :, v % 4],
                                   start=(v == 0), stop=(v == HD - 1))
                ins.then_inc(s_o, 1)
            for g, (lo, hi) in enumerate(QGROUPS):
                pe.wait_ge(s_og, g + 1)
                T.matmul(bank[g][:, 0:(hi - lo) * P], c["mean"], og[:, lo * P:hi * P], start=True,
                         stop=True).then_inc(s_mu, 1)
            for s in range(L2):
                pe.wait_ge(s_osq, s // 4 + 1)
                ins = T.matmul(bank[3][:, s:s + 1], osq[:, s * P:(s + 1) * P], c["mean"][:, 0:1], start=True, stop=True)
            ins.then_inc(s_var, 1)
            for g, (lo, hi) in enumerate(QGROUPS):
                pe.wait_ge(s_dw, g + 1)
                for s in range(lo, hi):
                    ins = T.matmul(bank[4 + g][:, (s - lo) * D:(s - lo + 1) * D], od[:, s * P:(s + 1) * P], wout[:],
                                   start=True, stop=True)
                ins.then_inc(s_at, 1)
            for g in range(len(MIXED.groups)):
                if g:
                    logits(MIXED, g - 1)
                route_transposes(MIXED, g)
            logits(MIXED, len(MIXED.groups) - 1)
            shared(MIXED, ranks=True)
            pe.wait_ge(s_fa, GA[MIXED.name] + len(MIXED.groups))
            pe.wait_ge(s_idx, 2)
            pairs(RUNS[2])


_NAMES = {
    "L0_attn_x": "x", "L0_attn_Wq": "Wq", "L0_attn_Wk": "Wk", "L0_attn_Wv": "Wv", "L0_attn_Wf1": "Wf1",
    "L0_attn_Wf2": "Wf2", "L0_attn_Wg": "Wg", "L0_attn_Wo1": "Wo1", "L0_attn_Wo2": "Wo2",
    "L0_attn_ln_w": "ln_w", "L0_attn_Wout": "Wout", "L0_ffn_w_router": "w_router",
    "L0_ffn_gate_up_proj": "gate_up_proj", "L0_ffn_down_proj": "down_proj", "L0_ffn_w_gate": "w_gate",
    "L0_ffn_w_up": "w_up", "L0_ffn_w_down": "w_down",
}


def kernel(**inputs):
    import concourse.bacc as bacc
    from concourse.bass_utils import run_bass_kernel_spmd

    nc = bacc.Bacc("TRN2", target_bir_lowering=False, num_devices=1)
    arrays, aps = {}, {}
    for name, short in _NAMES.items():
        arrays[short] = np.ascontiguousarray(inputs[name])
    arrays["const"] = CONST
    for short, v in arrays.items():
        aps[short] = nc.dram_tensor(short, v.shape, F32, kind="ExternalInput").ap()
    out = nc.dram_tensor("out", (B, N, D), F32, kind="ExternalOutput").ap()
    xs = {t.name: nc.dram_tensor("xs_" + t.name, ((t.tiles + 1) * P, D), F32).ap() for t in (OTHERS, MIXED)}
    ys = {t.name: nc.dram_tensor("ys_" + t.name, ((t.tiles + 1) * P, D), F32).ap() for t in (OTHERS, MIXED)}
    scr = {"m": [nc.dram_tensor(f"chain_m{r}", (P, COLS), F32).ap() for r in (0, 1)],
           "b": [nc.dram_tensor(f"chain_b{r}", (P, COLS), F32).ap() for r in (0, 1)],
           "s": nc.dram_tensor("chain_s", (P * HD, C * 4), F32).ap()}
    build(nc, aps, out, xs, ys, scr)
    r = run_bass_kernel_spmd(nc, [arrays], core_ids=[0])
    return r.results[0]["out"]
```

```python
import numpy as np

import concourse.bass as bass
from concourse import mybir
from contextlib import ExitStack

F32 = mybir.dt.float32
I32 = mybir.dt.int32
U32 = mybir.dt.uint32
ALU = mybir.AluOpType
ACT = mybir.ActivationFunctionType
AX = mybir.AxisListType

B, N, D = 4, 1024, 128
H = 16
HD = D // H
C = 32
P = 128
NOUT = (N + 2) // 3
L2 = -(-NOUT // C)
L1 = (N - C * L2) // C
T1 = C * L1
SKIP = (N - NOUT) - T1
NT = L1 + L2
ROWS = 3 * L2
LN_EPS = 1e-5
NORM_EPS = 1e-12
E, F = 16, 256
COLS = P * HD
HALF = COLS // 2
assert T1 + C * L2 == N and SKIP >= 0


U = 2


class Tokens:

    def __init__(self, name, rows, valid):
        self.name, self.rows = name, rows
        self.n = len(rows)
        self.need = (valid - E) // P + E
        self.tiles = -(-self.need // U) * U
        self.groups = [(4 * g, min(4 * g + 4, self.n)) for g in range(-(-self.n // 4))]


class Run:

    def __init__(self, t, first, n, g0, base):
        self.t, self.first, self.n, self.g0, self.base = t, first, n, g0, base


OTHERS = Tokens("others", [j for j in range(ROWS) if j % 3], 2 * B * (N // 3))
MIXED = Tokens("mixed", [j for j in range(ROWS) if j % 3 == 0], B * NOUT)


def row_valid():
    tok = 3 * L2 * (np.arange(P)[:, None] % C) - 3 * SKIP + np.arange(ROWS)[None, :]
    return (tok >= 0) & (tok < N)


def constants():
    p = np.arange(P)
    parts = {}
    parts["ident"] = np.eye(P)
    parts["block"] = (p[:, None] // HD == p[None, :] // HD)
    parts["heads"] = (p[:, None] // HD == np.arange(H)[None, :])
    parts["diag8"] = (p[:, None] % HD == np.arange(HD)[None, :])
    parts["sel"] = np.concatenate([parts["block"] & (p[None, :] % HD == v) for v in range(HD)], 1)
    parts["before"] = (p[:, None] < p[None, :])
    parts["ones"] = np.ones((P, P))
    parts["mean"] = np.full((P, P), 1.0 / D)
    valid = row_valid()
    for t in (OTHERS, MIXED):
        v = valid[:, t.rows]
        parts["valid_" + t.name] = v
        spare = np.where(v, 0, t.tiles * P + np.cumsum(~v.ravel()).reshape(v.shape) - 1)
        parts["spare_" + t.name] = spare
        assert (~v).sum() <= P
    parts["prefer"] = np.tile(E - np.arange(E)[None, :], (P, 1))
    parts["steps128"] = np.tile(P * np.arange(OTHERS.n)[None, :], (P, 1))
    parts["tileno"] = np.tile(np.arange(OTHERS.tiles)[None, :], (P, 1))
    at, n = {}, 0
    for k, a in parts.items():
        at[k] = (n, n + a.shape[1])
        n += a.shape[1]
    return np.concatenate([np.asarray(a, np.float32) for a in parts.values()], 1), at


CONST, AT = constants()



Y, K, PP, FF, VV = range(5)
GROUPS = [(4 * g, min(4 * g + 4, NT)) for g in range(-(-NT // 4))]
QGROUPS = [(4 * g, min(4 * g + 4, L2)) for g in range(-(-L2 // 4))]
NG, NQ = len(GROUPS), len(QGROUPS)


def spread(ap, *shape):
    return ap.to_broadcast([P, *shape])


def build(nc, a, out, xs, ys, scr):
    ctx = ExitStack()
    with ctx:
        def sb(name, shape, dt=F32):
            return ctx.enter_context(nc.sbuf_tensor(name, shape, dt))

        def sem(name):
            return ctx.enter_context(nc.semaphore(name))

        V, S, G, T = nc.vector, nc.scalar, nc.gpsimd, nc.tensor

        cst = sb("cst", [P, CONST.shape[1]])
        c = {k: cst[:, lo:hi] for k, (lo, hi) in AT.items()}
        zeros = sb("zeros", [P, HALF])
        eps = sb("eps", [P, 1])
        early = sb("early", [P, L2 * COLS])
        xr = early[:, 0:NT * D].rearrange("p (s d) -> p s d", s=NT)
        xnT = early[:, NT * D:2 * NT * D]
        xa = early[:, 2 * NT * D:2 * NT * D + L2 * D].rearrange("p (s d) -> p s d", s=L2)
        xaT = early[:, 2 * NT * D + L2 * D:2 * NT * D + 2 * L2 * D]
        nm, nb = C * HD * HD, C * HD * 4
        ch_m = [early[:, r * nm:(r + 1) * nm].rearrange("p (j c i) -> p j c i", j=HD, c=C) for r in (0, 1)]
        ch_b = [early[:, 2 * nm + r * nb:2 * nm + (r + 1) * nb].rearrange("p (v c i) -> p v c i", v=4, c=C)
                for r in (0, 1)]
        at = 2 * nm + 2 * nb
        ch_s = early[:, at:at + HD * (C + 1) * 4].rearrange("p (i c v) -> p i c v", i=HD, c=C + 1)
        at += HD * (C + 1) * 4
        ch_pr = early[:, at:at + 2 * 4 * HD * (HD + 1)].rearrange("p (b v i j) -> p b v i j", b=2, v=4, i=HD)
        at += 2 * 4 * HD * (HD + 1)
        ch_end = at
        qs = early[:, :].rearrange("p (s h x v) -> p s h x v", s=L2, h=2, v=4)
        xf = sb("xf", [P, ROWS, D])
        steps = sb("steps", [P, NT, 5, P])
        qT = sb("qT", [P, L2 * P])
        gateT = sb("gateT", [P, L2 * P])
        wqkv = sb("wqkv", [P, 3, D])
        wgs = sb("wgs", [P, H])
        wge = sb("wge", [P, D])
        wlow = sb("wlow", [P, 2, HD])
        wlowT = sb("wlowT", [HD, 2, P])
        wup = sb("wup", [HD, 2, D])
        wfo = sb("wfo", [P, 2, D])
        wout = sb("wout", [P, D])
        lnw = sb("lnw", [P, 1])
        state = sb("state", [P, 2, HALF])
        work = sb("work", [P, 2, 2, HALF])
        decayed = sb("decayed", [P, 2, HALF])
        uv = sb("uv", [P, 2, 2, HALF])
        ucopy, vterm = uv[:, 0], uv[:, 1]
        mv = sb("mv", [P, NT + L2, 2])
        rstd = sb("rstd", [P, NT + L2])
        rk = sb("rk", [P, NT * H])
        stats = rk[:, 0:(NT + L2) * 6].rearrange("p (s x) -> p s x", x=6)
        og = work[:].rearrange("p a b c -> p (a b c)")[:, 0:L2 * P]
        od = uv[:].rearrange("p a b c -> p (a b c)")[:, 0:L2 * P]
        osq = early[:, 0:L2 * P]
        rstd2 = sb("rstd2", [P, L2])

        ps = [ctx.enter_context(nc.psum_tensor(f"ps{i}", [P, 2, HALF], F32)) for i in range(4)]
        bank = [ps[i // 2][:, i % 2, :] for i in range(8)]

        s_cst, s_x, s_xf, s_wa = sem("s_const"), sem("s_x"), sem("s_xf"), sem("s_attn_weights")
        s_zero, s_xfz = sem("s_zeros"), sem("s_xf_zeroed")
        s_st, s_mv, s_sd, s_rs, s_xn = sem("s_stats"), sem("s_mv"), sem("s_std"), sem("s_rstd"), sem("s_xn")
        s_tp, s_xT = sem("s_transposed"), sem("s_xT")
        s_wt, s_wtc, s_wp, s_w = sem("s_wlow_transposed"), sem("s_wlowT"), sem("s_wproduct"), sem("s_wfo")
        s_wge = sem("s_wge")
        s_pj, s_ev, s_sq = sem("s_projected"), sem("s_evicted"), sem("s_ksq")
        s_ss, s_no, s_nm, s_rk, s_rb = sem("s_ss"), sem("s_norm"), sem("s_normmax"), sem("s_rk"), sem("s_rb")
        s_rke = sem("s_rk_spread")
        s_k, s_fk, s_fkk, s_gk = sem("s_k"), sem("s_fk"), sem("s_fkk"), sem("s_gk")
        s_c, s_gc, s_y, s_m, s_p = sem("s_c"), sem("s_gc"), sem("s_y"), sem("s_m"), sem("s_p")
        two = lambda n: [sem(f"{n}{h}") for h in (0, 1)]
        s_state, s_prod, s_red, s_term = two("s_state"), two("s_prod"), two("s_red"), two("s_term")
        s_add, s_dec, s_uc, s_bp, s_ba = two("s_add"), two("s_dec"), two("s_uc"), two("s_bp"), two("s_ba")
        s_usum, s_uterm = two("s_usum"), two("s_uterm")
        s_bs, s_bc = sem("s_bsum"), sem("s_bcopy")
        s_min, s_bin = sem("s_matrices_in"), sem("s_sums_in")
        s_mout, s_bout, s_sout = sem("s_m_out"), sem("s_b_out"), sem("s_s_out")
        s_cm, s_cb, s_ca = sem("s_chain_mul"), sem("s_chain_sums"), sem("s_chain_state")
        s_chout = sem("s_chain_out")
        s_vd, s_q = two("s_vd"), two("s_q")
        s_o, s_og, s_mu, s_od, s_osq, s_dw = (sem("s_o"), sem("s_og"), sem("s_mu"), sem("s_od"), sem("s_osq"),
                                              sem("s_dw"))
        s_var, s_sd2, s_rs2, s_at, s_x1 = sem("s_var"), sem("s_std2"), sem("s_rstd2"), sem("s_at"), sem("s_x1")
        gu = steps[:].rearrange("p a b c -> p (a b c)")[:, 0:E * 2 * F]
        dw = steps[:].rearrange("p a b c -> p (a b c)")[:, E * 2 * F:E * 3 * F]
        wnat = sb("wnat", [P, 7, D])
        wT = sb("wT", [P, 6, P])
        wrT = sb("wrT", [P, E])
        work_all, uv_all = (x[:].rearrange("p a b c -> p (a b c)") for x in (work, uv))
        rooms = [early[:, L2 * P:]]

        def take(n, dt=F32):
            k = next(k for k, r in enumerate(rooms) if r.shape[1] >= n)
            piece, rooms[k] = rooms[k][:, 0:n], rooms[k][:, n:]
            return piece if dt == F32 else piece.bitcast(dt)

        fb = {}
        w16, rest = work_all.shape[1] // D, OTHERS.n - work_all.shape[1] // D
        early_rows = [work_all[:, j * D:(j + 1) * D] for j in range(w16)]
        early_rows += [uv_all[:, j * D:(j + 1) * D] for j in range(rest)]
        assert ch_end + OTHERS.n * D <= L2 * COLS
        late = [early[:, ch_end + j * D:ch_end + (j + 1) * D] for j in range(OTHERS.n)]
        for t in (MIXED, OTHERS):
            q = {}
            fb[t.name] = q
            if t is OTHERS:
                q["back"] = take(t.n * D)
                rooms = [early[:, nm:2 * nm], early[:, 2 * nm + nb:2 * nm + 2 * nb]]
                q["rows"] = early_rows
                q["shared"] = late
                held = (decayed[:].rearrange("p a b -> p (a b)"), vterm.rearrange("p a b -> p (a b)"),
                        state[:].rearrange("p a b -> p (a b)"))
                q["scaled"] = [r[:, k * D:(k + 1) * D] for r in held for k in range(2 * HALF // D)][0:t.n]
                q["lg"] = take(t.n * E)
            else:
                rows, scaled = take(t.n * D), take(t.n * D)
                q["rows"] = q["shared"] = [rows[:, j * D:(j + 1) * D] for j in range(t.n)]
                q["scaled"] = [scaled[:, j * D:(j + 1) * D] for j in range(t.n)]
                q["back"] = rows
                q["lg"] = take(t.n * E)
            q["r_te"], q["oh"] = take(t.tiles * E), take(t.n * E)
            for name in ("r_tot", "r_inc", "r_a", "r_keep"):
                q[name] = take(t.n * E)
            for name in ("r_nt", "r_ti", "r_ts", "r_one"):
                q[name] = take(E)
            q["r_tf"] = take(t.tiles)
            q["score"] = sb("score_" + t.name, [P, t.n])[:]
            for name in ("mx", "mw", "slot"):
                q[name] = take(t.n)
            q["idx"] = sb("slots_" + t.name, [P, t.n], I32)
            q["stats"] = stats[:, 0:t.n]
            q["mv"] = sb("mv_" + t.name, [P, t.n, 2])
            q["rstd"] = sb("rstd_" + t.name, [P, t.n])
            q["shift"] = sb("shift_" + t.name, [P, t.n])[:]
            q["te"] = sb("te_" + t.name, [1, t.tiles // U * 4], I32)
        def xT_route(t, g):
            lo, hi = t.groups[g]
            return gateT[:, 0:(hi - lo) * P] if t is OTHERS else work_all[:, lo * P:hi * P]

        def xT_shared(t, g):
            lo, hi = t.groups[g]
            return work_all[:, 0:(hi - lo) * P] if t is OTHERS else work_all[:, lo * P:hi * P]

        at = {OTHERS.name: 4 * P, MIXED.name: MIXED.n * P}
        f_silu = {t.name: work_all[:, at[t.name]:at[t.name] + 4 * P] for t in (OTHERS, MIXED)}
        f_h = {OTHERS.name: work_all[:, 8 * P:16 * P].rearrange("p (k x) -> p k x", k=2),
               MIXED.name: uv_all[:, 0:8 * P].rearrange("p (k x) -> p k x", k=2)}
        left = steps[:].rearrange("p a b c -> p (a b c)")[:, E * 3 * F:L1 * 5 * P]
        assert 4 * U * P <= left.shape[1]
        e_in, e_xT = (left[:, k * 2 * U * P:(k + 1) * 2 * U * P].rearrange("p (b u d) -> p b u d", b=2, u=U)
                      for k in (0, 1))
        e_y = sb("e_y", [P, 2, U, P])
        e_sg = rk[:].rearrange("p (u d) -> p u d", u=U)
        e_h, e_hT = sb("e_h", [P, U, F]), sb("e_hT", [P, U, F])
        b_x, b_h = bank[6][:, 0:U * P], bank[7]

        def b_gu(run, b):
            return (bank[0], bank[1]) if b and run is not RUNS[1] else (bank[4], bank[5])

        def b_y(run):
            return bank[6][:, U * P:] if run is RUNS[1] else bank[2][:, 0:U * P]

        b_gate, b_up, b_tok = (bank[0], bank[2]), (bank[1], bank[3]), bank[7]

        def b_xT(t, g):
            return bank[6] if t is OTHERS else (bank[6], bank[3], bank[0])[g]

        b_rank = {OTHERS.name: (bank[4], bank[5]), MIXED.name: (bank[4], bank[5])}

        s_wf, s_wft, s_wfT = sem("s_ffn_weights"), sem("s_ffn_w_transposed"), sem("s_ffn_wT")
        s_we = sem("s_expert_weights")
        s_xz = sem("s_slots_zeroed")
        s_fst, s_fmv, s_fsd, s_frs, s_fn = (sem("s_f_stats"), sem("s_f_mv"), sem("s_f_std"), sem("s_f_rstd"),
                                            sem("s_f_normed"))
        s_lt, s_lx, s_lg, s_flc = sem("s_r_transposed"), sem("s_r_xT"), sem("s_logits"), sem("s_logits_out")
        s_late, s_shift = sem("s_rows_again"), sem("s_shift")
        s_ft, s_fx, s_fgu = sem("s_f_transposed"), sem("s_f_xT"), sem("s_f_gate_up")
        s_fsg, s_fh, s_fy, s_fa = sem("s_f_silu"), sem("s_f_h"), sem("s_f_y"), sem("s_f_added")
        s_link = sem("s_route_link")
        s_oh, s_rank, s_mx, s_score = sem("s_onehot"), sem("s_rank"), sem("s_max"), sem("s_score")
        s_idx, s_te, s_sc, s_scat = sem("s_slots"), sem("s_tile_experts"), sem("s_scaled"), {t: sem("s_scattered_" + t) for t in fb}
        s_ei, s_et, s_ex, s_eg, s_es = (two("s_e_in"), sem("s_e_transposed"), sem("s_e_xT"), sem("s_e_gate_up"),
                                        sem("s_e_silu"))
        s_eh, s_eht, s_ehc, s_ey, s_eo, s_ew = (sem("s_e_h"), sem("s_e_h_transposed"), sem("s_e_hT"), sem("s_e_y"),
                                                sem("s_e_out"), two("s_e_written"))
        s_gat, s_fin, s_out = {t: two("s_gathered_" + t) for t in fb}, sem("s_final"), sem("s_out")
        s_ends = sem("s_out_ends")
        SETS = (OTHERS, MIXED)
        GB = {OTHERS.name: 0, MIXED.name: len(OTHERS.groups)}
        TB = {OTHERS.name: 0, MIXED.name: OTHERS.n}
        GA = {OTHERS.name: 0, MIXED.name: len(OTHERS.groups)}
        PARTS = ((0, MIXED.n // 2 + 1), (MIXED.n // 2 + 1, MIXED.n))
        both = OTHERS.tiles // U
        BESIDE = 12
        RUNS = [Run(OTHERS, 0, BESIDE, 0, (0, 0)),
                Run(OTHERS, BESIDE, both - BESIDE, BESIDE, ((BESIDE + 1) // 2, BESIDE // 2)),
                Run(MIXED, 0, MIXED.tiles // U, both, ((BESIDE + 1) // 2 + both - BESIDE, BESIDE // 2))]
        block = ctx.enter_context(nc.Block())

        jobs = []
        for lo, hi in GROUPS:
            jobs += [(wqkv[:, 1], lo, hi, K, ACT.Silu), (wqkv[:, 2], lo, hi, VV, ACT.Silu)]
        for lo, hi in QGROUPS:
            jobs.append((wqkv[:, 0], L1 + lo, L1 + hi, None, ACT.Silu))
        for lo, hi in GROUPS:
            jobs += [(wfo[:, 0], lo, hi, FF, ACT.Sigmoid), (wge[:], lo, hi, Y, ACT.Sigmoid)]
        for lo, hi in QGROUPS:
            jobs.append((wfo[:, 1], lo, hi, None, ACT.Sigmoid))
        NJ = len(jobs)
        BEGIN, SHARED_EVERY, PAIRS_FROM, PAIR_EVERY = 3, 5, 33, 3
        NSILU = 2 * NG + NQ
        NOG = len(OTHERS.groups)
        RK_FIRST = 2
        rks, fk_at, fkk_at, gk_at = (early[:, k * 2 * HALF:(k + 1) * 2 * HALF].rearrange("p (b x) -> p b x", b=2)
                                     for k in range(4))

        def at_group(ap, g):
            lo, hi = GROUPS[g]
            return ap[:, g % 2, 0:(hi - lo) * P].rearrange("p (s x) -> p s x", x=P)
        NTP = NG + NQ

        def slot(lo, hi, k):
            return steps[:, lo:hi, k, :]

        def cols(ap, lo, hi):
            return ap[:, lo * P:hi * P].rearrange("p (s x) -> p s x", x=P)

        def psum(b, lo, hi):
            return bank[b][:, 0:(hi - lo) * P].rearrange("p (s x) -> p s x", x=P)

        def rows_of(ap, t, lo, hi):
            if t is MIXED:
                return ap[:, 3 * lo:3 * hi - 2:3, :]
            return ap[:, 3 * lo // 2:3 * hi // 2, :].rearrange("p (r q) d -> p r q d", q=3)[:, :, 1:3, :]

        def tiles_of(ap, t):
            if t is MIXED:
                return ap.rearrange("p (r d) -> p r d", d=D)
            return ap.rearrange("p (r q d) -> p r q d", q=2, d=D)

        def over_pairs(engine, run, pair):
            n = run.n
            looped = (n - 3) // 2 * 2
            with engine.Fori(0, looped // 2) as half:
                i = half * 2
                for k in (0, 1):
                    pair(i, k, 3)
            for k in range(looped, n):
                pair(0, k, n - 1 - k)

        REGION = ((0, L1), (L1, L2))

        def per_col(tile, k, n, h, w):
            x = slice(h * P // 2, (h + 1) * P // 2) if w == HD else slice(0, P)
            ap = steps[:, bass.ds(tile, 1), k:k + n, x].rearrange("p t e x -> p (t e) x")
            return ap.unsqueeze(3).to_broadcast([P, n, P * 4 // w, w])

        def wide(ap, w):
            return ap.rearrange("p (e x w) -> p e x w", e=1, w=w)

        def routed(t):
            return (xs[t.name].rearrange("(m p) d -> p m d", p=P), ys[t.name].rearrange("(m p) d -> p m d", p=P))

        def middle_rows(b):
            n = 3 * SKIP
            return out[b, ROWS - n:(C - 1) * ROWS - n:3, :].rearrange("(g r) d -> g r d", r=L2)

        def pairs_in_out(engine, run):
            x_in, y_out = routed(run.t)

            def load(i, k):
                if type(i) is not int or i + k >= 2:
                    engine.wait_ge(s_et, i + (k + run.g0 - 1))
                elif run.g0:
                    engine.wait_ge(s_et, run.g0)
                engine.dma_start(e_in[:, k % 2], x_in[:, bass.ds(i * U + (k + run.first) * U, U), :]
                             ).then_inc(s_ei[k % 2], 16)

            def pair(i, k, ahead):
                if ahead > 2:
                    load(i, k + 3)
                engine.wait_ge(s_eo, i + (k + run.g0 + 2))
                engine.dma_start(y_out[:, bass.ds(i * U + (k + run.first) * U, U), :], e_y[:, k % 2]
                             ).then_inc(s_ew[k % 2], 16)

            for k in range(3):
                load(0, k)
            over_pairs(engine, run, pair)

        @block.sync
        def _(sp):
            for b in range(B):
                sp.dma_start(xr[b * C:(b + 1) * C, 0:L1, :],
                             a["x"][b, 0:T1, :].rearrange("(c s) d -> c s d", s=L1)).then_inc(s_x, 16)
                sp.dma_start(xr[b * C:(b + 1) * C, L1:, :],
                             a["x"][b, T1:, :].rearrange("(c s) d -> c s d", s=L2)).then_inc(s_x, 16)
            sp.wait_ge(s_xfz, 1)
            n = 3 * SKIP
            for b in range(B):
                g0 = b * C
                sp.dma_start(xf[g0:g0 + 1, n:, :], a["x"][b:b + 1, 0:ROWS - n, :]).then_inc(s_xf, 16)
                sp.dma_start(xf[g0 + 1:g0 + C - 1, :, :],
                             a["x"][b, ROWS - n:(C - 1) * ROWS - n, :].rearrange("(g r) d -> g r d", r=ROWS)
                             ).then_inc(s_xf, 16)
                last = N - ((C - 1) * ROWS - n)
                sp.dma_start(xf[g0 + C - 1:g0 + C, 0:last, :], a["x"][b:b + 1, N - last:, :]).then_inc(s_xf, 16)
            sp.wait_ge(s_zero, 2)
            sp.wait_ge(s_xn, NT + L2)
            for t in SETS:
                sp.dma_start(xs[t.name].rearrange("(m p) d -> p m d", p=P),
                             zeros[:, 0:D].unsqueeze(1).to_broadcast([P, t.tiles + 1, D])).then_inc(s_xz, 16)
                sp.dma_start(ys[t.name][t.tiles * P:, :], zeros[:, 0:D]).then_inc(s_xz, 16)
            for r in (0, 1):
                if r:
                    for h in (0, 1):
                        sp.wait_ge(s_state[h], L1 + 1)
                        sp.wait_ge(s_bp[h], L1 + 1)
                    sp.dma_start(gu.rearrange("p (e f) -> p e f", e=E), a["gate_up_proj"].rearrange("e p f -> p e f")
                                 ).then_inc(s_we, 16)
                    for k in (0, 1):
                        sp.dma_start(dw.rearrange("p (e k d) -> p e k d", e=E, k=2)[:, :, k],
                                     a["down_proj"][:, k * P:(k + 1) * P, :].rearrange("e p d -> p e d")
                                     ).then_inc(s_we, 16)
                for h in (0, 1):
                    sp.wait_ge(s_state[h], sum(n + 1 for _, n in REGION[:r + 1]))
                sp.dma_start(scr["m"][r].rearrange("(b p) x -> p b x", p=P),
                             state[:].rearrange("p a (b x) -> p (a b) x", b=B // 2)).then_inc(s_mout, 16)
                sp.wait_ge(s_mout, 16 * (r + 1))
                if r:
                    sp.wait_ge(s_te, 1)
                    sp.wait_ge(s_idx, 1)
                    sp.wait_ge(s_score, 1)
                for vh in (0, 1):
                    sp.dma_start(ch_m[r][vh * B * H:(vh + 1) * B * H].rearrange("l j c i -> l (j c i)"),
                                 scr["m"][r].rearrange("(l j) x -> l (j x)", j=HD)).then_inc(s_min, 16)
                sp.wait_ge(s_bc, r + 1)
                sp.dma_start(scr["b"][r].rearrange("(b p) x -> p b x", p=P),
                             ucopy.rearrange("p a (b x) -> p (a b) x", b=B // 2)).then_inc(s_bout, 16)
                sp.wait_ge(s_bout, 16 * (r + 1))
                for vh in (0, 1):
                    sp.dma_start(ch_b[r][vh * B * H:(vh + 1) * B * H].rearrange("l v c i -> l (v c i)"),
                                 scr["b"][r].rearrange("(l v) x -> l (v x)", v=HD)[:, vh * COLS:(vh + 1) * COLS]
                                 ).then_inc(s_bin, 16)
            for k in (0, 1):
                sp.sem_inc(s_ew[k], 16)
            sp.wait_ge(s_scat[OTHERS.name], 16 * OTHERS.n)
            pairs_in_out(sp, RUNS[0])
            run = RUNS[1]
            x_in, y_out = routed(run.t)

            def load_one(i):
                sp.wait_ge(s_et, i + run.g0)
                sp.dma_start(e_in[:, 0], x_in[:, bass.ds((i + run.first) * U, U), :]).then_inc(s_ei[0], 16)

            def store_one(i):
                sp.wait_ge(s_eo, i + (run.g0 + 2))
                sp.dma_start(y_out[:, bass.ds((i + run.first) * U, U), :], e_y[:, 0]).then_inc(s_ew[0], 16)

            load_one(0)
            load_one(1)
            with sp.Fori(2, run.n) as i:
                load_one(i)
                store_one(i - 2)
            store_one(run.n - 2)
            store_one(run.n - 1)
            sp.wait_ge(s_scat[MIXED.name], 16 * MIXED.n)
            pairs_in_out(sp, RUNS[2])
            n = 3 * SKIP
            last = N - ((C - 1) * ROWS - n)
            sp.wait_ge(s_fin, 1)
            for b in range(B):
                g0 = b * C
                sp.dma_start(out[b:b + 1, 1:ROWS - n, :], xf[g0:g0 + 1, n + 1:, :]).then_inc(s_out, 16)
                for q in (1, 2):
                    sp.dma_start(out[b, ROWS - n + q:(C - 1) * ROWS - n:3, :].rearrange("(g r) d -> g r d", r=L2),
                                 xf[g0 + 1:g0 + C - 1, q::3, :]).then_inc(s_out, 16)
                    sp.dma_start(out[b:b + 1, N - last + q:N:3, :],
                                 xf[g0 + C - 1:g0 + C, q:last:3, :]).then_inc(s_out, 16)
            for part, (lo, hi) in enumerate(PARTS):
                sp.wait_ge(s_fin, 2 + part)
                for b in range(B):
                    sp.dma_start(middle_rows(b)[:, lo:hi, :], xf[b * C + 1:b * C + C - 1, 3 * lo:3 * hi - 2:3, :]
                                 ).then_inc(s_out, 16)
            sp.wait_ge(s_out, 16 * 7 * B)
            sp.wait_ge(s_ends, 16 * 2 * B)
        @block.scalar
        def _(act):
            act.dma_start(cst[:], a["const"]).then_inc(s_cst, 16)
            for dst, src in ((wqkv[:, 0], "Wq"), (wqkv[:, 1], "Wk"), (wqkv[:, 2], "Wv"), (wgs[:], "Wg"),
                             (wlow[:, 0], "Wf1"), (wlow[:, 1], "Wo1"), (wup[:, 0], "Wf2"), (wup[:, 1], "Wo2"),
                             (wout[:], "Wout")):
                act.dma_start(dst, a[src]).then_inc(s_wa, 16)
            act.dma_start(lnw[:], a["ln_w"].rearrange("(p o) -> p o", o=1)).then_inc(s_wa, 16)
            for k, name in ((0, "w_gate"), (2, "w_up")):
                act.dma_start(wnat[:, k:k + 2], a[name].rearrange("(k p) d -> p k d", p=P)).then_inc(s_wf, 16)
            for k in (0, 1):
                act.dma_start(wnat[:, 4 + k], a["w_down"][:, k * P:(k + 1) * P]).then_inc(s_wf, 16)
            act.dma_start(wnat[0:E, 6], a["w_router"]).then_inc(s_wf, 16)
            act.wait_ge(s_wt, 1)
            S.activation(wlowT[:], bank[7][0:HD, 0:2 * P].rearrange("p (a b) -> p a b", a=2), ACT.Copy).then_inc(s_wtc, 1)
            act.wait_ge(s_wp, 1)
            S.activation(wfo[:], bank[7][:, 0:2 * D].rearrange("p (a b) -> p a b", a=2), ACT.Copy).then_inc(s_w, 1)
            act.wait_ge(s_wft, 1)
            S.activation(wT[:, 0:4], bank[6].rearrange("p (k x) -> p k x", k=4), ACT.Copy).then_inc(s_wfT, 1)
            S.activation(wT[:, 4:6], bank[7][:, 0:2 * P].rearrange("p (k x) -> p k x", k=2), ACT.Copy).then_inc(s_wfT, 1)
            S.activation(wrT[:], bank[7][:, 2 * P:2 * P + E], ACT.Copy).then_inc(s_wfT, 1)
            act.wait_ge(s_mv, NT)
            act.wait_ge(s_zero, 2)
            S.activation(rstd[:, 0:NT], mv[:, 0:NT, 1], ACT.Sqrt, bias=eps[:]).then_inc(s_sd, 1)
            act.wait_ge(s_mv, NT + L2)
            S.activation(rstd[:, NT:], mv[:, NT:, 1], ACT.Sqrt, bias=eps[:]).then_inc(s_sd, 1)

            def copy_xT(n):
                lo, hi = (GROUPS + QGROUPS)[n]
                act.wait_ge(s_tp, n + 1)
                S.activation(cols(xnT if n < NG else xaT, lo, hi), psum(n % 2, lo, hi), ACT.Copy).then_inc(s_xT, 1)

            def route_xT(t, g):
                lo, hi = t.groups[g]
                act.wait_ge(s_lt, GB[t.name] + g + 1)
                S.activation(xT_route(t, g), b_xT(t, g)[:, 0:(hi - lo) * P], ACT.Copy).then_inc(s_lx, 1)

            def logits_out(t):
                act.wait_ge(s_lg, 1 + (t is MIXED))
                S.activation(fb[t.name]["lg"], b_tok[:, 0:t.n * E], ACT.Copy).then_inc(s_flc, 1)

            def score(t):
                act.wait_ge(s_mx, 1 + (t is MIXED))
                S.activation(fb[t.name]["score"], fb[t.name]["mx"], ACT.Sigmoid).then_inc(s_score, 1)

            def row_std(t):
                q = fb[t.name]
                act.wait_ge(s_fmv, TB[t.name] + t.n)
                S.activation(q["rstd"][:], q["mv"][:, :, 1], ACT.Sqrt, bias=eps[:]).then_inc(s_fsd, 1)

            def norm_rows(t, dst, lo, hi, done):
                q = fb[t.name]
                for j in range(lo, hi):
                    S.activation(dst[j], xf[:, t.rows[j]], ACT.Identity, bias=q["shift"][:, j:j + 1],
                                 scale=q["rstd"][:, j:j + 1]).then_inc(done, 1)

            def evict(j):
                _, lo, hi, k, func = jobs[j]
                act.wait_ge(s_pj, j + 1)
                if k is None:
                    dst = cols(qT, lo - L1, hi - L1) if func == ACT.Silu else cols(gateT, lo, hi)
                else:
                    dst = slot(lo, hi, k)
                S.activation(dst, psum(2 + j % 4, lo, hi), func).then_inc(s_ev, 1)
                if k == K:
                    act.wait_ge(s_ev, j + 1)
                    S.activation(slot(lo, hi, PP), slot(lo, hi, K), ACT.Square).then_inc(s_sq, 1)

            for n in range(NTP):
                copy_xT(n)
                if 1 <= n <= NG:
                    evict(2 * n - 2)
                    evict(2 * n - 1)
            for j in range(2 * NG, NSILU):
                evict(j)
            row_std(OTHERS)
            act.wait_ge(s_ss, 1)
            S.activation(rk[:], bank[6], ACT.Sqrt).then_inc(s_no, 1)

            def spread_rk(g):
                lo, hi = GROUPS[g]
                act.wait_ge(s_rk, 1 + (g >= RK_FIRST))
                if g >= 2:
                    act.wait_ge(s_rb, g - 1)
                S.activation(at_group(rks, g).rearrange("p s (h i) -> p (s h) i", i=HD),
                             rk[:, lo * H:hi * H].unsqueeze(2).to_broadcast([P, (hi - lo) * H, HD]),
                             ACT.Copy).then_inc(s_rke, 1)

            for g in range(NG):
                evict(NSILU + 2 * g)
                evict(NSILU + 2 * g + 1)
                if g:
                    spread_rk(g - 1)
                if g < NOG:
                    if not g:
                        act.wait_ge(s_shift, 1)
                    norm_rows(OTHERS, early_rows, *OTHERS.groups[g], s_fn)
                if 1 <= g <= NOG:
                    route_xT(OTHERS, g - 1)
            spread_rk(NG - 1)
            for j in range(NJ - NQ, NJ):
                evict(j)
            def shared(t):
                for g, (lo, hi) in enumerate(t.groups):
                    n, w = GA[t.name] + g, (hi - lo) * P
                    if t is OTHERS:
                        act.wait_ge(s_ft, n + 1)
                        S.activation(xT_shared(t, g), b_xT(t, g)[:, 0:w], ACT.Copy).then_inc(s_fx, 1)
                    for k in (0, 1):
                        act.wait_ge(s_fgu, 2 * n + k + 1)
                        if n or k:
                            act.wait_ge(s_fh, 2 * n + k)
                        S.activation(f_silu[t.name][:, 0:w], b_gate[k][:, 0:w], ACT.Silu).then_inc(s_fsg, 1)
            act.sem_inc(s_uc[0], 1)
            act.sem_inc(s_uc[1], 1)
            for r, (_, n) in enumerate(REGION):
                base = r * L1
                with act.Fori(0, n) as i:
                    for h in (1, 0):
                        act.wait_ge(s_uterm[h], i + (base + 1))
                        act.wait_ge(s_bp[h], i + (base + 1))
                        S.activation(ucopy[:, h], bank[2 * h + 1], ACT.Copy).then_inc(s_uc[h], 1)
                for h in (0, 1):
                    act.wait_ge(s_bp[h], base + n + 1)
                act.wait_ge(s_bs, 2 * r + 2)
                S.activation(ucopy, ps[2][:], ACT.Copy).then_inc(s_bc, 1)
                if r == 0:
                    logits_out(OTHERS)
                    norm_rows(OTHERS, late, 0, OTHERS.n, s_late)
                    score(OTHERS)
                    act.wait_ge(s_bout, 16)
            act.wait_ge(s_bout, 32)
            def copy_x(run, i, k, b):
                act.wait_ge(s_et, i + (k + run.g0 + 1))
                S.activation(e_xT[:, b], b_x.rearrange("p (u d) -> p u d", u=U), ACT.Copy).then_inc(s_ex, 1)

            def silu(run, i, k, u, b):
                act.wait_ge(s_eg, i * U + ((k + run.g0) * U + u + 1))
                if type(i) is not int or i + k + run.g0:
                    act.wait_ge(s_eh, i * U + ((k + run.g0 - 1) * U + u + 1))
                S.activation(e_sg[:, u], b_gu(run, b)[u][:, 0:F], ACT.Silu).then_inc(s_es, 1)

            def copy_h(run, i, k):
                act.wait_ge(s_eht, i + (k + run.g0 + 1))
                S.activation(e_hT[:], b_h.rearrange("p (u x) -> p u x", u=U), ACT.Copy).then_inc(s_ehc, 1)

            def copy_y(run, i, k, b, written):
                act.wait_ge(s_ey, i + (k + run.g0 + 1))
                act.wait_ge(s_ew[b], written)
                S.activation(e_y[:, b], b_y(run).rearrange("p (u d) -> p u d", u=U), ACT.Copy).then_inc(s_eo, 1)

            def pairs(run):
                def pair(i, k, ahead):
                    if ahead:
                        silu(run, i, k + 1, 0, (k + 1) % 2)
                    copy_h(run, i, k)
                    if ahead:
                        silu(run, i, k + 1, 1, (k + 1) % 2)
                    if ahead > 1:
                        copy_x(run, i, k + 2, k % 2)
                    copy_y(run, i, k, k % 2, i * 8 + 16 * (k // 2 + 1 + run.base[k % 2]))

                copy_x(run, 0, 0, 0)
                copy_x(run, 0, 1, 1)
                for u in range(U):
                    silu(run, 0, 0, u, 0)
                over_pairs(act, run, pair)

            act.sem_inc(s_eo, 1)
            shared(OTHERS)
            pairs(RUNS[0])
            turn = act.alloc_register("turn_act")
            run = RUNS[1]

            def v_term(i, h):
                act.wait_ge(s_red[h], i + NT)
                tile = i + L1
                if h and type(i) is not int:
                    act.reg_add(turn, turn, 1)
                    tile = act.snap(turn, min_val=L1, max_val=NT - 1)
                for v in range(4):
                    ins = S.activation(vterm[:, h].rearrange("p (x v) -> p x v", v=4)[:, :, v],
                                       steps[:, bass.ds(tile, 1), VV, :].rearrange("p a x -> p (a x)"),
                                       ACT.Copy, scale=c["diag8"][:, 4 * h + v:4 * h + v + 1])
                ins.then_inc(s_vd[h], 1)

            def step(i, begins, ends, more=True):
                if ends:
                    for u in range(U):
                        silu(run, i, -2, u, 0)
                v_term(i, 1)
                if begins:
                    copy_x(run, i, -1, 0)
                if ends:
                    copy_h(run, i, -2)
                if more:
                    v_term(i + 1, 0)
                if ends:
                    copy_y(run, i, -2, 0, i * 16 + 16 * (run.base[0] - 1))

            v_term(0, 0)
            step(0, False, False)
            step(1, True, False)
            act.reg_mov(turn, L1 + 1)
            with act.Fori(2, run.n + 1) as i:
                step(i, True, True)
            step(run.n + 1, False, True)
            if run.n + 2 < L2:
                act.reg_mov(turn, L1 + run.n + 1)
                with act.Fori(run.n + 2, L2 - 1) as i:
                    step(i, False, False)
                step(L2 - 1, False, False, more=False)
            S.activation(rstd2[:, 0:1], eps[:], ACT.Sqrt)
            for g, (lo, hi) in enumerate(QGROUPS):
                act.wait_ge(s_od, g + 1)
                S.activation(osq[:, lo * P:hi * P], od[:, lo * P:hi * P], ACT.Square).then_inc(s_osq, 1)
            act.wait_ge(s_var, 1)
            S.activation(rstd2[:], bank[3][:, 0:L2], ACT.Sqrt, bias=eps[:]).then_inc(s_sd2, 1)

            row_std(MIXED)
            for g in range(len(MIXED.groups)):
                route_xT(MIXED, g)
            logits_out(MIXED)
            score(MIXED)
            act.wait_ge(s_score, 2)
            q = fb[MIXED.name]
            for j in range(MIXED.n):
                S.activation(q["scaled"][j], q["rows"][j], ACT.Copy, scale=q["score"][:, j:j + 1]).then_inc(s_sc, 1)
            shared(MIXED)
            pairs(RUNS[2])
            n = 3 * SKIP
            last = N - ((C - 1) * ROWS - n)
            act.wait_ge(s_fin, 3)
            for b in range(B):
                g0 = b * C
                act.dma_start(out[b:b + 1, 0:1, :], xf[g0:g0 + 1, n:n + 1, :]).then_inc(s_ends, 16)
                act.dma_start(out[b:b + 1, N - last:N:3, :], xf[g0 + C - 1:g0 + C, 0:last:3, :]).then_inc(s_ends, 16)

        def pool_tt(dst, src, tile, k, h, w):
            tile = G.snap(tile)
            return G.tensor_tensor(wide(dst, w), wide(src, w), per_col(tile, k, 1, h, w), ALU.mult)

        @block.gpsimd
        def _(pool):
            G.memset(zeros[:], 0.0).then_inc(s_zero, 1)
            G.memset(eps[:], LN_EPS).then_inc(s_zero, 1)
            G.memset(xf[:], 0.0).then_inc(s_xfz, 1)
            pool.wait_ge(s_wa, 160)
            G.tensor_copy(wge[:].rearrange("p (h i) -> p h i", i=HD),
                          wgs[:].unsqueeze(2).to_broadcast([P, H, HD])).then_inc(s_wge, 1)
            def scatter_tile(t, j):
                q = fb[t.name]
                pool.wait_ge(s_sc, TB[t.name] + j + 1)
                G.indirect_dma_start(xs[t.name], bass.IndirectOffsetOnAxis(ap=q["idx"][:, j:j + 1].bitcast(U32), axis=0),
                                     q["scaled"][j], None).then_inc(s_scat[t.name], 16)

            def scatter(t):
                pool.wait_ge(s_xz, 64)
                pool.wait_ge(s_idx, 1 + (t is MIXED))
                for j in range(t.n):
                    scatter_tile(t, j)

            def gather(t, pairs):
                q = fb[t.name]
                for k in (0, 1):
                    pool.wait_ge(s_ew[k], 16 * (pairs[k] + 1))
                for j in range(t.n):
                    G.indirect_dma_start(q["back"][:, j * D:(j + 1) * D], None, ys[t.name],
                                         bass.IndirectOffsetOnAxis(ap=q["idx"][:, j:j + 1].bitcast(U32), axis=0)
                                         ).then_inc(s_gat[t.name][int(t is MIXED and j >= PARTS[1][0])], 16)


            def last_p(g):
                lo, hi = GROUPS[g]
                pool.wait_ge(s_m, g + 1)
                G.tensor_tensor(slot(lo, hi, PP), slot(lo, hi, PP), slot(lo, hi, Y), ALU.add).then_inc(s_p, 1)

            for g, (lo, hi) in enumerate(GROUPS):
                pool.wait_ge(s_k, g + 1)
                pool.wait_ge(s_ev, NSILU + 2 * g + 2)
                if g >= 2:
                    pool.wait_ge(s_y, g - 1)
                G.tensor_tensor(at_group(fk_at, g), slot(lo, hi, FF), slot(lo, hi, K), ALU.mult).then_inc(s_fk, 1)
                pool.wait_ge(s_fk, g + 1)
                G.tensor_tensor(at_group(fkk_at, g), at_group(fk_at, g), slot(lo, hi, K), ALU.mult).then_inc(s_fkk, 1)
                if g >= 2:
                    last_p(g - 2)
            last_p(NG - 2)
            last_p(NG - 1)
            for h in (0, 1):
                pool.sem_inc(s_bp[h], 1)
            for r, (_, n) in enumerate(REGION):
                base = r * L1
                last = base + n - 1

                def decay(h, tile, ready):
                    pool.wait_ge(s_state[h], ready)
                    pool_tt(decayed[:, h], state[:, h], tile, FF, h, HD).then_inc(s_dec[h], 1)

                def v_times_u(h, tile, n):
                    pool.wait_ge(s_uc[h], n + 1)
                    pool.wait_ge(s_ba[h], n)
                    pool_tt(vterm[:, h], ucopy[:, h], tile, VV, h, HD).then_inc(s_bp[h], 1)

                def add_u_term(h, step):
                    pool.wait_ge(s_uterm[h], step)
                    G.tensor_tensor(decayed[:, h], decayed[:, h], work[:, h, 1], ALU.add).then_inc(s_add[h], 1)

                for h in (1, 0):
                    decay(h, last, base + r + 1)
                with pool.Fori(1, n) as i:
                    for h in (1, 0):
                        pool.wait_ge(s_dec[h], i + base)
                        add_u_term(h, i + base)
                    for h in (1, 0):
                        v_times_u(h, (i * -1) + (last + 1), i + base)
                    for h in (1, 0):
                        decay(h, (i * -1) + last, i + (base + r + 1))
                for h in (1, 0):
                    pool.wait_ge(s_dec[h], base + n)
                    add_u_term(h, base + n)
                for h in (1, 0):
                    v_times_u(h, base, base + n)
            first = NT + 2
            pool.wait_ge(s_xz, 64)
            pool.wait_ge(s_idx, 1)
            for m in range(1, 2 * C):
                r, i = (m - 1) // C, (m - 1) % C
                pool.wait_ge(s_bin, 32 * (r + 1))
                if m > 2:
                    pool.wait_ge(s_ca, m - 2 + (m - 3) // C + 1)
                G.tensor_copy(ch_pr[:, m % 2, :, :, HD], ch_b[r][:, :, i, :]).then_inc(s_cb, 1)
                if m <= OTHERS.n:
                    scatter_tile(OTHERS, m - 1)
            pool.wait_ge(s_ca, 2 * C + 1)
            pool.wait_ge(s_mout, 32)
            G.dma_start(scr["s"].rearrange("(l i) x -> l i x", i=HD),
                        ch_s[:, :, 0:C, :].rearrange("l i c v -> l i (c v)")).then_inc(s_sout, 16)
            pool.wait_ge(s_sout, 16)
            pool.wait_ge(s_scat[OTHERS.name], 16 * OTHERS.n)
            G.dma_start(state[:].rearrange("p v (b x) -> p (v b) x", b=B),
                        scr["s"].rearrange("(g q) x -> q g x", q=P)).then_inc(s_chout, 16)
            turn = pool.alloc_register("turn_pool")
            pool.wait_ge(s_scat[OTHERS.name], 16 * OTHERS.n)
            for h in (0, 1):
                pool.sem_inc(s_q[h], 1)
            pool.reg_mov(turn, L1 - 1)
            with pool.Fori(0, L2) as i:
                tile = i + L1
                for h in (0, 1):
                    pool.wait_ge(s_state[h], i + (first + 1))
                    if h:
                        pool.reg_add(turn, turn, 1)
                        tile = pool.snap(turn, min_val=L1, max_val=NT - 1)
                    pool_tt(decayed[:, h], state[:, h], tile, FF, h, 4).then_inc(s_dec[h], 1)
                for h in (0, 1):
                    pool.wait_ge(s_state[h], i + (first + 2))
                    G.tensor_tensor(qs[:, bass.ds(i, 1), h].rearrange("p s x v -> p (s x) v"),
                                    state[:, h].rearrange("p (x v) -> p x v", v=4),
                                    qT[:, bass.ds(G.snap(i * P), P)].unsqueeze(2).to_broadcast([P, P, 4]),
                                    ALU.mult).then_inc(s_q[h], 1)
            pool.wait_ge(s_o, NQ)
            gather(OTHERS, RUNS[2].base)
            scatter(MIXED)
            pool.wait_ge(s_fa, GA[MIXED.name] + len(MIXED.groups))
            m = RUNS[2].n
            gather(MIXED, (RUNS[2].base[0] + (m + 1) // 2, RUNS[2].base[1] + m // 2))

        @block.vector
        def _(dve):
            chained = [0]

            def link(ins):
                chained[0] += 1
                ins.then_inc(s_link, 1)
                dve.wait_ge(s_link, chained[0])

            def row_stats(t):
                q, t0 = fb[t.name], TB[t.name]
                if t is MIXED:
                    dve.wait_ge(s_x1, L2)
                for j, row in enumerate(t.rows):
                    V.bn_stats(q["stats"][:, j], xf[:, row]).then_inc(s_fst, 1)
                for j in range(t.n):
                    dve.wait_ge(s_fst, t0 + j + 1)
                    V.bn_aggr(q["mv"][:, j], q["stats"][:, j]).then_inc(s_fmv, 1)

            def row_norm(t):
                q, m = fb[t.name], t is MIXED
                dve.wait_ge(s_fsd, 1 + m)
                V.reciprocal(q["rstd"][:], q["rstd"][:]).then_inc(s_frs, 1)
                dve.wait_ge(s_frs, 1 + m)
                for j, row in enumerate(t.rows):
                    V.tensor_scalar(q["rows"][j], xf[:, row], q["mv"][:, j, 0:1], q["rstd"][:, j:j + 1], ALU.subtract,
                                    ALU.mult).then_inc(s_fn, 1)

            def route(t):
                q, m = fb[t.name], t is MIXED
                dve.wait_ge(s_flc, 1 + m)
                ne = lambda ap: ap.rearrange("p (n e) -> p n e", e=E)
                en = lambda ap: ap.rearrange("p (e n) -> p e n", e=E)
                lg, oh = ne(q["lg"]), ne(q["oh"])
                r_tot, r_inc, r_a, r_keep = (q[k] for k in ("r_tot", "r_inc", "r_a", "r_keep"))
                r_nt, r_ti, r_ts, r_one = (q[k] for k in ("r_nt", "r_ti", "r_ts", "r_one"))
                ranks, totals = b_rank[t.name]
                full, w = [P, t.n, E], t.n * E
                V.tensor_reduce(q["mx"], lg, AX.X, ALU.max).then_inc(s_mx, 1)
                dve.wait_ge(s_mx, 1 + m)
                link(V.tensor_tensor(oh, lg, q["mx"].unsqueeze(2).to_broadcast(full), ALU.is_equal))
                prefer = c["prefer"].unsqueeze(1).to_broadcast(full)
                link(V.tensor_tensor(oh, oh, prefer, ALU.mult))
                link(V.tensor_reduce(q["mw"], oh, AX.X, ALU.max))
                link(V.tensor_tensor(oh, prefer, q["mw"].unsqueeze(2).to_broadcast(full), ALU.is_equal))
                V.tensor_tensor(oh, oh, c["valid_" + t.name].unsqueeze(2).to_broadcast(full), ALU.mult).then_inc(s_oh, 1)
                V.memset(r_one, 1.0).then_inc(s_link, 1)
                V.memset(r_keep, 1.0).then_inc(s_link, 1)
                chained[0] += 2
                dve.wait_ge(s_link, chained[0])
                link(V.memset(en(r_keep)[:, :, 0:1], 0.0))
                dve.wait_ge(s_rank, 1 + m)
                link(V.tensor_copy(en(r_tot), totals[:, 0:w].rearrange("p (n e) -> p e n", e=E)))
                link(V.tensor_tensor_scan(r_inc, r_keep, r_tot, 0.0, ALU.mult, ALU.add))
                link(V.tensor_tensor(en(r_a), c["steps128"][:, 0:t.n].unsqueeze(1).to_broadcast([P, E, t.n]),
                                     en(r_inc)[:, :, t.n - 1:t.n].to_broadcast([P, E, t.n]), ALU.is_lt))
                link(V.tensor_reduce(r_nt, en(r_a), AX.X, ALU.add))
                link(V.tensor_tensor_scan(r_ti, r_one, r_nt, 0.0, ALU.mult, ALU.add))
                link(V.tensor_tensor(r_ts, r_ti, r_nt, ALU.subtract))
                if m:
                    shared_h(t, 0, 0)
                    shared_h(t, 0, 1)
                link(V.tensor_tensor(r_inc, r_inc, r_tot, ALU.subtract))
                link(V.scalar_tensor_tensor(en(r_inc), r_ts.unsqueeze(2).to_broadcast([P, E, t.n]), float(P), en(r_inc),
                                            ALU.mult, ALU.add))
                link(V.tensor_tensor(ne(r_a), ranks[:, 0:w].rearrange("p (n e) -> p n e", e=E),
                                     en(r_inc).rearrange("p e n -> p n e"), ALU.add))
                link(V.tensor_tensor(ne(r_a), ne(r_a), oh, ALU.mult))
                link(V.tensor_reduce(q["slot"], ne(r_a), AX.X, ALU.add))
                V.tensor_tensor(q["idx"][:], q["slot"], c["spare_" + t.name], ALU.add).then_inc(s_idx, 1)
                te = q["r_te"][0:1].rearrange("p (m e) -> p m e", e=E)
                link(V.tensor_tensor(te, r_ti[0:1].unsqueeze(1).to_broadcast([1, t.tiles, E]),
                                     c["tileno"][0:1, 0:t.tiles].unsqueeze(2).to_broadcast([1, t.tiles, E]), ALU.is_le))
                link(V.tensor_reduce(q["r_tf"][0:1], te, AX.X, ALU.add))
                V.tensor_scalar(q["te"][:].rearrange("p (m u) -> p m u", u=4)[:, :, 0:U],
                                q["r_tf"][0:1].rearrange("p (m u) -> p m u", u=U), float(E - 1), None, ALU.min
                                ).then_inc(s_te, 1)

            def shared_h(t, g, k):
                lo, hi = t.groups[g]
                n, w = GA[t.name] + g, (hi - lo) * P
                dve.wait_ge(s_fsg, 2 * n + k + 1)
                if n and not k:
                    dve.wait_ge(s_fy, n)
                V.tensor_tensor(f_h[t.name][:, k, 0:w], f_silu[t.name][:, 0:w], b_up[k][:, 0:w], ALU.mult).then_inc(s_fh, 1)

            def shared_add(t, g):
                lo, hi = t.groups[g]
                dve.wait_ge(s_fy, GA[t.name] + g + 1)
                V.tensor_tensor(rows_of(xf, t, lo, hi), rows_of(xf, t, lo, hi), tiles_of(b_tok[:, 0:(hi - lo) * D], t),
                                ALU.add).then_inc(s_fa, 1)

            def gate(run, i, k, b):
                if type(i) is not int or i + k + run.g0:
                    dve.wait_ge(s_eht, i + (k + run.g0))
                for u in range(U):
                    dve.wait_ge(s_es, i * U + ((k + run.g0) * U + u + 1))
                    V.tensor_tensor(e_h[:, u], e_sg[:, u], b_gu(run, b)[u][:, F:], ALU.mult).then_inc(s_eh, 1)

            dve.wait_ge(s_x, 16 * 2 * B)
            for s in range(NT):
                V.bn_stats(stats[:, s], xr[:, s]).then_inc(s_st, 1)
            for s in range(NT):
                dve.wait_ge(s_st, s + 1)
                V.bn_aggr(mv[:, s], stats[:, s]).then_inc(s_mv, 1)
            dve.wait_ge(s_xf, 16 * 3 * B)
            for s in range(L2):
                V.bn_stats(stats[:, NT + s], xf[:, 3 * s]).then_inc(s_st, 1)
            for s in range(L2):
                dve.wait_ge(s_st, NT + s + 1)
                V.bn_aggr(mv[:, NT + s], stats[:, NT + s]).then_inc(s_mv, 1)
            dve.wait_ge(s_sd, 1)
            V.reciprocal(rstd[:, 0:NT], rstd[:, 0:NT]).then_inc(s_rs, 1)
            dve.wait_ge(s_rs, 1)
            for s in range(NT):
                V.tensor_scalar(xr[:, s], xr[:, s], mv[:, s, 0:1], rstd[:, s:s + 1], ALU.subtract,
                                ALU.mult).then_inc(s_xn, 1)
            dve.wait_ge(s_sd, 2)
            V.reciprocal(rstd[:, NT:], rstd[:, NT:]).then_inc(s_rs, 1)
            dve.wait_ge(s_rs, 2)
            for s in range(L2):
                V.tensor_scalar(xa[:, s], xf[:, 3 * s], mv[:, NT + s, 0:1], rstd[:, NT + s:NT + s + 1],
                                ALU.subtract, ALU.mult).then_inc(s_xn, 1)
            row_stats(OTHERS)
            dve.wait_ge(s_fsd, 1)
            q = fb[OTHERS.name]
            V.reciprocal(q["rstd"][:], q["rstd"][:]).then_inc(s_frs, 1)
            dve.wait_ge(s_frs, 1)
            V.scalar_tensor_tensor(q["shift"], q["mv"][:, :, 0], -1.0, q["rstd"][:], ALU.mult, ALU.mult
                                   ).then_inc(s_shift, 1)
            dve.wait_ge(s_no, 1)
            V.tensor_scalar(rk[:], rk[:], NORM_EPS, None, ALU.max).then_inc(s_nm, 1)
            dve.wait_ge(s_nm, 1)
            first = GROUPS[RK_FIRST][0] * H
            V.reciprocal(rk[:, 0:first], rk[:, 0:first]).then_inc(s_rk, 1)
            V.reciprocal(rk[:, first:], rk[:, first:]).then_inc(s_rk, 1)

            def y_and_p(g):
                lo, hi = GROUPS[g]
                dve.wait_ge(s_c, g + 1)
                V.tensor_tensor(slot(lo, hi, PP), slot(lo, hi, Y), psum(1, lo, hi), ALU.mult).then_inc(s_gc, 1)
                V.tensor_tensor(at_group(gk_at, g), slot(lo, hi, Y), slot(lo, hi, K), ALU.mult).then_inc(s_gk, 1)
                dve.wait_ge(s_gk, g + 1)
                dve.wait_ge(s_gc, g + 1)
                V.scalar_tensor_tensor(slot(lo, hi, Y), at_group(fk_at, g), -1.0, slot(lo, hi, Y), ALU.mult,
                                       ALU.mult).then_inc(s_y, 1)
                V.tensor_tensor(slot(lo, hi, PP), slot(lo, hi, PP), at_group(gk_at, g), ALU.mult).then_inc(s_m, 1)

            for g, (lo, hi) in enumerate(GROUPS):
                dve.wait_ge(s_rb, g + 1)
                V.tensor_tensor(slot(lo, hi, K), slot(lo, hi, K), psum(0, lo, hi), ALU.mult).then_inc(s_k, 1)
                if g >= 2:
                    y_and_p(g - 2)
            y_and_p(NG - 2)
            y_and_p(NG - 1)

            def products(h, tile, ready, w):
                dve.wait_ge(s_state[h], ready)
                st = state[:, h].unsqueeze(1).to_broadcast([P, 2, HALF]).rearrange("p e (x w) -> p e x w", w=w)
                V.tensor_tensor(work[:, h].rearrange("p e (x w) -> p e x w", w=w), st, per_col(tile, Y, 2, h, w),
                                ALU.mult).then_inc(s_prod[h], 1)

            def update(h, tile, done, w, used=None):
                dve.wait_ge(s_red[h], done)
                V.tensor_tensor(work[:, h].rearrange("p e (x w) -> p e x w", w=w),
                                ps[h][:].rearrange("p e (x w) -> p e x w", w=w), per_col(tile, K, 2, h, w),
                                ALU.mult).then_inc(s_term[h], 1)
                dve.wait_ge(s_term[h], done)
                dve.wait_ge(s_dec[h], done)
                V.tensor_tensor(decayed[:, h], decayed[:, h], work[:, h, 1], ALU.add).then_inc(s_add[h], 1)
                dve.wait_ge(s_add[h], done)
                if used is not None:
                    dve.wait_ge(s_q[h], used)
                V.tensor_tensor(state[:, h], decayed[:, h], work[:, h, 0], ALU.add).then_inc(s_state[h], 1)

            for r, (first, n) in enumerate(REGION):
                base = r * L1
                if r:
                    route(OTHERS)
                    dve.wait_ge(s_mout, 16)
                else:
                    dve.wait_ge(s_p, NG)
                for h in (0, 1):
                    V.tensor_copy(state[:, h].rearrange("p (x w) -> p x w", w=HD),
                                  c["diag8"].unsqueeze(1).to_broadcast([P, P // 2, HD])).then_inc(s_state[h], 1)
                last = base + n - 1
                r0 = base + r + 1

                def term(h, e, tile, step):
                    dve.wait_ge((s_red, s_usum)[e][h], step)
                    V.tensor_tensor(wide(work[:, h, e], HD), wide(ps[h][:, e], HD), per_col(tile, K + e, 1, h, HD),
                                    ALU.mult).then_inc((s_term, s_uterm)[e][h], 1)

                def next_state(h, step):
                    dve.wait_ge(s_term[h], step)
                    dve.wait_ge(s_add[h], step)
                    V.tensor_tensor(state[:, h], decayed[:, h], work[:, h, 0], ALU.add).then_inc(s_state[h], 1)

                def terms(tile, step):
                    for h in (1, 0):
                        term(h, 1, tile, step)
                        term(h, 0, tile, step)

                for h in (1, 0):
                    products(h, last, r0, HD)
                with dve.Fori(1, n) as i:
                    tile = (i * -1) + last
                    terms(tile + 1, i + base)
                    for h in (1, 0):
                        next_state(h, i + base)
                        products(h, tile, i + r0, HD)
                terms(base, base + n)
                for h in (1, 0):
                    next_state(h, base + n)
            dve.wait_ge(s_score, 1)
            dve.wait_ge(s_late, OTHERS.n)
            dve.wait_ge(s_bs, 4)
            for h in (0, 1):
                dve.wait_ge(s_state[h], NT + 2)
            q = fb[OTHERS.name]
            for j in range(OTHERS.n):
                if j == 4 * HALF // D:
                    dve.wait_ge(s_mout, 32)
                V.tensor_scalar(q["scaled"][j], q["shared"][j], q["score"][:, j:j + 1], None, ALU.mult
                                ).then_inc(s_sc, 1)
            def beside(m):
                if 0 <= m < SHARED_EVERY * NOG:
                    g, at = m // SHARED_EVERY, m % SHARED_EVERY
                    if at in (0, 1):
                        shared_h(OTHERS, g, at)
                    elif at == 3:
                        shared_add(OTHERS, g)
                elif (m - PAIRS_FROM) % PAIR_EVERY == 0 and 0 <= (m - PAIRS_FROM) // PAIR_EVERY < BESIDE:
                    k = (m - PAIRS_FROM) // PAIR_EVERY
                    gate(RUNS[0], 0, k, k % 2)

            V.memset(ch_s[:, :, 0, :], 0.0).then_inc(s_ca, 1)
            for h in (0, 1):
                dve.wait_ge(s_uc[h], NT + 1)
            for r, n in ((0, C), (1, C - 1)):
                dve.wait_ge(s_min, 32 * (r + 1))
                dve.wait_ge(s_bin, 32 * (r + 1))
                if r:
                    dve.wait_ge(s_ca, C + 1)
                    V.tensor_copy(ch_s[:, :, 0, :], ch_s[:, :, C, :]).then_inc(s_ca, 1)
                for i in range(n):
                    m = r * C + i + 1
                    dve.wait_ge(s_ca, m + r)
                    V.tensor_tensor(ch_pr[:, m % 2, :, :, 0:HD], ch_m[r][:, :, i, :].rearrange("p j i -> p i j").unsqueeze(1)
                                    .to_broadcast([P, 4, HD, HD]), ch_s[:, :, i, :].rearrange("p j v -> p v j")
                                    .unsqueeze(2).to_broadcast([P, 4, HD, HD]), ALU.mult).then_inc(s_cm, 1)
                    dve.wait_ge(s_cm, m)
                    dve.wait_ge(s_cb, m)
                    V.tensor_reduce(ch_s[:, :, i + 1, :].rearrange("p i v -> p v i"), ch_pr[:, m % 2], AX.X,
                                    ALU.add).then_inc(s_ca, 1)
                    beside(m - BEGIN)
            for k in range((2 * C - 1 - BEGIN - PAIRS_FROM) // PAIR_EVERY + 1, BESIDE):
                gate(RUNS[0], 0, k, k % 2)
            dve.wait_ge(s_chout, 16)
            for h in (0, 1):
                dve.sem_inc(s_state[h], 1)
            r0 = NT + 3
            products(0, L1, r0, 4)
            products(1, L1, r0, 4)
            update(0, L1, NT + 1, 4)

            def step(i, ends):
                products(0, i + L1, i + r0, 4)
                update(1, i + (L1 - 1), i + NT, 4, i)
                if ends:
                    gate(RUNS[1], i, -2, 0)
                products(1, i + L1, i + r0, 4)
                update(0, i + L1, i + (NT + 1), 4, i + 1)

            step(1, False)
            with dve.Fori(2, RUNS[1].n + 2) as i:
                step(i, True)
            if RUNS[1].n + 2 < L2:
                with dve.Fori(RUNS[1].n + 2, L2) as i:
                    step(i, False)
            update(1, NT - 1, NT + L2, 4, L2)
            for g, (lo, hi) in enumerate(QGROUPS):
                dve.wait_ge(s_o, g + 1)
                if g == 0:
                    dve.wait_ge(s_state[0], NT + 3 + L2)
                    dve.wait_ge(s_state[1], NT + 3 + L2)
                V.tensor_tensor(cols(og, lo, hi), psum(4 + g, lo, hi), cols(gateT, lo, hi), ALU.mult).then_inc(s_og, 1)
            for g, (lo, hi) in enumerate(QGROUPS):
                dve.wait_ge(s_mu, g + 1)
                V.tensor_tensor(cols(od, lo, hi), cols(og, lo, hi), psum(g, lo, hi), ALU.subtract).then_inc(s_od, 1)
            for g, (lo, hi) in enumerate(QGROUPS):
                dve.wait_ge(s_osq, g + 1)
                V.tensor_scalar(cols(od, lo, hi), cols(od, lo, hi), lnw[:], None, ALU.mult).then_inc(s_dw, 1)
            dve.wait_ge(s_sd2, 1)
            V.reciprocal(rstd2[:], rstd2[:]).then_inc(s_rs2, 1)
            dve.wait_ge(s_rs2, 1)
            for g, (lo, hi) in enumerate(QGROUPS):
                dve.wait_ge(s_at, g + 1)
                for s in range(lo, hi):
                    V.scalar_tensor_tensor(xf[:, 3 * s], psum(4 + g, lo, hi)[:, s - lo], rstd2[:, s:s + 1], xf[:, 3 * s],
                                           ALU.mult, ALU.add).then_inc(s_x1, 1)
            row_stats(MIXED)
            row_norm(MIXED)
            route(MIXED)
            shared_add(MIXED, 0)
            for g in range(1, len(MIXED.groups)):
                for k in (0, 1):
                    shared_h(MIXED, g, k)
                shared_add(MIXED, g)
            dve.wait_ge(s_gat[OTHERS.name][0], 16 * OTHERS.n)
            V.tensor_tensor(rows_of(xf, OTHERS, 0, OTHERS.n), rows_of(xf, OTHERS, 0, OTHERS.n),
                            tiles_of(fb[OTHERS.name]["back"], OTHERS), ALU.add).then_inc(s_fin, 1)
            gate(RUNS[2], 0, 0, 0)

            def pair(i, k, ahead):
                if ahead:
                    gate(RUNS[2], i, k + 1, (k + 1) % 2)

            over_pairs(dve, RUNS[2], pair)
            for part, (lo, hi) in enumerate(PARTS):
                dve.wait_ge(s_gat[MIXED.name][part], 16 * (hi - lo))
                V.tensor_tensor(rows_of(xf, MIXED, lo, hi), rows_of(xf, MIXED, lo, hi),
                                tiles_of(fb[MIXED.name]["back"][:, lo * D:hi * D], MIXED), ALU.add).then_inc(s_fin, 1)

        @block.tensor
        def _(pe):
            pe.wait_ge(s_cst, 16)
            pe.wait_ge(s_wa, 160)
            for k in (0, 1):
                ins = T.transpose(bank[7][0:HD, k * P:(k + 1) * P], wlow[:, k], c["ident"])
            ins.then_inc(s_wt, 1)
            pe.wait_ge(s_wtc, 1)
            for k in (0, 1):
                ins = T.matmul(bank[7][:, k * D:(k + 1) * D], wlowT[:, k], wup[:, k], start=True, stop=True)
            ins.then_inc(s_wp, 1)
            pe.wait_ge(s_wf, 80)
            pe.wait_ge(s_w, 1)
            for k in range(4):
                T.transpose(bank[6][:, k * P:(k + 1) * P], wnat[:, k], c["ident"])
            for k in range(2):
                T.transpose(bank[7][:, k * P:(k + 1) * P], wnat[:, 4 + k], c["ident"])
            T.transpose(bank[7][:, 2 * P:2 * P + E], wnat[0:E, 6], c["ident"][0:E, 0:E]).then_inc(s_wft, 1)
            def transposes_x(n):
                lo, hi = (GROUPS + QGROUPS)[n]
                pe.wait_ge(s_xn, hi + (NT if n >= NG else 0))
                if n >= 2:
                    pe.wait_ge(s_xT, n - 1)
                for s in range(lo, hi):
                    src = xr[:, s] if n < NG else xa[:, s]
                    ins = T.transpose(bank[n % 2][:, (s - lo) * P:(s - lo + 1) * P], src, c["ident"])
                ins.then_inc(s_tp, 1)

            def route_transposes(t, g):
                lo, hi = t.groups[g]
                pe.wait_ge(s_fn, TB[t.name] + hi)
                for j in range(lo, hi):
                    ins = T.transpose(b_xT(t, g)[:, (j - lo) * P:(j - lo + 1) * P], fb[t.name]["rows"][j], c["ident"])
                ins.then_inc(s_lt, 1)

            def logits(t, g):
                lo, hi = t.groups[g]
                pe.wait_ge(s_lx, GB[t.name] + g + 1)
                for j in range(lo, hi):
                    ins = T.matmul(b_tok[:, j * E:(j + 1) * E], xT_route(t, g)[:, (j - lo) * P:(j - lo + 1) * P],
                                   wrT[:], start=True, stop=True)
                if g == len(t.groups) - 1:
                    ins.then_inc(s_lg, 1)

            def rank(t):
                pe.wait_ge(s_oh, 1 + (t is MIXED))
                pe.wait_ge(s_flc, 1 + (t is MIXED))
                ranks, totals = b_rank[t.name]
                T.matmul(ranks[:, 0:t.n * E], c["before"], fb[t.name]["oh"], start=True, stop=True)
                T.matmul(totals[:, 0:t.n * E], c["ones"], fb[t.name]["oh"], start=True, stop=True).then_inc(s_rank, 1)

            def project(j):
                w, lo, hi, k, func = jobs[j]
                if j >= 4:
                    pe.wait_ge(s_ev, j - 3)
                src = xaT if k is None and func == ACT.Sigmoid else xnT
                T.matmul(bank[2 + j % 4][:, 0:(hi - lo) * P], w, src[:, lo * P:hi * P],
                         start=True, stop=True).then_inc(s_pj, 1)

            def head_sum(g):
                lo, hi = GROUPS[g]
                pe.wait_ge(s_fkk, g + 1)
                if g:
                    pe.wait_ge(s_gc, g)
                T.matmul(bank[1][:, 0:(hi - lo) * P], c["block"], fkk_at[:, g % 2, 0:(hi - lo) * P],
                         start=True, stop=True).then_inc(s_c, 1)

            def square_sums(g):
                lo, hi = GROUPS[g]
                pe.wait_ge(s_sq, g + 1)
                for s in range(lo, hi):
                    ins = T.matmul(bank[6][:, s * H:(s + 1) * H], steps[:, s, PP], c["heads"], start=True, stop=True)
                if g == NG - 1:
                    ins.then_inc(s_ss, 1)

            def spread_rk(g):
                lo, hi = GROUPS[g]
                pe.wait_ge(s_rke, g + 1)
                if g:
                    pe.wait_ge(s_k, g)
                for s in range(lo, hi):
                    ins = T.matmul(bank[0][:, (s - lo) * P:(s - lo + 1) * P], rks[:, g % 2, (s - lo) * P:(s - lo + 1) * P],
                                   c["ident"], start=True, stop=True)
                ins.then_inc(s_rb, 1)

            for n in range(NTP):
                transposes_x(n)
                if n == 1:
                    pe.wait_ge(s_wge, 1)
                    pe.wait_ge(s_wfT, 3)
                if 1 <= n <= NG:
                    pe.wait_ge(s_xT, n)
                    project(2 * n - 2)
                    project(2 * n - 1)
                if 2 <= n <= NG + 1:
                    square_sums(n - 2)
            pe.wait_ge(s_xT, NTP)
            for j in range(2 * NG, NSILU):
                project(j)
            for g in range(NG):
                project(NSILU + 2 * g)
                project(NSILU + 2 * g + 1)
                if 2 <= g < NOG + 2:
                    logits(OTHERS, g - 2)
                if 1 <= g <= NOG:
                    if g == 1:
                        pe.wait_ge(s_no, 1)
                    route_transposes(OTHERS, g - 1)
                if g:
                    spread_rk(g - 1)
                if g >= 3:
                    head_sum(g - 3)
            assert NOG + 2 == NG
            for j in range(NJ - NQ, NJ):
                project(j)
            spread_rk(NG - 1)
            for g in range(NG - 3, NG):
                head_sum(g)
            pe.wait_ge(s_ev, NJ)

            def shared(t):
                def transposes(g):
                    lo, hi = t.groups[g]
                    pe.wait_ge(s_late, hi)
                    for j in range(lo, hi):
                        ins = T.transpose(b_xT(t, g)[:, (j - lo) * P:(j - lo + 1) * P], fb[t.name]["shared"][j], c["ident"])
                    ins.then_inc(s_ft, 1)

                if t is OTHERS:
                    transposes(0)
                for g, (lo, hi) in enumerate(t.groups):
                    n, w = GA[t.name] + g, (hi - lo) * P
                    if t is OTHERS:
                        pe.wait_ge(s_fx, n + 1)
                    for k in (0, 1):
                        if n:
                            pe.wait_ge(s_fh, 2 * n + k - 1)
                        T.matmul(b_gate[k][:, 0:w], wT[:, k], xT_shared(t, g), start=True, stop=True)
                        T.matmul(b_up[k][:, 0:w], wT[:, 2 + k], xT_shared(t, g), start=True, stop=True).then_inc(s_fgu, 1)
                    if t is OTHERS and g + 1 < len(t.groups):
                        transposes(g + 1)
                    pe.wait_ge(s_fh, 2 * n + 2)
                    if n:
                        pe.wait_ge(s_fa, n)
                    for j in range(lo, hi):
                        at = (j - lo) * P
                        for k in (0, 1):
                            ins = T.matmul(b_tok[:, at:at + D], f_h[t.name][:, k, at:at + P], wT[:, 4 + k], start=(k == 0),
                                           stop=(k == 1))
                    ins.then_inc(s_fy, 1)

            for h in (0, 1):
                pe.sem_inc(s_ba[h], 1)
            pe.wait_ge(s_zero, 1)

            def sums(h, step):
                pe.wait_ge(s_prod[h], step)
                pe.wait_ge(s_uc[h], step)
                T.matmul(bank[2 * h + 1], c["block"], work[:, h, 1], start=True, stop=True).then_inc(s_usum[h], 1)
                T.matmul(bank[2 * h], c["block"], work[:, h, 0], start=True, stop=True).then_inc(s_red[h], 1)

            for r, (_, n) in enumerate(REGION):
                base = r * L1
                if r:
                    pe.wait_ge(s_bc, 1)
                    pe.wait_ge(s_flc, 1)
                    rank(OTHERS)
                    pe.wait_ge(s_idx, 1)
                pe.wait_ge(s_gc, NG)
                for h in (0, 1):
                    T.matmul(bank[4 + h], zeros[:, 0:P], zeros[:], start=True, stop=False)

                def add_sum(h, n):
                    pe.wait_ge(s_bp[h], n)
                    T.matmul(bank[4 + h], c["ident"], vterm[:, h], start=False, stop=False).then_inc(s_ba[h], 1)

                for h in (1, 0):
                    sums(h, base + 1)
                with pe.Fori(1, n) as i:
                    for h in (1, 0):
                        sums(h, i + (base + 1))
                    for h in (1, 0):
                        add_sum(h, i + (base + 1))
                for h in (1, 0):
                    add_sum(h, base + n + 1)
                for h in (0, 1):
                    T.matmul(bank[4 + h], zeros[:, 0:P], zeros[:], start=False, stop=True).then_inc(s_bs, 1)
            now, then = ([pe.alloc_register(f"{name}{u}") for u in range(U)] for name in ("now", "then"))

            for r in then:
                pe.reg_mov(r, 0)

            def next_experts(run, i, k):
                for u in range(U):
                    pe.reg_mov(now[u], then[u])
                pe.load(then, fb[run.t.name]["te"][0:1, bass.ds(i * 4 + (k + run.first) * 4, U)])

            def x_transposes(run, i, k, b, loaded):
                pe.wait_ge(s_ei[b], loaded)
                for u in range(U):
                    ins = T.transpose(b_x[:, u * P:(u + 1) * P], e_in[:, b, u], c["ident"])
                ins.then_inc(s_et, 1)

            def gate_up(run, i, k, b, u):
                ex = pe.snap(then[u], min_val=0, max_val=E - 1)
                pe.wait_ge(s_ex, i + (k + run.g0 + 1))
                T.matmul(b_gu(run, b)[u], e_xT[:, b, u], gu[:, bass.ds(ex * (2 * F), 2 * F)],
                         start=True, stop=True).then_inc(s_eg, 1)

            def h_transposes(run, i, k):
                for u in range(U):
                    pe.wait_ge(s_eh, i * U + ((k + run.g0) * U + u + 1))
                    for f in (0, 1):
                        ins = T.transpose(b_h[:, (2 * u + f) * P:(2 * u + f + 1) * P],
                                          e_h[:, u, f * P:(f + 1) * P], c["ident"])
                ins.then_inc(s_eht, 1)

            def down(run, i, k, of):
                ex = [pe.snap(r, min_val=0, max_val=E - 1) for r in of]
                pe.wait_ge(s_eo, i + (k + run.g0 + 1))
                pe.wait_ge(s_ehc, i + (k + run.g0 + 1))
                for u in range(U):
                    for f in (0, 1):
                        ins = T.matmul(b_y(run)[:, u * D:(u + 1) * D], e_hT[:, u, f * P:(f + 1) * P],
                                       dw[:, bass.ds(ex[u] * F + f * D, D)], start=(f == 0), stop=(f == 1))
                ins.then_inc(s_ey, 1)

            def pairs(run):
                def loaded(i, k):
                    return i * 8 + 16 * (k // 2 + 1 + run.base[k % 2])

                def pair(i, k, ahead):
                    if ahead:
                        next_experts(run, i, k + 1)
                        gate_up(run, i, k + 1, (k + 1) % 2, 0)
                    h_transposes(run, i, k)
                    if ahead:
                        gate_up(run, i, k + 1, (k + 1) % 2, 1)
                    if ahead > 1:
                        x_transposes(run, i, k + 2, k % 2, loaded(i, k + 2))
                    down(run, i, k, now if ahead else then)

                pe.wait_ge(s_te, 1 + (run.t is MIXED))
                next_experts(run, 0, 0)
                pe.wait_ge(s_eo, run.g0 + 1)
                x_transposes(run, 0, 0, 0, loaded(0, 0))
                pe.wait_ge(s_ex, run.g0 + 1)
                x_transposes(run, 0, 1, 1, loaded(0, 1))
                for u in range(U):
                    gate_up(run, 0, 0, 0, u)
                over_pairs(pe, run, pair)

            pe.wait_ge(s_bc, 2)
            shared(OTHERS)
            pe.wait_ge(s_fa, NOG)
            pe.wait_ge(s_we, 48)
            pairs(RUNS[0])
            run = RUNS[1]

            def forward(i, h):
                pe.wait_ge(s_prod[h], i + (NT + 1))
                T.matmul(bank[2 * h + 1], c["block"], work[:, h, 1], start=True, stop=True)
                T.matmul(bank[2 * h], c["block"], work[:, h, 0], start=True, stop=False)
                pe.wait_ge(s_vd[h], i + 1)
                T.matmul(bank[2 * h], c["block"], vterm[:, h], start=False, stop=True).then_inc(s_red[h], 1)

            def step(i, begins, ends):
                forward(i, 0)
                if begins:
                    pe.wait_ge(s_eo, i + (run.g0 - 1))
                    x_transposes(run, i, -1, 0, i * 16 + 16 * run.base[0])
                    next_experts(run, i, -1)
                forward(i, 1)
                if ends:
                    h_transposes(run, i, -2)
                if begins:
                    for u in range(U):
                        gate_up(run, i, -1, 0, u)
                if ends:
                    down(run, i, -2, now if begins else then)

            pe.wait_ge(s_eo, run.g0 + 1)
            step(0, False, False)
            step(1, True, False)
            with pe.Fori(2, run.n + 1) as i:
                step(i, True, True)
            step(run.n + 1, False, True)

            def output(g, channels):
                lo, hi = QGROUPS[g]
                for h in (0, 1):
                    pe.wait_ge(s_q[h], hi + 1)
                for v in channels:
                    ins = T.matmul(psum(4 + g, lo, hi), c["sel"][:, v * P:(v + 1) * P], qs[:, lo:hi, v // 4, :, v % 4],
                                   start=(v == 0), stop=(v == HD - 1))
                if channels[-1] == HD - 1:
                    ins.then_inc(s_o, 1)

            for i in range(run.n + 2, L2):
                for h in (0, 1):
                    forward(i, h)
                    if i >= L2 - 2:
                        v = (2 * (i - L2 + 2) + h) * 2
                        output(0, (v, v + 1))
            pe.wait_ge(s_eo, run.g0 + run.n + 1)
            pe.wait_ge(s_bc, 2)
            for g in range(0 if run.n + 2 > L2 - 2 else 1, NQ):
                output(g, tuple(range(HD)))
            for g, (lo, hi) in enumerate(QGROUPS):
                pe.wait_ge(s_og, g + 1)
                T.matmul(bank[g][:, 0:(hi - lo) * P], c["mean"], og[:, lo * P:hi * P], start=True,
                         stop=True).then_inc(s_mu, 1)
            for s in range(L2):
                pe.wait_ge(s_osq, s // 4 + 1)
                ins = T.matmul(bank[3][:, s:s + 1], osq[:, s * P:(s + 1) * P], c["mean"][:, 0:1], start=True, stop=True)
            ins.then_inc(s_var, 1)
            for g, (lo, hi) in enumerate(QGROUPS):
                pe.wait_ge(s_dw, g + 1)
                for s in range(lo, hi):
                    ins = T.matmul(bank[4 + g][:, (s - lo) * D:(s - lo + 1) * D], od[:, s * P:(s + 1) * P], wout[:],
                                   start=True, stop=True)
                ins.then_inc(s_at, 1)
            for g in range(len(MIXED.groups)):
                route_transposes(MIXED, g)
            for g in range(len(MIXED.groups)):
                logits(MIXED, g)
            rank(MIXED)
            shared(MIXED)
            pe.wait_ge(s_fa, GA[MIXED.name] + len(MIXED.groups))
            pe.wait_ge(s_idx, 2)
            pairs(RUNS[2])


_NAMES = {
    "L0_attn_x": "x", "L0_attn_Wq": "Wq", "L0_attn_Wk": "Wk", "L0_attn_Wv": "Wv", "L0_attn_Wf1": "Wf1",
    "L0_attn_Wf2": "Wf2", "L0_attn_Wg": "Wg", "L0_attn_Wo1": "Wo1", "L0_attn_Wo2": "Wo2",
    "L0_attn_ln_w": "ln_w", "L0_attn_Wout": "Wout", "L0_ffn_w_router": "w_router",
    "L0_ffn_gate_up_proj": "gate_up_proj", "L0_ffn_down_proj": "down_proj", "L0_ffn_w_gate": "w_gate",
    "L0_ffn_w_up": "w_up", "L0_ffn_w_down": "w_down",
}


def kernel(**inputs):
    import concourse.bacc as bacc
    from concourse.bass_utils import run_bass_kernel_spmd

    nc = bacc.Bacc("TRN2", target_bir_lowering=False, num_devices=1)
    arrays, aps = {}, {}
    for name, short in _NAMES.items():
        arrays[short] = np.ascontiguousarray(inputs[name])
    arrays["const"] = CONST
    for short, v in arrays.items():
        aps[short] = nc.dram_tensor(short, v.shape, F32, kind="ExternalInput").ap()
    out = nc.dram_tensor("out", (B, N, D), F32, kind="ExternalOutput").ap()
    xs = {t.name: nc.dram_tensor("xs_" + t.name, ((t.tiles + 1) * P, D), F32).ap() for t in (OTHERS, MIXED)}
    ys = {t.name: nc.dram_tensor("ys_" + t.name, ((t.tiles + 1) * P, D), F32).ap() for t in (OTHERS, MIXED)}
    scr = {"m": [nc.dram_tensor(f"chain_m{r}", (B * P, COLS // B), F32).ap() for r in (0, 1)],
           "b": [nc.dram_tensor(f"chain_b{r}", (B * P, COLS // B), F32).ap() for r in (0, 1)],
           "s": nc.dram_tensor("chain_s", (P * HD, C * 4), F32).ap()}
    build(nc, aps, out, xs, ys, scr)
    r = run_bass_kernel_spmd(nc, [arrays], core_ids=[0])
    return r.results[0]["out"]
```
